# Optimizing a Trainium2 kernel written in Bass

```python
import numpy as np
import jax
import jax.numpy as jnp

def _softmax(x, axis=-1):
    return jax.nn.softmax(x, axis=axis)

def _gelu(x):
    return jax.nn.gelu(x, approximate=True)

def _silu(x):
    return jax.nn.silu(x)

def _sigmoid(x):
    return jax.nn.sigmoid(x)

def _layernorm(x, axis=-1, eps=1e-05):
    m = jnp.mean(x, axis=axis, keepdims=True)
    v = jnp.var(x, axis=axis, keepdims=True)
    return (x - m) / jnp.sqrt(v + eps)

def _scatter_add(tgt, idx, src, axis=0):
    return tgt.at[idx].add(src)

def _segment_sum(src, seg, n):
    return jax.ops.segment_sum(src, seg, n)
kernel_name = 'mk_recurrent_d4_jaxref_r8_bc6c00'

def setup_inputs(seed: int=0):
    np.random.seed(seed)
    _w = jnp.asarray

    def _L0_attn_setup():
        import math
        import jax, jax.numpy as jnp
        import numpy as np
        HEADS = 8
        SCALE_BASE = 512.0
        GN_EPS = 1e-05

        def _gammas(heads):
            return 1.0 - np.exp(np.linspace(math.log(1.0 / 32.0), math.log(1.0 / 512.0), heads))

        def _xpos(x, downscale):
            N, S, d = x.shape
            half = d // 2
            scale = (jnp.arange(0, d, 2, dtype=jnp.float32) + 0.4 * d) / (1.4 * d)
            pos = jnp.arange(S, dtype=jnp.float32)
            sc = scale[None, :] ** (pos / SCALE_BASE)[:, None]
            inv_freq = 1.0 / 10000.0 ** (jnp.arange(half, dtype=jnp.float32) / half)
            sinusoid = pos[:, None] * inv_freq[None, :]
            sin, cos = (jnp.sin(sinusoid), jnp.cos(sinusoid))
            if downscale:
                sc = 1.0 / sc
            sin_s = jnp.repeat(sin * sc, 2, axis=-1)
            cos_s = jnp.repeat(cos * sc, 2, axis=-1)
            x1, x2 = (x[..., ::2], x[..., 1::2])
            rot = jnp.stack((-x2, x1), axis=-1).reshape(x.shape)
            return x * cos_s + rot * sin_s
        key = jax.random.key(seed)
        ks = jax.random.split(key, 6)
        B, S, H = (2, 256, 128)
        h = HEADS
        d = H // h
        X = jax.random.normal(ks[0], (B, S, H), dtype=jnp.float32)
        W_Q = jax.random.normal(ks[1], (h, d, d), dtype=jnp.float32) / d
        W_K = jax.random.normal(ks[2], (h, d, d), dtype=jnp.float32) / d
        W_V = jax.random.normal(ks[3], (h, d, d), dtype=jnp.float32) / d
        W_G = jax.random.normal(ks[4], (H, H), dtype=jnp.float32) / H
        W_O = jax.random.normal(ks[5], (H, H), dtype=jnp.float32) / H
        gn_weight = jnp.ones((H,), dtype=jnp.float32)
        gn_bias = jnp.zeros((H,), dtype=jnp.float32)
        return {'X': X, 'W_Q': W_Q, 'W_K': W_K, 'W_V': W_V, 'W_G': W_G, 'W_O': W_O, 'gn_weight': gn_weight, 'gn_bias': gn_bias}
    _L0_attn_in = _L0_attn_setup()

    def _L0_ffn_setup():
        import jax, jax.numpy as jnp
        import numpy as np
        N_EXPERTS = 8
        CAP_FACTOR = 1.25
        BATCH, SEQ, DMODEL, DFF = (4, 256, 128, 512)
        key = jax.random.key(seed)
        k0, k1, k2, k3 = jax.random.split(key, 4)
        x = jax.random.normal(k0, (BATCH, SEQ, DMODEL), dtype=jnp.float32)
        Wr = jax.random.normal(k1, (DMODEL, N_EXPERTS), dtype=jnp.float32) * 0.02
        W1 = jax.random.normal(k2, (N_EXPERTS, DMODEL, DFF), dtype=jnp.float32) * 0.02
        W2 = jax.random.normal(k3, (N_EXPERTS, DFF, DMODEL), dtype=jnp.float32) * 0.02
        return {'x': x, 'Wr': Wr, 'W1': W1, 'W2': W2}
    _L0_ffn_in = _L0_ffn_setup()

    def _L1_attn_setup():
        import jax, jax.numpy as jnp
        import numpy as np
        EMBED_DIM = 128
        NUM_HEADS = 16
        HEAD_DIM = EMBED_DIM // NUM_HEADS
        BATCH = 2
        SEQ = 256
        NEG_INF = float('-inf')
        key = jax.random.key(seed)
        k1, k2, k3, k4, k5 = jax.random.split(key, 5)
        return {'query': jax.random.normal(k1, (BATCH, SEQ, EMBED_DIM), dtype=jnp.float32), 'key': jax.random.normal(k2, (BATCH, SEQ, EMBED_DIM), dtype=jnp.float32), 'value': jax.random.normal(k3, (BATCH, SEQ, EMBED_DIM), dtype=jnp.float32), 'in_proj_weight': jax.random.normal(k4, (3 * EMBED_DIM, EMBED_DIM), dtype=jnp.float32) * (1.0 / np.sqrt(EMBED_DIM)), 'out_proj_weight': jax.random.normal(k5, (EMBED_DIM, EMBED_DIM), dtype=jnp.float32) * (1.0 / np.sqrt(EMBED_DIM))}
    _L1_attn_in = _L1_attn_setup()

    def _L1_ffn_setup():
        import jax, jax.numpy as jnp
        import numpy as np
        B, S, D, E, F = (8, 256, 128, 8, 512)
        key = jax.random.key(seed)
        ks = jax.random.split(key, 5)
        scale_in = 1.0 / np.sqrt(D)
        scale_hid = 1.0 / np.sqrt(F)
        return {'x': jax.random.normal(ks[0], (B, S, D), dtype=jnp.float32), 'gate_w': jax.random.normal(ks[1], (D, E), dtype=jnp.float32) * scale_in, 'gate_b': jnp.zeros((E,), dtype=jnp.float32), 'W1': jax.random.normal(ks[2], (E, D, F), dtype=jnp.float32) * scale_in, 'b1': jnp.zeros((E, F), dtype=jnp.float32), 'W2': jax.random.normal(ks[3], (E, F, D), dtype=jnp.float32) * scale_hid, 'b2': jnp.zeros((E, D), dtype=jnp.float32)}
    _L1_ffn_in = _L1_ffn_setup()

    def _L2_attn_setup():
        import jax, jax.numpy as jnp
        import numpy as np
        LN_EPS = 1e-05

        def g(x):
            return jnp.where(x >= 0, x + 0.5, jax.nn.sigmoid(x))

        def log_g(x):
            return jnp.where(x >= 0, jnp.log(jax.nn.relu(x) + 0.5), -jax.nn.softplus(-x))

        def layernorm(x, gamma, beta):
            mu = jnp.mean(x, axis=-1, keepdims=True)
            var = jnp.var(x, axis=-1, keepdims=True)
            return (x - mu) * jax.lax.rsqrt(var + LN_EPS) * gamma + beta

        def mingru_scan(gate, hidden, h0):
            log_z = -jax.nn.softplus(-gate)
            log_coeffs = -jax.nn.softplus(gate)
            log_h0 = jnp.log(h0)
            log_tilde_h = log_g(hidden)
            a_star = jnp.cumsum(jnp.concatenate([jnp.zeros_like(log_h0), log_coeffs], axis=1), axis=1)
            log_vals = jnp.concatenate([log_h0, log_z + log_tilde_h], axis=1) - a_star
            log_h = a_star + jax.lax.cumlogsumexp(log_vals, axis=1)
            return jnp.exp(log_h)[:, 1:]

        def _reference_tuple_inner(x, ln_gamma, ln_beta, W, b):
            B, S, D = x.shape
            L = W.shape[0]
            inp = x
            next_hidden = []
            for l in range(L):
                h_prev = jnp.full((B, 1, D), 0.5, dtype=x.dtype)
                xn = layernorm(inp, ln_gamma[l], ln_beta[l])
                gh = jnp.einsum('bsd,de->bse', xn, W[l]) + b[l]
                gate, hidden = jnp.split(gh, 2, axis=2)
                out = mingru_scan(gate, hidden, h_prev)
                next_hidden.append(out[:, -1:])
                out = out + inp
                inp = out
            return (out, *next_hidden)
        key = jax.random.key(seed)
        k1, k2 = jax.random.split(key)
        B, S, D, L = (8, 512, 128, 3)
        x = jax.random.normal(k1, (B, S, D), dtype=jnp.float32)
        W = jax.random.normal(k2, (L, D, 2 * D), dtype=jnp.float32) * 0.02
        b = jnp.zeros((L, 2 * D), dtype=jnp.float32)
        ln_gamma = jnp.ones((L, D), dtype=jnp.float32)
        ln_beta = jnp.zeros((L, D), dtype=jnp.float32)
        return {'x': x, 'ln_gamma': ln_gamma, 'ln_beta': ln_beta, 'W': W, 'b': b}
    _L2_attn_in = _L2_attn_setup()

    def _L2_ffn_setup():
        import jax, jax.numpy as jnp
        import numpy as np
        B, S, D = (4, 256, 128)
        E = 16
        K = 2
        F = 64
        FS = 256
        key = jax.random.key(seed)
        ks = jax.random.split(key, 9)
        s = 0.02
        return {'hidden_states': jax.random.normal(ks[0], (B, S, D), jnp.float32), 'router_w': jax.random.normal(ks[1], (E, D), jnp.float32) * s, 'Wg': jax.random.normal(ks[2], (E, D, F), jnp.float32) * s, 'Wu': jax.random.normal(ks[3], (E, D, F), jnp.float32) * s, 'Wd': jax.random.normal(ks[4], (E, F, D), jnp.float32) * s, 'Sg': jax.random.normal(ks[5], (D, FS), jnp.float32) * s, 'Su': jax.random.normal(ks[6], (D, FS), jnp.float32) * s, 'Sd': jax.random.normal(ks[7], (FS, D), jnp.float32) * s, 'shared_gate_w': jax.random.normal(ks[8], (D, 1), jnp.float32) * s}
    _L2_ffn_in = _L2_ffn_setup()

    def _L3_attn_setup():
        import jax, jax.numpy as jnp
        import numpy as np
        import math
        B, N, D, H = (1, 512, 128, 16)
        HS = D // H
        NEG_INF = -10000.0
        key = jax.random.key(seed)
        k1, k2, k3, k4, k5 = jax.random.split(key, 5)
        return {'encodings': jax.random.normal(k1, (B, N, D), dtype=jnp.float32), 'attn_W': jax.random.normal(k2, (D, 3 * D), dtype=jnp.float32) * 0.02, 'attn_b': jax.random.normal(k3, (3 * D,), dtype=jnp.float32) * 0.02, 'out_W': jax.random.normal(k4, (D, D), dtype=jnp.float32) * 0.02, 'out_b': jax.random.normal(k5, (D,), dtype=jnp.float32) * 0.02}
    _L3_attn_in = _L3_attn_setup()

    def _L3_ffn_setup():
        import jax, jax.numpy as jnp
        import numpy as np
        NUM_EXPERTS = 8
        TOP_K = 2
        MODEL_DIM = 128
        INTER_DIM = 512

        def _grouped_matmul(x, w, seg_ids):
            out = jnp.zeros((x.shape[0], w.shape[2]), dtype=x.dtype)
            for e in range(w.shape[0]):
                xe = jnp.where((seg_ids == e)[:, None], x, 0)
                out = out + xe @ w[e]
            return out
        key = jax.random.key(seed)
        k1, k2, k3, k4 = jax.random.split(key, 4)
        hidden_states = jax.random.normal(k1, (4, 64, MODEL_DIM), jnp.float32)
        gate_w = jax.random.normal(k2, (NUM_EXPERTS, MODEL_DIM), jnp.float32) * 0.02
        w_up = jax.random.normal(k3, (NUM_EXPERTS, MODEL_DIM, INTER_DIM), jnp.float32) * 0.02
        w_down = jax.random.normal(k4, (NUM_EXPERTS, INTER_DIM, MODEL_DIM), jnp.float32) * 0.02
        return {'hidden_states': hidden_states, 'gate_w': gate_w, 'w_up': w_up, 'w_down': w_down}
    _L3_ffn_in = _L3_ffn_setup()
    _d = {'L0_attn_X': _L0_attn_in['X'], 'L0_attn_W_Q': _L0_attn_in['W_Q'], 'L0_attn_W_K': _L0_attn_in['W_K'], 'L0_attn_W_V': _L0_attn_in['W_V'], 'L0_attn_W_G': _L0_attn_in['W_G'], 'L0_attn_W_O': _L0_attn_in['W_O'], 'L0_attn_gn_weight': _L0_attn_in['gn_weight'], 'L0_attn_gn_bias': _L0_attn_in['gn_bias'], 'L0_ffn_Wr': _L0_ffn_in['Wr'], 'L0_ffn_W1': _L0_ffn_in['W1'], 'L0_ffn_W2': _L0_ffn_in['W2'], 'L1_attn_key': _L1_attn_in['key'], 'L1_attn_value': _L1_attn_in['value'], 'L1_attn_in_proj_weight': _L1_attn_in['in_proj_weight'], 'L1_attn_out_proj_weight': _L1_attn_in['out_proj_weight'], 'L1_ffn_gate_w': _L1_ffn_in['gate_w'], 'L1_ffn_gate_b': _L1_ffn_in['gate_b'], 'L1_ffn_W1': _L1_ffn_in['W1'], 'L1_ffn_b1': _L1_ffn_in['b1'], 'L1_ffn_W2': _L1_ffn_in['W2'], 'L1_ffn_b2': _L1_ffn_in['b2'], 'L2_attn_ln_gamma': _L2_attn_in['ln_gamma'], 'L2_attn_ln_beta': _L2_attn_in['ln_beta'], 'L2_attn_W': _L2_attn_in['W'], 'L2_attn_b': _L2_attn_in['b'], 'L2_ffn_router_w': _L2_ffn_in['router_w'], 'L2_ffn_Wg': _L2_ffn_in['Wg'], 'L2_ffn_Wu': _L2_ffn_in['Wu'], 'L2_ffn_Wd': _L2_ffn_in['Wd'], 'L2_ffn_Sg': _L2_ffn_in['Sg'], 'L2_ffn_Su': _L2_ffn_in['Su'], 'L2_ffn_Sd': _L2_ffn_in['Sd'], 'L2_ffn_shared_gate_w': _L2_ffn_in['shared_gate_w'], 'L3_attn_attn_W': _L3_attn_in['attn_W'], 'L3_attn_attn_b': _L3_attn_in['attn_b'], 'L3_attn_out_W': _L3_attn_in['out_W'], 'L3_attn_out_b': _L3_attn_in['out_b'], 'L3_ffn_gate_w': _L3_ffn_in['gate_w'], 'L3_ffn_w_up': _L3_ffn_in['w_up'], 'L3_ffn_w_down': _L3_ffn_in['w_down']}
    _x0 = _d['L0_attn_X']
    _d['L0_attn_X'] = jax.random.normal(jax.random.fold_in(jax.random.key(seed), 1), (4, 512, 128), dtype=_x0.dtype)
    del _x0
    return _d

def reference(L0_attn_X, L0_attn_W_Q, L0_attn_W_K, L0_attn_W_V, L0_attn_W_G, L0_attn_W_O, L0_attn_gn_weight, L0_attn_gn_bias, L0_ffn_Wr, L0_ffn_W1, L0_ffn_W2, L1_attn_key, L1_attn_value, L1_attn_in_proj_weight, L1_attn_out_proj_weight, L1_ffn_gate_w, L1_ffn_gate_b, L1_ffn_W1, L1_ffn_b1, L1_ffn_W2, L1_ffn_b2, L2_attn_ln_gamma, L2_attn_ln_beta, L2_attn_W, L2_attn_b, L2_ffn_router_w, L2_ffn_Wg, L2_ffn_Wu, L2_ffn_Wd, L2_ffn_Sg, L2_ffn_Su, L2_ffn_Sd, L2_ffn_shared_gate_w, L3_attn_attn_W, L3_attn_attn_b, L3_attn_out_W, L3_attn_out_b, L3_ffn_gate_w, L3_ffn_w_up, L3_ffn_w_down):

    def _L0_attn_ref(X, W_Q, W_K, W_V, W_G, W_O, gn_weight, gn_bias):
        import math
        import jax, jax.numpy as jnp
        import numpy as np
        HEADS = 8
        SCALE_BASE = 512.0
        GN_EPS = 1e-05

        def _gammas(heads):
            return 1.0 - np.exp(np.linspace(math.log(1.0 / 32.0), math.log(1.0 / 512.0), heads))

        def _xpos(x, downscale):
            N, S, d = x.shape
            half = d // 2
            scale = (jnp.arange(0, d, 2, dtype=jnp.float32) + 0.4 * d) / (1.4 * d)
            pos = jnp.arange(S, dtype=jnp.float32)
            sc = scale[None, :] ** (pos / SCALE_BASE)[:, None]
            inv_freq = 1.0 / 10000.0 ** (jnp.arange(half, dtype=jnp.float32) / half)
            sinusoid = pos[:, None] * inv_freq[None, :]
            sin, cos = (jnp.sin(sinusoid), jnp.cos(sinusoid))
            if downscale:
                sc = 1.0 / sc
            sin_s = jnp.repeat(sin * sc, 2, axis=-1)
            cos_s = jnp.repeat(cos * sc, 2, axis=-1)
            x1, x2 = (x[..., ::2], x[..., 1::2])
            rot = jnp.stack((-x2, x1), axis=-1).reshape(x.shape)
            return x * cos_s + rot * sin_s
        B, S, H = X.shape
        h = HEADS
        d = H // h
        gammas = jnp.asarray(_gammas(h), dtype=X.dtype)
        Xh = X.reshape(B, S, h, d)
        Q = jnp.einsum('bshd,hde->bhse', Xh, W_Q)
        K = jnp.einsum('bshd,hde->bhse', Xh, W_K)
        V = jnp.einsum('bshd,hde->bhse', Xh, W_V)
        Q = _xpos(Q.reshape(B * h, S, d), downscale=False).reshape(B, h, S, d)
        K = _xpos(K.reshape(B * h, S, d), downscale=True).reshape(B, h, S, d)
        n = jnp.arange(S)
        diff = n[:, None] - n[None, :]
        causal = diff >= 0
        D = gammas[:, None, None] ** jnp.where(causal, diff, 0).astype(X.dtype) * causal[None].astype(X.dtype)
        att = jnp.einsum('bhsd,bhtd->bhst', Q, K) * D[None]
        Y = jnp.einsum('bhst,bhtd->bshd', att, V).reshape(B, S, H)
        Yg = Y.reshape(B * S, h, d)
        mu = Yg.mean(axis=-1, keepdims=True)
        var = Yg.var(axis=-1, keepdims=True)
        Yn = ((Yg - mu) / jnp.sqrt(var + GN_EPS)).reshape(B * S, H)
        Yn = (Yn * gn_weight + gn_bias).reshape(B, S, H)
        G = X @ W_G
        return G * jax.nn.sigmoid(G) * Yn @ W_O

    def _L0_ffn_ref(x, Wr, W1, W2):
        import jax, jax.numpy as jnp
        import numpy as np
        N_EXPERTS = 8
        CAP_FACTOR = 1.25
        BATCH, SEQ, DMODEL, DFF = (4, 256, 128, 512)
        B, S, D = x.shape
        E = W1.shape[0]
        cap = int(CAP_FACTOR * B * S / E)
        t = x.reshape(-1, D)
        probs = jax.nn.softmax(t @ Wr, axis=-1)
        idx = jnp.argmax(probs, axis=-1)
        pmax = jnp.max(probs, axis=-1)
        onehot = jax.nn.one_hot(idx, E, dtype=jnp.int32)
        pos = jnp.sum(jnp.cumsum(onehot, axis=0) * onehot, axis=-1) - 1
        kept = pos < cap
        flat = idx * cap + jnp.minimum(pos, cap - 1)
        disp = jnp.zeros((E * cap, D), t.dtype).at[flat].add(t * kept[:, None].astype(t.dtype))
        ein = disp.reshape(E, cap, D)
        h = jax.nn.relu(jnp.einsum('ecd,edf->ecf', ein, W1))
        eout = jnp.einsum('ecf,efd->ecd', h, W2).reshape(E * cap, D)
        comb = jnp.where(kept[:, None], eout[flat], t)
        factor = jnp.where(kept, pmax, jnp.ones_like(pmax))
        out = (comb * factor[:, None]).reshape(B, S, D)
        return out

    def _L1_attn_ref(query, key, value, in_proj_weight, out_proj_weight):
        import jax, jax.numpy as jnp
        import numpy as np
        EMBED_DIM = 128
        NUM_HEADS = 16
        HEAD_DIM = EMBED_DIM // NUM_HEADS
        BATCH = 2
        SEQ = 256
        NEG_INF = float('-inf')
        B, T, E = query.shape
        H, D = (NUM_HEADS, HEAD_DIM)
        projected = jnp.einsum('bte,fe->btf', query, in_proj_weight)
        packed = projected.reshape(B, T, 3, H, D).transpose(0, 3, 2, 1, 4)
        q, k, v = (packed[:, :, 0], packed[:, :, 1], packed[:, :, 2])
        q = q / jnp.sqrt(jnp.asarray(D, dtype=q.dtype))
        attention = jnp.einsum('bhtd,bhkd->bhtk', q, k)
        qpos = jnp.arange(T)[:, None]
        kpos = jnp.arange(T)[None, :]
        mask = jnp.where(qpos - kpos >= 0, 0.0, NEG_INF).astype(attention.dtype)
        attention = attention + mask[None, None]
        activation = jax.nn.softmax(attention, axis=-1)
        x = jnp.einsum('bhtk,bhkd->bhtd', activation, v)
        x = x.transpose(0, 2, 1, 3).reshape(B, T, E)
        out = jnp.einsum('bte,fe->btf', x, out_proj_weight)
        return out

    def _L1_ffn_ref(x, gate_w, gate_b, W1, b1, W2, b2):
        import jax, jax.numpy as jnp
        import numpy as np
        B, S, D, E, F = (8, 256, 128, 8, 512)
        num_experts = W1.shape[0]
        logits = jnp.einsum('bsd,de->bse', x, gate_w) + gate_b
        gates = jax.nn.softmax(logits, axis=-1)
        top_g, top_i = jax.lax.top_k(gates, 2)
        top_g = top_g / jnp.sum(top_g, axis=-1, keepdims=True)
        onehot = jax.nn.one_hot(top_i, num_experts, dtype=x.dtype)
        comb = jnp.sum(top_g[..., None] * onehot, axis=-2)
        out = jnp.zeros_like(x)
        for e in range(num_experts):
            h = jax.nn.relu(jnp.einsum('bsd,df->bsf', x, W1[e]) + b1[e])
            out = out + comb[..., e:e + 1] * (jnp.einsum('bsf,fd->bsd', h, W2[e]) + b2[e])
        return out

    def _L2_attn_ref(x, ln_gamma, ln_beta, W, b):
        import jax, jax.numpy as jnp
        import numpy as np
        LN_EPS = 1e-05

        def g(x):
            return jnp.where(x >= 0, x + 0.5, jax.nn.sigmoid(x))

        def log_g(x):
            return jnp.where(x >= 0, jnp.log(jax.nn.relu(x) + 0.5), -jax.nn.softplus(-x))

        def layernorm(x, gamma, beta):
            mu = jnp.mean(x, axis=-1, keepdims=True)
            var = jnp.var(x, axis=-1, keepdims=True)
            return (x - mu) * jax.lax.rsqrt(var + LN_EPS) * gamma + beta

        def mingru_scan(gate, hidden, h0):
            log_z = -jax.nn.softplus(-gate)
            log_coeffs = -jax.nn.softplus(gate)
            log_h0 = jnp.log(h0)
            log_tilde_h = log_g(hidden)
            a_star = jnp.cumsum(jnp.concatenate([jnp.zeros_like(log_h0), log_coeffs], axis=1), axis=1)
            log_vals = jnp.concatenate([log_h0, log_z + log_tilde_h], axis=1) - a_star
            log_h = a_star + jax.lax.cumlogsumexp(log_vals, axis=1)
            return jnp.exp(log_h)[:, 1:]

        def _reference_tuple_inner(x, ln_gamma, ln_beta, W, b):
            B, S, D = x.shape
            L = W.shape[0]
            inp = x
            next_hidden = []
            for l in range(L):
                h_prev = jnp.full((B, 1, D), 0.5, dtype=x.dtype)
                xn = layernorm(inp, ln_gamma[l], ln_beta[l])
                gh = jnp.einsum('bsd,de->bse', xn, W[l]) + b[l]
                gate, hidden = jnp.split(gh, 2, axis=2)
                out = mingru_scan(gate, hidden, h_prev)
                next_hidden.append(out[:, -1:])
                out = out + inp
                inp = out
            return (out, *next_hidden)
        return _reference_tuple_inner(x, ln_gamma, ln_beta, W, b)[0]

    def _L2_ffn_ref(hidden_states, router_w, Wg, Wu, Wd, Sg, Su, Sd, shared_gate_w):
        import jax, jax.numpy as jnp
        import numpy as np
        B, S, D = (4, 256, 128)
        E = 16
        K = 2
        F = 64
        FS = 256
        b, s, d = hidden_states.shape
        x = hidden_states.reshape(-1, d)
        T = x.shape[0]
        logits = jnp.einsum('td,ed->te', x.astype(jnp.float32), router_w.astype(jnp.float32))
        probs = jax.nn.softmax(logits, axis=-1)
        top_w, top_i = jax.lax.top_k(probs, K)
        top_w = top_w / jnp.sum(top_w, axis=-1, keepdims=True)
        top_w = top_w.astype(x.dtype)
        dense_w = jnp.zeros((T, E), x.dtype).at[jnp.arange(T)[:, None], top_i].add(top_w)

        def body(acc, params):
            wg, wu, wd, cw = params
            h = jax.nn.silu(x @ wg) * (x @ wu)
            return (acc + cw[:, None] * (h @ wd), None)
        expert_out, _ = jax.lax.scan(body, jnp.zeros_like(x), (Wg, Wu, Wd, dense_w.T))
        shared = jax.nn.silu(x @ Sg) * (x @ Su) @ Sd
        shared = jax.nn.sigmoid(x @ shared_gate_w) * shared
        out = expert_out + shared
        return out.reshape(b, s, d)

    def _L3_attn_ref(encodings, attn_W, attn_b, out_W, out_b):
        import jax, jax.numpy as jnp
        import numpy as np
        import math
        B, N, D, H = (1, 512, 128, 16)
        HS = D // H
        NEG_INF = -10000.0
        b, n, d = encodings.shape
        qkv = encodings @ attn_W + attn_b
        qkv = qkv.reshape(b, n, H, 3 * HS).transpose(0, 2, 1, 3)
        q, k, v = jnp.split(qkv, 3, axis=-1)
        scores = jnp.einsum('bhki,bhqi->bhkq', k, q) / math.sqrt(HS)
        mask = jnp.arange(n)[:, None] <= jnp.arange(n)[None, :]
        scores = jnp.where(mask, scores, jnp.float32(NEG_INF))
        prob = jax.nn.softmax(scores, axis=2)
        combined = jnp.einsum('bhkq,bhkl->bhql', prob, v)
        out = combined.transpose(0, 2, 1, 3).reshape(b, n, d)
        return out @ out_W + out_b

    def _L3_ffn_ref(hidden_states, gate_w, w_up, w_down):
        import jax, jax.numpy as jnp
        import numpy as np
        NUM_EXPERTS = 8
        TOP_K = 2
        MODEL_DIM = 128
        INTER_DIM = 512

        def _grouped_matmul(x, w, seg_ids):
            out = jnp.zeros((x.shape[0], w.shape[2]), dtype=x.dtype)
            for e in range(w.shape[0]):
                xe = jnp.where((seg_ids == e)[:, None], x, 0)
                out = out + xe @ w[e]
            return out
        orig_shape = hidden_states.shape
        x = hidden_states.reshape(-1, orig_shape[-1])
        T = x.shape[0]
        logits = x @ gate_w.T
        probs = jax.nn.softmax(logits.astype(jnp.float32), axis=-1)
        _, topk_idx = jax.lax.top_k(probs, TOP_K)
        idx_flat = topk_idx.T.reshape(-1)
        order = jnp.argsort(idx_flat)
        seg_ids = idx_flat[order]
        token_ids = order % T
        moe_in = x[token_ids]
        h = _grouped_matmul(moe_in, w_up, seg_ids)
        moe_out = _grouped_matmul(h, w_down, seg_ids)
        out = jnp.zeros_like(x).at[token_ids].add(moe_out)
        return out.reshape(orig_shape)
    x = L0_attn_X
    xn = _layernorm(x, axis=-1)
    s = _L0_attn_ref(xn, L0_attn_W_Q, L0_attn_W_K, L0_attn_W_V, L0_attn_W_G, L0_attn_W_O, L0_attn_gn_weight, L0_attn_gn_bias)
    g = _silu(_L0_ffn_ref(xn, L0_ffn_Wr, L0_ffn_W1, L0_ffn_W2))
    x = x + s * g
    xn = _layernorm(x, axis=-1)
    s = _L1_attn_ref(xn, L1_attn_key, L1_attn_value, L1_attn_in_proj_weight, L1_attn_out_proj_weight)
    g = _silu(_L1_ffn_ref(xn, L1_ffn_gate_w, L1_ffn_gate_b, L1_ffn_W1, L1_ffn_b1, L1_ffn_W2, L1_ffn_b2))
    x = x + s * g
    xn = _layernorm(x, axis=-1)
    s = _L2_attn_ref(xn, L2_attn_ln_gamma, L2_attn_ln_beta, L2_attn_W, L2_attn_b)
    g = _silu(_L2_ffn_ref(xn, L2_ffn_router_w, L2_ffn_Wg, L2_ffn_Wu, L2_ffn_Wd, L2_ffn_Sg, L2_ffn_Su, L2_ffn_Sd, L2_ffn_shared_gate_w))
    x = x + s * g
    xn = _layernorm(x, axis=-1)
    s = _L3_attn_ref(xn, L3_attn_attn_W, L3_attn_attn_b, L3_attn_out_W, L3_attn_out_b)
    g = _silu(_L3_ffn_ref(xn, L3_ffn_gate_w, L3_ffn_w_up, L3_ffn_w_down))
    x = x + s * g
    return x

_drawn_inputs = setup_inputs


def setup_inputs(seed=0):
    import zlib

    import numpy as np

    out = dict(_drawn_inputs(seed))
    spreads = {'L0_attn_gn_weight': (1.0, 0.6),
     'L0_attn_gn_bias': (0.0, 0.8),
     'L1_ffn_gate_b': (0.0, 0.752),
     'L1_ffn_b1': (0.0, 0.8),
     'L1_ffn_b2': (0.0, 0.8),
     'L2_attn_ln_gamma': (1.0, 0.6),
     'L2_attn_ln_beta': (0.0, 0.8),
     'L2_attn_b': (0.0, 0.8)}
    factors = {'L0_attn_W_Q': 8.0,
     'L0_attn_W_K': 8.0,
     'L0_attn_W_V': 8.0,
     'L0_attn_W_G': 8.0,
     'L0_attn_W_O': 8.0,
     'L0_ffn_Wr': 8.0,
     'L0_ffn_W1': 8.0,
     'L0_ffn_W2': 8.0,
     'L2_attn_W': 8.0,
     'L2_ffn_router_w': 8.0,
     'L2_ffn_Wg': 8.0,
     'L2_ffn_Wu': 8.0,
     'L2_ffn_Wd': 8.0,
     'L2_ffn_Sg': 8.0,
     'L2_ffn_Su': 8.0,
     'L2_ffn_Sd': 8.0,
     'L2_ffn_shared_gate_w': 8.0,
     'L3_attn_attn_W': 8.0,
     'L3_attn_attn_b': 8.0,
     'L3_attn_out_W': 8.0,
     'L3_attn_out_b': 8.0,
     'L3_ffn_gate_w': 8.0,
     'L3_ffn_w_up': 8.0,
     'L3_ffn_w_down': 8.0}
    for name, (base, spread) in spreads.items():
        noise = np.random.default_rng([zlib.crc32(name.encode()), seed]).standard_normal(out[name].shape)
        drawn = base * np.exp(spread * noise) if base else spread * noise
        out[name] = jnp.asarray(drawn.astype(out[name].dtype))
    for name, factor in factors.items():
        out[name] = (out[name] * factor).astype(out[name].dtype)
    return out
```

```python
from contextlib import ExitStack, contextmanager

import numpy as np

import concourse.bass as bass
from concourse import mybir

P = 128
D = 128
BATCH, SEQ = 4, 512
T = BATCH * SEQ
TILES = T // P
BT = SEQ // P
EPS = 1e-5

F32 = mybir.dt.float32
BF16 = mybir.dt.bfloat16
I32 = mybir.dt.int32
U32 = mybir.dt.uint32
ALU = mybir.AluOpType
ACT = mybir.ActivationFunctionType
X = mybir.AxisListType.X

H0, D0 = 8, 16
H1, D1 = 16, 8
F = 512
CAP = T * 5 // 4 // 8
LATE = 16640
ARENA = LATE + 13 * 1024
PART = CAP // 4

WIDTHS = dict(ident=128, tri=128, neg=128, decay=128, cosq=SEQ, sinq=SEQ, cosk=SEQ, sink=SEQ, heads=8,
              rev8=8, rev16=16, start320=8, dump=16, thr=128)
COLS = {}
_at = 0
for _k, _w in WIDTHS.items():
    COLS[_k] = (_at, _at + _w)
    _at += _w
CONST_W = _at


def constants():
    c = np.zeros((P, CONST_W), np.float32)

    def put(name, value):
        c[:, COLS[name][0]:COLS[name][1]] = value

    p = np.arange(P)
    put("ident", np.eye(P))
    put("tri", p[:, None] <= p[None, :])
    put("neg", np.where(p[None, :] > p[:, None], np.float32(-1e30), np.float32(0)))
    gammas = (1.0 - np.exp(np.linspace(np.log(1 / 32), np.log(1 / 512), H0))).astype(np.float32).astype(np.float64)
    head, j = p // D0, p % D0
    put("decay", (head[:, None] == head[None, :]) * (gammas[head] ** P)[:, None])
    pos = np.arange(SEQ)
    scale = ((np.arange(0, D0, 2) + 0.4 * D0) / (1.4 * D0))[j // 2]
    sc = scale[:, None] ** (pos / 512.0)[None, :]
    half = D0 // 2
    inv = (1.0 / np.float32(10000.0) ** (np.arange(half, dtype=np.float32) / np.float32(half))).astype(np.float32)
    angle = (pos[None, :].astype(np.float32) * inv[j // 2][:, None]).astype(np.float64)
    sign = np.where(j % 2 == 0, -1.0, 1.0)[:, None]
    grow = gammas[head][:, None] ** (pos % P)[None, :]
    put("cosq", np.cos(angle) * sc * grow)
    put("sinq", np.sin(angle) * sc * grow * sign)
    put("cosk", np.cos(angle) / sc / grow)
    put("sink", np.sin(angle) / sc / grow * sign)
    put("heads", head[:, None] == np.arange(H0)[None, :])
    put("rev8", 8 - np.arange(8)[None, :])
    put("rev16", 16 - np.arange(16)[None, :])
    put("start320", 320 * np.arange(8)[None, :])
    put("dump", 2560 + np.arange(16)[None, :] * P + p[:, None])
    put("thr", 128 * np.arange(128)[None, :])
    return c


class Steps:

    def __init__(self, eng, sem):
        self.eng, self.sem, self.count, self.turn = eng, sem, 0, 0

    def __call__(self, instruction):
        instruction.then_inc(self.sem, 1)
        self.count += 1
        self.eng.wait_ge(self.sem, self.count + self.turn)

    def loop(self, times, steps):
        return self.loop_from(0, times, steps)

    @contextmanager
    def loop_from(self, start, times, steps):
        first = self.count
        with self.eng.Fori(start, start + times) as i:
            self.turn = (i - start) * steps if start else i * steps
            yield i
        assert self.count == first + steps, self.count - first
        self.count, self.turn = first + times * steps, 0


def bcast(ap, shape):
    return ap.broadcast_to(list(shape))


def build(nc, a, out, scratch):
    ctx = ExitStack()
    with ctx:
        def sb(name, shape, dt=F32):
            return ctx.enter_context(nc.sbuf_tensor(name, shape, dt))

        def sem(name):
            return ctx.enter_context(nc.semaphore(name))

        banks = ctx.enter_context(nc.psum_tensor("banks", [P, 8, 512], F32))

        const = sb("const", [P, CONST_W])
        C = {k: const[:, lo:hi] for k, (lo, hi) in COLS.items()}
        x = sb("x", [P, TILES, D])
        xn = sb("xn", [P, TILES, D])
        xnT = sb("xnT", [P, T])
        s_out = sb("s_out", [P, TILES, D])
        g_out = sb("g_out", [P, TILES, D])
        squares = sb("squares", [P, TILES, D])
        mean = sb("mean", [P, 64])
        var = sb("var", [P, 64])
        rstd = sb("rstd", [P, 64])
        minus_half = sb("minus_half", [P, 64])
        ones = sb("ones", [P, P])

        const_loaded = sem("const_loaded")
        x_loaded = sem("x_loaded")
        out_stored = sem("out_stored")
        x_final = sem("x_final")
        pool_consts_set = sem("pool_consts_set")
        dve_step = sem("dve_step")
        act_step = sem("act_step")
        pool_step = sem("pool_step")

        norm_centered = sem("norm_centered")
        norm_squared = sem("norm_squared")
        norm_var = sem("norm_var")
        norm_rstd = sem("norm_rstd")
        norm_done = sem("norm_done")
        norm_transposed = sem("norm_transposed")
        xnT_ready = sem("xnT_ready")

        def norm_vector(dve, step, layer):
            step(dve.tensor_reduce(mean[:, 0:TILES], x[:, :, :], X, ALU.add))
            step(dve.tensor_scalar(mean[:, 0:TILES], mean[:, 0:TILES], 1.0 / D, None, ALU.mult))
            dve.tensor_tensor(xn[:, :, :], x[:, :, :], bcast(mean[:, 0:TILES].unsqueeze(2), (P, TILES, D)),
                              ALU.subtract).then_inc(norm_centered, 1)
            dve.wait_ge(norm_squared, layer + 1)
            step(dve.tensor_reduce(var[:, 0:TILES], squares[:, :, :], X, ALU.add))
            dve.tensor_scalar(var[:, 0:TILES], var[:, 0:TILES], 1.0 / D, EPS, ALU.mult, ALU.add).then_inc(norm_var, 1)
            dve.wait_ge(norm_rstd, layer + 1)
            dve.tensor_tensor(xn[:, :, :], xn[:, :, :], bcast(rstd[:, 0:TILES].unsqueeze(2), (P, TILES, D)),
                              ALU.mult).then_inc(norm_done, 1)

        def norm_scalar(act, layer):
            act.wait_ge(norm_centered, layer + 1)
            act.activation(squares[:, :, :], xn[:, :, :], ACT.Square).then_inc(norm_squared, 1)
            for k in range(4):
                act.wait_ge(norm_transposed, 4 * layer + k + 1)
                act.activation(xnT[:, k * 512:(k + 1) * 512], banks[:, k, :], ACT.Copy).then_inc(xnT_ready, 1)

        def norm_gpsimd(pool, step, layer):
            pool.wait_ge(norm_var, layer + 1)
            pool.tensor_tensor(rstd[:, 0:TILES], var[:, 0:TILES], minus_half[:, 0:TILES], ALU.pow).then_inc(norm_rstd, 1)

        def norm_tensor(pe, layer):
            pe.wait_ge(norm_done, layer + 1)
            for t in range(TILES):
                ins = pe.transpose(banks[:, t // 4, (t % 4) * P:(t % 4 + 1) * P], xn[:, t, :], C["ident"])
                if t % 4 == 3:
                    ins.then_inc(norm_transposed, 1)

        arena = sb("arena", [P, ARENA])

        class Region:

            def __init__(self, at, end=ARENA):
                self.at, self.end = at, end

            def __call__(self, name, shape, dt=F32):
                n = int(np.prod(shape[1:]))
                words = n if dt != BF16 else (n + 1) // 2
                ap = arena[0:shape[0], self.at:self.at + words]
                self.at += words
                assert self.at <= self.end, (name, self.at, self.end)
                if dt != F32:
                    ap = ap.bitcast(dt)
                if len(shape) > 2:
                    dims = "abcd"[:len(shape) - 1]
                    ap = ap.rearrange(f"p ({' '.join(dims)}) -> p {' '.join(dims)}", **dict(zip(dims, shape[1:])))
                return ap

        l0 = Region(0, LATE)
        w0 = l0("w0", [P, 4, P])
        w0vg = l0("w0vg", [P, 2, P])
        w0o = l0("w0o", [P, P])
        gn_w = l0("gn_w", [P, D])
        gn_b = l0("gn_b", [P, D])
        xb = l0("xb", [P, SEQ])
        qT = l0("qT", [P, SEQ])
        kT = l0("kT", [P, SEQ])
        rot = l0("rot", [P, SEQ])
        v_tok = l0("v_tok", [P, BT, D])
        gate_sig = l0("gate_sig", [P, BT, D])
        gate = l0("gate", [P, BT, D])
        q_heads = l0("q_heads", [P, 2, H0, P])
        attT = l0("attT", [P, 2, H0, P])
        k_tok = l0("k_tok", [P, BT - 1, P])
        state = l0("state", [P, BT - 1, P])
        yc = l0("yc", [P, BT * H0, D0])
        zT = l0("zT", [P, SEQ])

        l0_weights = sem("l0_weights")
        l0_x_copied = sem("l0_x_copied")
        l0_projected = sem("l0_projected")
        l0_v_copied = sem("l0_v_copied")
        l0_sig = sem("l0_sig")
        l0_q_ready = sem("l0_q_ready")
        l0_k_ready = sem("l0_k_ready")
        l0_q_heads = sem("l0_q_heads")
        l0_k_turned = sem("l0_k_turned")
        l0_k_tok = sem("l0_k_tok")
        l0_scores = sem("l0_scores")
        l0_att = sem("l0_att")
        l0_y = sem("l0_y")
        l0_update = sem("l0_update")
        l0_state = sem("l0_state")
        l0_centered = sem("l0_centered")
        l0_squared = sem("l0_squared")
        l0_var = sem("l0_var")
        l0_rstd = sem("l0_rstd")
        l0_z = sem("l0_z")
        l0_z_turned = sem("l0_z_turned")
        l0_zT = sem("l0_zT")
        l0_s = sem("l0_s")
        l0_s_copied = sem("l0_s_copied")

        def retention_tensor(pe):
            pe.wait_ge(l0_weights, 16 * 5)
            with pe.Fori(0, BATCH) as b:
                pe.wait_ge(l0_x_copied, b + 1)
                for n in range(4):
                    ins = pe.matmul(banks[:, n, :], w0[:, n, :], xb[:, :], start=True, stop=True)
                ins.then_inc(l0_projected, 1)
                for t in range(BT):
                    ins = pe.matmul(banks[:, 4 + t // 2, (t % 2) * 256:(t % 2 + 1) * 256], xb[:, t * P:(t + 1) * P],
                                    w0vg[:, :, :], start=True, stop=True)
                ins.then_inc(l0_projected, 1)

                def scores(c):
                    pe.wait_ge(l0_q_heads, BT * b + c + 1)
                    if c >= 2:
                        pe.wait_ge(l0_att, BT * b + c - 1)
                    for n in range(2):
                        ins = pe.matmul(banks[:, 2 * (c % 2) + n, :], kT[:, c * P:(c + 1) * P],
                                        q_heads[:, c % 2, 4 * n:4 * n + 4, :], start=True, stop=True)
                    ins.then_inc(l0_scores, 1)

                pe.wait_ge(l0_k_ready, b + 1)
                for c in range(BT - 1):
                    ins = pe.transpose(banks[:, 6, c * P:(c + 1) * P], kT[:, c * P:(c + 1) * P], C["ident"])
                ins.then_inc(l0_k_turned, 1)
                scores(0)
                pe.wait_ge(l0_k_tok, b + 1)
                for c in range(BT - 1):
                    ins = pe.matmul(banks[:, 6, c * P:(c + 1) * P], k_tok[:, c, :], v_tok[:, c, :], start=True, stop=True)
                ins.then_inc(l0_update, 1)
                for c in range(BT):
                    if c + 1 < BT:
                        scores(c + 1)
                    y = banks[:, 7, c * P:(c + 1) * P]
                    if c >= 1:
                        pe.wait_ge(l0_state, b + 1)
                        pe.matmul(y, qT[:, c * P:(c + 1) * P], state[:, c - 1, :], start=True, stop=False)
                    pe.wait_ge(l0_att, BT * b + c + 1)
                    for h in range(H0):
                        ins = pe.matmul(y[:, h * D0:(h + 1) * D0], attT[:, c % 2, h, :],
                                        v_tok[:, c, h * D0:(h + 1) * D0], start=(c == 0 and h == 0), stop=(h == H0 - 1))
                    ins.then_inc(l0_y, 1)
                pe.wait_ge(l0_z, b + 1)
                for t in range(BT):
                    ins = pe.transpose(banks[:, 4, t * P:(t + 1) * P],
                                       yc[:, t * H0:(t + 1) * H0, :].rearrange("p h d -> p (h d)"), C["ident"])
                ins.then_inc(l0_z_turned, 1)
                pe.wait_ge(l0_zT, b + 1)
                for t in range(BT):
                    ins = pe.matmul(banks[:, 5, t * P:(t + 1) * P], zT[:, t * P:(t + 1) * P], w0o[:, :],
                                    start=True, stop=True)
                ins.then_inc(l0_s, 1)
                pe.wait_ge(l0_s_copied, b + 1)

        def retention_vector(dve, step):
            dve.wait_ge(l0_weights, 16 * 5)
            with step.loop(BATCH, 15) as b:
                dve.wait_ge(l0_projected, 2 * b + 1)
                step(dve.tensor_tensor(rot[:, :], banks[:, 0, :], C["cosq"], ALU.mult))
                step(dve.tensor_tensor(qT[:, :], banks[:, 1, :], C["sinq"], ALU.mult))
                dve.tensor_tensor(qT[:, :], qT[:, :], rot[:, :], ALU.add).then_inc(l0_q_ready, 1)
                dve.wait_ge(l0_q_ready, b + 1)
                step(dve.tensor_tensor(rot[:, :], banks[:, 2, :], C["cosk"], ALU.mult))
                step(dve.tensor_tensor(kT[:, :], banks[:, 3, :], C["sink"], ALU.mult))
                dve.tensor_tensor(kT[:, :], kT[:, :], rot[:, :], ALU.add).then_inc(l0_k_ready, 1)

                def mask(c):
                    dve.wait_ge(l0_scores, BT * b + c + 1)
                    dve.tensor_tensor(attT[:, c % 2, :, :],
                                      banks[:, 2 * (c % 2):2 * (c % 2) + 2, :].rearrange("p n (h s) -> p (n h) s", h=4),
                                      bcast(C["tri"].unsqueeze(1), (P, H0, P)), ALU.mult).then_inc(l0_att, 1)

                mask(0)
                dve.wait_ge(l0_sig, b + 1)
                step(dve.tensor_tensor(gate[:, :, :],
                                       banks[:, 4:6, :].rearrange("p n (t w e) -> p (n t) w e", t=2, w=2)[:, :, 1, :],
                                       gate_sig[:, :, :], ALU.mult))
                dve.wait_ge(l0_update, b + 1)
                step(dve.tensor_tensor(state[:, 0, :], banks[:, 6, 0:P], C["decay"], ALU.mult))
                for c in range(1, BT - 1):
                    step(dve.tensor_tensor(state[:, c, :], state[:, c - 1, :], banks[:, 6, c * P:(c + 1) * P], ALU.add))
                    ins = dve.tensor_tensor(state[:, c, :], state[:, c, :], C["decay"], ALU.mult)
                    if c < BT - 2:
                        step(ins)
                ins.then_inc(l0_state, 1)
                for c in range(1, BT):
                    if c >= 2:
                        dve.wait_ge(l0_y, BT * b + c - 1)
                    mask(c)
                dve.wait_ge(l0_y, BT * b + BT)
                y = banks[:, 7, :].rearrange("p (g d) -> p g d", d=D0)
                step(dve.tensor_reduce(mean[:, 0:32], y, X, ALU.add))
                step(dve.tensor_scalar(mean[:, 0:32], mean[:, 0:32], 1.0 / D0, None, ALU.mult))
                dve.tensor_tensor(yc[:, :, :], y, bcast(mean[:, 0:32].unsqueeze(2), (P, 32, D0)), ALU.subtract)\
                    .then_inc(l0_centered, 1)
                dve.wait_ge(l0_squared, b + 1)
                step(dve.tensor_reduce(var[:, 0:32], squares[:, 0:4, :].rearrange("p t (h d) -> p (t h) d", d=D0), X, ALU.add))
                dve.tensor_scalar(var[:, 0:32], var[:, 0:32], 1.0 / D0, EPS, ALU.mult, ALU.add).then_inc(l0_var, 1)
                dve.wait_ge(l0_rstd, b + 1)
                step(dve.tensor_tensor(yc[:, :, :], yc[:, :, :], bcast(rstd[:, 0:32].unsqueeze(2), (P, 32, D0)), ALU.mult))
                y4 = yc[:, :, :].rearrange("p (t h) d -> p t (h d)", t=BT)
                step(dve.tensor_tensor(y4, y4, bcast(gn_w[:, :].unsqueeze(1), (P, BT, D)), ALU.mult))
                step(dve.tensor_tensor(y4, y4, bcast(gn_b[:, :].unsqueeze(1), (P, BT, D)), ALU.add))
                dve.tensor_tensor(y4, y4, gate[:, :, :], ALU.mult).then_inc(l0_z, 1)
                dve.wait_ge(l0_s, b + 1)
                dve.tensor_copy(s_out[:, bass.ds(b * BT, BT), :], banks[:, 5, :].rearrange("p (t d) -> p t d", d=D))\
                    .then_inc(l0_s_copied, 1)

        def retention_scalar(act):
            with act.Fori(0, BATCH) as b:
                act.wait_ge(l0_projected, 2 * b + 2)
                vg = banks[:, 4:6, :].rearrange("p n (t w e) -> p (n t) w e", t=2, w=2)
                act.activation(v_tok[:, :, :], vg[:, :, 0, :], ACT.Copy).then_inc(l0_v_copied, 1)
                act.activation(gate_sig[:, :, :], vg[:, :, 1, :], ACT.Sigmoid).then_inc(l0_sig, 1)
                act.wait_ge(l0_k_turned, b + 1)
                act.activation(k_tok[:, :, :], banks[:, 6, 0:(BT - 1) * P].rearrange("p (c e) -> p c e", e=P), ACT.Copy)\
                    .then_inc(l0_k_tok, 1)
                act.wait_ge(l0_centered, b + 1)
                act.activation(squares[:, 0:4, :], yc[:, :, :].rearrange("p (t h) d -> p t (h d)", t=BT), ACT.Square)\
                    .then_inc(l0_squared, 1)
                act.wait_ge(l0_z_turned, b + 1)
                act.activation(zT[:, :], banks[:, 4, :], ACT.Copy).then_inc(l0_zT, 1)

        def retention_gpsimd(pool, step):
            with pool.Fori(0, BATCH) as b:
                pool.tensor_copy(xb[:, :], xnT[:, bass.ds(b * SEQ, SEQ)]).then_inc(l0_x_copied, 1)
                for c in range(BT):
                    if c == 0:
                        pool.wait_ge(l0_q_ready, b + 1)
                    if c >= 2:
                        pool.wait_ge(l0_scores, BT * b + c - 1)
                    pool.tensor_tensor(q_heads[:, c % 2, :, :], bcast(qT[:, c * P:(c + 1) * P].unsqueeze(1), (P, H0, P)),
                                       bcast(C["heads"].unsqueeze(2), (P, H0, P)), ALU.mult).then_inc(l0_q_heads, 1)
                pool.wait_ge(l0_var, b + 1)
                pool.tensor_tensor(rstd[:, 0:32], var[:, 0:32], minus_half[:, 0:32], ALU.pow).then_inc(l0_rstd, 1)

        shared_logit = sb("shared_logit", [P, TILES])

        logits = sb("logits", [P, TILES, 16])
        second = sb("second", [P, TILES, 16])
        pick1 = sb("pick1", [P, TILES, 16])
        pick2 = sb("pick2", [P, TILES, 16])
        picks = sb("picks", [P, TILES * 16])
        match = sb("match", [P, TILES, 16])
        top = sb("top", [P, 8, TILES])
        totals = sb("totals", [P, 16 * TILES])
        prefix = sb("prefix", [P, 16 * TILES])
        place = sb("place", [P, TILES, 16])
        count = sb("count", [P, 4, 16])
        count_int = sb("count_int", [P, 16], I32)
        slots = sb("slots", [P, 3, TILES], I32)
        weights = sb("weights", [P, 2, TILES])
        tile_cmp = sb("tile_cmp", [P, 48 * 16])
        tile_sum = sb("tile_sum", [P, 48])
        tile_expert = sb("tile_expert", [P, 2, 48], I32)
        router = {0: sb("router0", [P, 8]), 1: sb("router1", [P, 8]), 2: sb("router2", [P, 17]), 3: sb("router3", [P, 8])}
        gate_b1 = sb("gate_b1", [P, 8])
        EXPERTS = {0: 8, 1: 8, 2: 16, 3: 8}
        FFN_TILES = {1: 40, 2: 48}

        routers_loaded = sem("routers_loaded")
        route_logits = sem("route_logits")
        route_gap = sem("route_gap")
        route_exp = sem("route_exp")
        route_picked = sem("route_picked")
        route_counted = sem("route_counted")
        route_slots = sem("route_slots")

        def routing_tensor(pe, layer):
            e = EXPERTS[layer]
            w = e + (layer == 2)
            if layer == 0:
                pe.wait_ge(routers_loaded, 16 * 5)
            pe.wait_ge(xnT_ready, 4 * layer + 4)
            for t in range(TILES):
                ins = pe.matmul(banks[:, 4, t * w:(t + 1) * w], xnT[:, t * P:(t + 1) * P], router[layer][:, 0:w],
                                start=True, stop=True)
            ins.then_inc(route_logits, 1)
            if layer < 3:
                pe.wait_ge(route_picked, layer + 1)
                pe.matmul(banks[:, 5, 0:TILES * e], C["tri"], picks[:, 0:TILES * e], start=True, stop=True)
                pe.matmul(banks[:, 6, 0:TILES * e], ones[:, :], picks[:, 0:TILES * e], start=True, stop=True)\
                    .then_inc(route_counted, 1)

        def routing_scalar(act, layer):
            e = EXPERTS[layer]
            act.wait_ge(route_gap, layer + 1)
            if layer == 0:
                act.activation(match[:, :, 0:e], match[:, :, 0:e], ACT.Exp).then_inc(route_exp, 1)
            else:
                act.activation(top[:, 2, :], top[:, 2, :], ACT.Exp).then_inc(route_exp, 1)

        def routing_vector(dve, step, layer):
            e = EXPERTS[layer]
            w = e + (layer == 2)
            shape = (P, TILES, e)
            lg, lg2, p1, p2, mt, pl = (v[:, :, 0:e] for v in (logits, second, pick1, pick2, match, place))
            rev = C["rev8" if e == 8 else "rev16"]
            rev3 = bcast(rev.unsqueeze(1), shape)

            def wide(v):
                return bcast(v.unsqueeze(2), shape)

            def pick(values, largest, chosen):
                step(dve.tensor_reduce(largest, values, X, ALU.max))
                step(dve.tensor_tensor(mt, values, wide(largest), ALU.is_equal))
                step(dve.tensor_tensor(mt, mt, rev3, ALU.mult))
                step(dve.tensor_reduce(top[:, 7, :], mt, X, ALU.max))
                step(dve.tensor_tensor(chosen, rev3, wide(top[:, 7, :]), ALU.is_equal))

            dve.wait_ge(route_logits, layer + 1)
            raw = banks[:, 4, 0:TILES * w].rearrange("p (t e) -> p t e", e=w)
            if layer == 1:
                step(dve.tensor_tensor(lg, raw[:, :, 0:e], bcast(gate_b1[:, :].unsqueeze(1), shape), ALU.add))
            else:
                step(dve.tensor_copy(lg, raw[:, :, 0:e]))
            if layer == 2:
                step(dve.tensor_copy(shared_logit[:, :], raw[:, :, e]))
            pick(lg, top[:, 0, :], p1)
            all_picks = picks[:, 0:TILES * e].rearrange("p (t e) -> p t e", e=e)
            if layer == 0:
                dve.tensor_copy(all_picks, p1).then_inc(route_picked, 1)
                dve.tensor_tensor(mt, lg, wide(top[:, 0, :]), ALU.subtract).then_inc(route_gap, 1)
            else:
                step(dve.scalar_tensor_tensor(lg2, p1, -1e30, lg, ALU.mult, ALU.add))
                pick(lg2, top[:, 1, :], p2)
                dve.tensor_tensor(all_picks, p1, p2, ALU.add).then_inc(route_picked, 1)
                if layer < 3:
                    dve.tensor_tensor(top[:, 2, :], top[:, 1, :], top[:, 0, :], ALU.subtract).then_inc(route_gap, 1)
                else:
                    return
            dve.wait_ge(route_exp, layer + 1)
            if layer == 0:
                step(dve.tensor_reduce(top[:, 3, :], mt, X, ALU.add))
                step(dve.reciprocal(top[:, 4, :], top[:, 3, :]))
            else:
                step(dve.tensor_scalar(top[:, 3, :], top[:, 2, :], 1.0, None, ALU.add))
                step(dve.reciprocal(weights[:, 0, :], top[:, 3, :]))
                step(dve.tensor_tensor(weights[:, 1, :], top[:, 2, :], weights[:, 0, :], ALU.mult))
            dve.wait_ge(route_counted, layer + 1)
            et = (P, e, TILES)
            tot = totals[:, 0:e * TILES]
            pre = prefix[:, 0:e * TILES]
            tot3, pre3 = (v.rearrange("p (e t) -> p e t", e=e) for v in (tot, pre))
            step(dve.tensor_copy(tot3, banks[:, 6, 0:TILES * e].rearrange("p (t e) -> p e t", e=e)))
            step(dve.tensor_tensor_scan(pre, bcast(ones[:, 0:1], (P, e * TILES)), tot, 0.0, ALU.mult, ALU.add))
            step(dve.tensor_tensor(pre, pre, tot, ALU.subtract))
            running = banks[:, 5, 0:TILES * e].rearrange("p (t e) -> p t e", e=e)
            start = count[:, 0, 0:e]
            if layer == 0:
                step(dve.tensor_copy(start, pre3[:, :, 0]))
                step(dve.tensor_tensor(pre3, pre3, bcast(start.unsqueeze(2), et), ALU.subtract))
                step(dve.tensor_tensor(pl, running, pre3.rearrange("p e t -> p t e"), ALU.add))
                step(dve.tensor_tensor(pl, pl, p1, ALU.mult))
                step(dve.tensor_reduce(top[:, 2, :], pl, X, ALU.add))
                step(dve.tensor_tensor(pl, p1, bcast(C["start320"].unsqueeze(1), shape), ALU.mult))
                step(dve.tensor_reduce(top[:, 3, :], pl, X, ALU.add))
                step(dve.tensor_scalar(top[:, 5, :], top[:, 2, :], float(CAP), None, ALU.is_le))
                step(dve.tensor_tensor(weights[:, 0, :], top[:, 4, :], top[:, 5, :], ALU.mult))
                step(dve.tensor_scalar(weights[:, 1, :], top[:, 5, :], -1.0, 1.0, ALU.mult, ALU.add))
                step(dve.scalar_tensor_tensor(top[:, 3, :], top[:, 2, :], -1.0, top[:, 3, :], ALU.add, ALU.add))
                step(dve.tensor_tensor(top[:, 2, :], top[:, 3, :], C["dump"], ALU.subtract))
                step(dve.tensor_tensor(top[:, 2, :], top[:, 2, :], top[:, 5, :], ALU.mult))
                step(dve.tensor_tensor(top[:, 2, :], top[:, 2, :], C["dump"], ALU.add))
                step(dve.tensor_scalar(top[:, 3, :], top[:, 3, :], float(8 * CAP - 1), None, ALU.min))
                step(dve.tensor_copy(slots[:, 2, :], top[:, 3, :]))
                dve.tensor_copy(slots[:, 0, :], top[:, 2, :]).then_inc(route_slots, 1)
            else:
                end, padded, shift = (count[:, n, 0:e] for n in (1, 2, 3))
                step(dve.tensor_copy(start, pre3[:, :, 0]))
                step(dve.tensor_tensor(end, pre3[:, :, TILES - 1], tot3[:, :, TILES - 1], ALU.add))
                step(dve.tensor_tensor(padded, end, start, ALU.subtract))
                step(dve.tensor_scalar(padded, padded, float(P - 1), None, ALU.add))
                step(dve.tensor_copy(count_int[:, 0:e], padded))
                step(dve.tensor_scalar(count_int[:, 0:e], count_int[:, 0:e], 7, None, ALU.arith_shift_right))
                step(dve.tensor_scalar(count_int[:, 0:e], count_int[:, 0:e], 7, None, ALU.logical_shift_left))
                step(dve.tensor_copy(padded, count_int[:, 0:e]))
                step(dve.tensor_tensor_scan(end, bcast(ones[:, 0:1], (P, e)), padded, 0.0, ALU.mult, ALU.add))
                step(dve.tensor_tensor(shift, end, padded, ALU.subtract))
                step(dve.tensor_tensor(shift, shift, start, ALU.subtract))
                step(dve.tensor_tensor(pre3, pre3, bcast(shift.unsqueeze(2), et), ALU.add))
                step(dve.tensor_tensor(pl, running, pre3.rearrange("p e t -> p t e"), ALU.add))
                for n, chosen in enumerate((p1, p2)):
                    step(dve.tensor_tensor(mt, pl, chosen, ALU.mult))
                    step(dve.tensor_reduce(top[:, 5, :], mt, X, ALU.add))
                    step(dve.tensor_scalar(slots[:, n, :], top[:, 5, :], -1.0, None, ALU.add))
                n_tiles = FFN_TILES[layer]
                cmp3 = tile_cmp[:, 0:n_tiles * e].rearrange("p (j e) -> p j e", e=e)
                step(dve.tensor_tensor(cmp3, bcast(end.unsqueeze(1), (P, n_tiles, e)),
                                       bcast(C["thr"][:, 0:n_tiles].unsqueeze(2), (P, n_tiles, e)), ALU.is_le))
                step(dve.tensor_reduce(tile_sum[:, 0:n_tiles], cmp3, X, ALU.add))
                step(dve.tensor_scalar(tile_sum[:, 0:n_tiles], tile_sum[:, 0:n_tiles], float(e - 1), None, ALU.min))
                dve.tensor_copy(tile_expert[:, layer - 1, 0:n_tiles], tile_sum[:, 0:n_tiles]).then_inc(route_slots, 1)

        rows_in, rows_out = scratch["rows_in"], scratch["rows_out"]
        zeros = sb("zeros", [P, 512])
        zeros_set = sem("zeros_set")
        rows_zeroed = sem("rows_zeroed")
        rows_sent = [sem(f"rows_sent{n}") for n in range(3)]
        rows_back = [sem(f"rows_back{n}") for n in range(3)]
        rows_stored = [sem(f"rows_stored{n}") for n in range(3)]
        fetched = Region(8 * 1024)("fetched", [P, 2, TILES, D])

        def send_rows(pool, layer):
            pool.wait_ge(route_slots, layer + 1)
            pool.wait_ge(rows_zeroed, 16 * 3)
            for k in range(1 if layer == 0 else 2):
                for t in range(TILES):
                    pool.indirect_dma_start(
                        out=rows_in[layer], out_offset=bass.IndirectOffsetOnAxis(ap=slots[:, k, t:t + 1].bitcast(U32), axis=0),
                        in_=xn[:, t, :], in_offset=None).then_inc(rows_sent[layer], 16)

        def fetch_rows(pool, layer, stores):
            pool.wait_ge(rows_stored[layer], 16 * stores)
            for k in range(1 if layer == 0 else 2):
                for t in range(TILES):
                    n = 2 if layer == 0 else k
                    pool.indirect_dma_start(
                        out=fetched[:, k, t, :], out_offset=None,
                        in_=rows_out[layer], in_offset=bass.IndirectOffsetOnAxis(ap=slots[:, n, t:t + 1].bitcast(U32), axis=0))\
                        .then_inc(rows_back[layer], 16)

        w1_buf = l0("w1_buf", [P, 2, F])
        w2_buf = l0("w2_buf", [P, 2, F // P, D])
        x80 = l0("x80", [PART, 2, 4, D])
        x80T = l0("x80T", [P, 2, CAP])
        hT0 = l0("hT0", [P, F // P, CAP])
        y80 = l0("y80", [PART, 2, 4, D])
        f0_loaded = [sem(f"f0_loaded{n}") for n in range(2)]
        f0_turned = sem("f0_turned")
        f0_xT = sem("f0_xT")
        f0_up = sem("f0_up")
        f0_hidden = sem("f0_hidden")
        f0_down = [sem(f"f0_down{n}") for n in range(2)]
        f0_copied = sem("f0_copied")

        def experts0_sync(sp):
            sp.wait_ge(rows_sent[0], 16 * TILES)
            with sp.Fori(0, 4) as i:
                for n in range(2):
                    e = sp.snap(2 * i + n)
                    at = sp.snap(e * D)
                    sp.wait_ge(f0_down[n], i + 1)
                    sp.dma_start(w1_buf[:, n, :], a["L0_ffn_W1"][bass.ds(at, D), :]).then_inc(f0_loaded[n], 16)
                    sp.dma_start(w2_buf[:, n, :, :], a["L0_ffn_W2"][bass.ds(e * F, F), :].rearrange("(c p) d -> p c d", p=P))\
                        .then_inc(f0_loaded[n], 16)
                    sp.dma_start(x80[:, n, :, :], rows_in[0][bass.ds(e * CAP, CAP), :].rearrange("(j p) d -> p j d", p=PART))\
                        .then_inc(f0_loaded[n], 16)

        def experts0_tensor(pe):
            for n in range(2):
                pe.sem_inc(f0_down[n], 1)
            with pe.Fori(0, 4) as i:
                for n in range(2):
                    pe.wait_ge(f0_loaded[n], 48 * i + 48)
                    for j in range(4):
                        ins = pe.transpose(banks[:, 4, j * PART:(j + 1) * PART], x80[:, n, j, :], C["ident"][0:PART, 0:PART])
                    ins.then_inc(f0_turned, 1)
                    pe.wait_ge(f0_xT, 2 * i + n + 1)
                    for c in range(F // P):
                        pe.matmul(banks[:, c, 0:CAP], w1_buf[:, n, c * P:(c + 1) * P], x80T[:, n, :], start=True, stop=True)\
                            .then_inc(f0_up, 1)
                    pe.wait_ge(f0_hidden, 4 * (2 * i + n) + 4)
                    for j in range(4):
                        for c in range(F // P):
                            ins = pe.matmul(banks[0:PART, 5, j * D:(j + 1) * D], hT0[:, c, j * PART:(j + 1) * PART],
                                            w2_buf[:, n, c, :], start=(c == 0), stop=(c == F // P - 1))
                    ins.then_inc(f0_down[n], 1)
                    pe.wait_ge(f0_copied, 2 * i + n + 1)

        def experts0_scalar(act):
            with act.Fori(0, 4) as i:
                for n in range(2):
                    act.wait_ge(f0_turned, 2 * i + n + 1)
                    act.activation(x80T[:, n, :], banks[:, 4, 0:CAP], ACT.Copy).then_inc(f0_xT, 1)
                    for c in range(0, F // P):
                        act.wait_ge(f0_up, 4 * (2 * i + n) + c + 1)
                        act.activation(hT0[:, c, :], banks[:, c, 0:CAP], ACT.Relu).then_inc(f0_hidden, 1)

        def experts0_vector(dve):
            with dve.Fori(0, 4) as i:
                for n in range(2):
                    dve.wait_ge(f0_down[n], i + 2)
                    dve.tensor_copy(y80[:, n, :, :], banks[0:PART, 5, :].rearrange("p (j d) -> p j d", d=D))\
                        .then_inc(f0_copied, 1)
                dve.wait_ge(rows_stored[0], 32 * i + 32)

        def experts0_gpsimd(pool):
            with pool.Fori(0, 4) as i:
                for n in range(2):
                    pool.wait_ge(f0_copied, 2 * i + n + 1)
                    pool.dma_start(rows_out[0][bass.ds((2 * i + n) * CAP, CAP), :].rearrange("(j p) d -> p j d", p=PART),
                                   y80[:, n, :, :]).then_inc(rows_stored[0], 16)

        mix_ready = sem("mix_ready")
        mix_sigmoid = sem("mix_sigmoid")

        def mix_vector(dve, step, layer):
            def wide(v):
                return bcast(v.unsqueeze(2), (P, TILES, D))
            if layer < 3:
                dve.wait_ge(rows_back[layer], 16 * TILES * (1 if layer == 0 else 2))
                w = [wide(weights[:, n, :]) for n in range(2)]
                step(dve.tensor_tensor(fetched[:, 0, :, :], fetched[:, 0, :, :], w[0], ALU.mult))
                if layer == 2:
                    step(dve.tensor_tensor(fetched[:, 0, :, :], fetched[:, 0, :, :], g_out[:, :, :], ALU.add))
                other = xn[:, :, :] if layer == 0 else fetched[:, 1, :, :]
                step(dve.tensor_tensor(g_out[:, :, :], other, w[1], ALU.mult))
                dve.tensor_tensor(g_out[:, :, :], g_out[:, :, :], fetched[:, 0, :, :], ALU.add).then_inc(mix_ready, 1)
                dve.wait_ge(mix_ready, layer + 1)
            step(dve.tensor_tensor(s_out[:, :, :], s_out[:, :, :], g_out[:, :, :], ALU.mult))
            dve.wait_ge(mix_sigmoid, layer + 1)
            step(dve.tensor_tensor(s_out[:, :, :], s_out[:, :, :], squares[:, :, :], ALU.mult))
            ins = dve.tensor_tensor(x[:, :, :], x[:, :, :], s_out[:, :, :], ALU.add)
            if layer < 3:
                step(ins)
            else:
                ins.then_inc(x_final, 1)

        def mix_scalar(act, layer):
            act.wait_ge(mix_ready, layer + 1)
            act.activation(squares[:, :, :], g_out[:, :, :], ACT.Sigmoid).then_inc(mix_sigmoid, 1)


        at = Region(0, LATE)
        wqkv = at("wqkv", [P, 3, P])
        wout = at("wout", [P, P])
        qk_bias = at("qk_bias", [P, 2])
        v_bias = at("v_bias", [P, P])
        out_bias = at("out_bias", [P, P])
        xb1 = at("xb1", [P, SEQ])
        qk = at("qk", [P, 2, SEQ])
        parts = at("parts", [P, 3, 2, SEQ], BF16)
        v_sum = at("v_sum", [P, TILES, H1, D1 + 1])
        stack = at("stack", [P, 2, H1 // 2, SEQ], BF16)
        neg_max = at("neg_max", [P, 2, 8])
        prob = at("prob", [P, 2, 1024])
        probT = at("probT", [P, 2, 2, 512])
        o_rec = at("o_rec", [P, 32])
        o_tok = at("o_tok", [P, BT, D])
        oT = at("oT", [P, SEQ])
        identb = sb("identb", [P, P], BF16)
        negb = sb("negb", [P, P], BF16)
        part_rows = scratch["parts"]
        Q_PARTS, K_PARTS = (0, 1, 0, 1, 0, 2), (0, 0, 1, 1, 2, 0)
        STACK = len(Q_PARTS) * D1

        UNITS = [(half, first, n, qt) for half in range(2)
                 for qt, n in ((0, 8), (1, 4), (2, 2), (3, 2)) for first in range(0, 8, n)]
        NU = len(UNITS)

        at_weights = sem("at_weights")
        at_x_copied = sem("at_x_copied")
        at_projected = sem("at_projected")
        at_biased = sem("at_biased")
        at_parts = sem("at_parts")
        at_parts_stored = sem("at_parts_stored")
        at_stacked = [sem(f"at_stacked{n}") for n in range(2)]
        at_half_done = [sem(f"at_half_done{n}") for n in range(2)]
        at_scores = sem("at_scores")
        at_max = sem("at_max")
        at_exp = sem("at_exp")
        at_turned = sem("at_turned")
        at_probT = [sem(f"at_probT{n}") for n in range(2)]
        at_pv = sem("at_pv")
        at_o = sem("at_o")
        at_o_turned = sem("at_o_turned")
        at_oT = sem("at_oT")
        at_s = sem("at_s")
        at_s_copied = sem("at_s_copied")

        def attention_sync(sp, run):
            layer = 2 * run + 1
            if run == 0:
                sp.wait_ge(norm_done, 2)
            else:
                sp.wait_ge(norm_done, 4)
            sp.dma_start(wqkv, a[f"wqkv{layer}"]).then_inc(at_weights, 16)
            sp.dma_start(wout, a[f"wout{layer}"]).then_inc(at_weights, 16)
            sp.dma_start(qk_bias, a[f"qk_bias{layer}"]).then_inc(at_weights, 16)
            sp.dma_start(v_bias, a[f"v_bias{layer}"].partition_broadcast(P)).then_inc(at_weights, 16)
            sp.dma_start(out_bias, a[f"out_bias{layer}"].partition_broadcast(P)).then_inc(at_weights, 16)
            B0 = BATCH * run
            with sp.Fori(B0, B0 + BATCH) as b:
                row = sp.snap((b - B0) * 6)
                sp.wait_ge(at_parts, b + 1)
                sp.dma_start(part_rows[bass.ds(row, 6), :, :].rearrange("n p s -> p n s"),
                             parts.rearrange("p a b s -> p (a b) s")).then_inc(at_parts_stored, 16)
            with sp.Fori(B0, B0 + BATCH) as b:
                for half in range(2):
                    if half == 0:
                        sp.wait_ge(at_parts_stored, 16 * (B0 + BATCH))
                    rows = [sp.snap((b - B0) * 6 + n) for n in range(6)]
                    sp.wait_ge(at_half_done[half], b + 1)
                    for w, which in enumerate((Q_PARTS, K_PARTS)):
                        for r, part in enumerate(which):
                            lo = 64 * half + r * D1
                            sp.dma_start(stack[lo:lo + D1, w, :, :],
                                         part_rows[bass.ds(rows[2 * part + w], 1), half * 64:half * 64 + 64, :]
                                         .rearrange("o (h i) s -> (o i) h s", i=D1)).then_inc(at_stacked[half], 16)

        def attention_gpsimd(pool, run):
            B0 = BATCH * run
            pool.wait_ge(xnT_ready, 8 * run + 8)
            with pool.Fori(B0, B0 + BATCH) as b:
                pool.tensor_copy(xb1, xnT[:, bass.ds((b - B0) * SEQ, SEQ)]).then_inc(at_x_copied, 1)
                pool.wait_ge(at_projected, b + 1)

        def attention_tensor(pe, run):
            B0 = BATCH * run
            pe.wait_ge(at_weights, 80 * (run + 1))
            with pe.Fori(B0, B0 + BATCH) as b:
                pe.wait_ge(at_x_copied, b + 1)
                for n in range(2):
                    pe.matmul(banks[:, n, :], wqkv[:, n, :], xb1, start=True, stop=True)
                for t in range(BT):
                    ins = pe.matmul(banks[:, 2, t * P:(t + 1) * P], xb1[:, t * P:(t + 1) * P], wqkv[:, 2, :],
                                    start=True, stop=True)
                ins.then_inc(at_projected, 1)
                pe.wait_ge(at_biased, b + 1)

            def scores(b, u):
                half, first, n, qt = UNITS[u]
                if u % (NU // 2) == 0:
                    pe.wait_ge(at_stacked[half], 16 * 12 * b + 16 * 12)
                if u >= 2:
                    pe.wait_ge(at_exp, NU * b + u - 1)
                lo, length = 64 * half, (qt + 1) * P
                for g in range(n):
                    flat = g * length if qt < 2 else g * 512
                    bank, col = 2 * (u % 2) + flat // 512, flat % 512
                    pe.matmul(banks[:, bank, col:col + length], stack[lo:lo + STACK, 0, first + g, qt * P:(qt + 1) * P],
                              stack[lo:lo + STACK, 1, first + g, 0:length], start=True, stop=False)
                    ins = pe.matmul(banks[:, bank, col + length - P:col + length], identb[:, :], negb[:, :],
                                    start=False, stop=True)
                ins.then_inc(at_scores, 1)

            def turn(b, u):
                half, first, n, qt = UNITS[u]
                length = (qt + 1) * P
                blocks = n * (qt + 1) // 2
                pe.wait_ge(at_exp, NU * b + u + 1)
                for k in range(2):
                    if u >= 1:
                        pe.wait_ge(at_probT[k], NU * b + u)
                    for m in range(blocks):
                        flat = (k * blocks + m) * P
                        ins = pe.transpose(banks[:, 4 + k, m * P:(m + 1) * P], prob[:, u % 2, flat:flat + P], C["ident"])
                    ins.then_inc(at_turned, 1)

            def values(b, u):
                half, first, n, qt = UNITS[u]
                for k in range(2):
                    pe.wait_ge(at_probT[k], NU * b + u + 1)
                    for g in range(n // 2):
                        h = first + k * (n // 2) + g
                        for kt in range(qt + 1):
                            m = g * (qt + 1) + kt
                            col = qt * 72 + h * 9
                            ins = pe.matmul(banks[:, 6 + half, col:col + 9], probT[:, u % 2, k, m * P:(m + 1) * P],
                                            v_sum[:, bass.ds((b - B0) * BT + kt, 1), 8 * half + h, :].rearrange("p a e -> p (a e)"),
                                            start=(kt == 0), stop=(kt == qt))
                ins.then_inc(at_pv, 1)

            with pe.Fori(B0, B0 + BATCH) as b:
                scores(b, 0)
                for u in range(NU):
                    if u + 1 < NU:
                        scores(b, u + 1)
                    turn(b, u)
                    if u >= 1:
                        values(b, u - 1)
                values(b, NU - 1)
                pe.wait_ge(at_o, 2 * b + 2)
                for t in range(BT):
                    ins = pe.transpose(banks[:, 4, t * P:(t + 1) * P], o_tok[:, t, :], C["ident"])
                ins.then_inc(at_o_turned, 1)
                pe.wait_ge(at_oT, b + 1)
                for t in range(BT):
                    ins = pe.matmul(banks[:, 5, t * P:(t + 1) * P], oT[:, t * P:(t + 1) * P], wout, start=True, stop=True)
                ins.then_inc(at_s, 1)
                pe.wait_ge(at_s_copied, b + 1)

        def unit_view(ap, n, qt):
            length = (qt + 1) * P
            if qt < 2:
                return ap[:, 0:n * length].rearrange("p (g l) -> p g l", g=n)
            return ap.rearrange("p (g l) -> p g l", g=n)[:, :, 0:length]

        def attention_vector(dve, step, run):
            B0 = BATCH * run
            dve.wait_ge(at_weights, 80 * (run + 1))
            step(dve.memset(v_sum, 1.0))
            with step.loop_from(B0, BATCH, 4) as b:
                dve.wait_ge(at_projected, b + 1)
                dve.tensor_scalar(qk[:, 0, :], banks[:, 0, :], qk_bias[:, 0:1], float(D1) ** -0.5, ALU.add, ALU.mult)
                dve.tensor_scalar(qk[:, 1, :], banks[:, 1, :], qk_bias[:, 1:2], None, ALU.add)
                v = banks[:, 2, :].rearrange("p (t h e) -> p t h e", t=BT, e=D1)
                vb = v_bias.rearrange("p (h e) -> p h e", e=D1)
                for t in range(BT):
                    ins = dve.tensor_tensor(v_sum[:, bass.ds((b - B0) * BT + t, 1), :, 0:D1].rearrange("p a h e -> p (a h) e"),
                                            v[:, t, :, :], vb, ALU.add)
                ins.then_inc(at_biased, 1)
                dve.wait_ge(at_biased, b + 1)
                step(dve.tensor_copy(parts[:, 0, :, :], qk))
                step(dve.tensor_tensor(qk, qk, parts[:, 0, :, :], ALU.subtract))
                step(dve.tensor_copy(parts[:, 1, :, :], qk))
                step(dve.tensor_tensor(qk, qk, parts[:, 1, :, :], ALU.subtract))
                dve.tensor_copy(parts[:, 2, :, :], qk).then_inc(at_parts, 1)
                dve.wait_ge(at_parts_stored, 16 * b + 16)

            def maxima(b, u):
                half, first, n, qt = UNITS[u]
                dve.wait_ge(at_scores, NU * b + u + 1)
                s = unit_view(banks[:, 2 * (u % 2):2 * (u % 2) + 2, :].rearrange("p a c -> p (a c)"), n, qt)
                dve.tensor_reduce(neg_max[:, u % 2, 0:n], s, X, ALU.max, negate=True).then_inc(at_max, 1)

            def copy_turned(b, u):
                half, first, n, qt = UNITS[u]
                cols = n * (qt + 1) // 2 * P
                dve.wait_ge(at_turned, 2 * NU * b + 2 * u + 1)
                if u >= 2:
                    dve.wait_ge(at_pv, NU * b + u - 1)
                dve.tensor_copy(probT[:, u % 2, 0, 0:cols], banks[:, 4, 0:cols]).then_inc(at_probT[0], 1)

            def normalize(b, half):
                dve.wait_ge(at_pv, NU * b + (NU // 2) * (half + 1))
                o = banks[:, 6 + half, 0:288].rearrange("p (t h e) -> p t h e", t=BT, e=D1 + 1)
                rec = o_rec.rearrange("p (t h) -> p t h", t=BT)
                step(dve.reciprocal(rec, o[:, :, :, D1]))
                dve.tensor_tensor(o_tok.rearrange("p t (h e) -> p t h e", e=D1)[:, :, 8 * half:8 * half + 8, :],
                                  o[:, :, :, 0:D1], bcast(rec.unsqueeze(3), (P, BT, 8, D1)), ALU.mult).then_inc(at_o, 1)

            with step.loop_from(B0, BATCH, 2) as b:
                maxima(b, 0)
                for u in range(NU):
                    if u + 1 < NU:
                        maxima(b, u + 1)
                    copy_turned(b, u)
                    if u == NU // 2 + 2:
                        normalize(b, 0)
                normalize(b, 1)
                dve.wait_ge(at_s, b + 1)
                dve.tensor_tensor(s_out[:, bass.ds((b - B0) * BT, BT), :], banks[:, 5, :].rearrange("p (t d) -> p t d", d=D),
                                  bcast(out_bias.unsqueeze(1), (P, BT, D)), ALU.add).then_inc(at_s_copied, 1)

        def attention_scalar(act, run):
            B0 = BATCH * run
            if run == 0:
                for half in range(2):
                    act.sem_inc(at_half_done[half], 1)

            def exps(b, u):
                half, first, n, qt = UNITS[u]
                length = (qt + 1) * P
                act.wait_ge(at_max, NU * b + u + 1)
                if u >= 2:
                    act.wait_ge(at_turned, 2 * NU * b + 2 * u - 2)
                s = unit_view(banks[:, 2 * (u % 2):2 * (u % 2) + 2, :].rearrange("p a c -> p (a c)"), n, qt)
                for g in range(n):
                    ins = act.activation(prob[:, u % 2, g * length:(g + 1) * length], s[:, g, :], ACT.Exp,
                                         bias=neg_max[:, u % 2, g:g + 1])
                    if g == 0 and u % (NU // 2) == NU // 2 - 1:
                        ins.then_inc(at_half_done[half], 1)
                ins.then_inc(at_exp, 1)

            def copy_turned(b, u):
                half, first, n, qt = UNITS[u]
                cols = n * (qt + 1) // 2 * P
                act.wait_ge(at_turned, 2 * NU * b + 2 * u + 2)
                if u >= 2:
                    act.wait_ge(at_pv, NU * b + u - 1)
                act.activation(probT[:, u % 2, 1, 0:cols], banks[:, 5, 0:cols], ACT.Copy).then_inc(at_probT[1], 1)

            with act.Fori(B0, B0 + BATCH) as b:
                exps(b, 0)
                for u in range(NU):
                    if u + 1 < NU:
                        exps(b, u + 1)
                    copy_turned(b, u)
                act.wait_ge(at_o_turned, b + 1)
                act.activation(oT, banks[:, 4, :], ACT.Copy).then_inc(at_oT, 1)

        f1w = Region(LATE)
        w1_all = f1w("w1_all", [P, 8, F])
        w2_all = f1w("w2_all", [P, 8, F // P, D])
        b1_all = f1w("b1_all", [P, 8, F])
        b2_all = f1w("b2_all", [P, 8, D])
        f1 = Region(0)
        rows4 = f1("rows4", [P, 2, 4, D])
        rowsT = f1("rowsT", [P, 2, 4, P])
        hid = f1("hid", [P, 2, F])
        hidT = f1("hidT", [P, 2, F])
        out4 = f1("out4", [P, 2, 4, D])
        f1_weights = sem("f1_weights")
        f1_loaded = [sem(f"f1_loaded{n}") for n in range(2)]
        f1_turned = sem("f1_turned")
        f1_rowsT = sem("f1_rowsT")
        f1_up = sem("f1_up")
        f1_hid = sem("f1_hid")
        f1_hid_turned = sem("f1_hid_turned")
        f1_hidT = sem("f1_hidT")
        f1_down = sem("f1_down")
        f1_out = sem("f1_out")

        def experts1_weights(sp):
            sp.dma_start(w1_all, a["L1_ffn_W1"].rearrange("(e p) f -> p e f", p=P)).then_inc(f1_weights, 16)
            sp.dma_start(w2_all, a["L1_ffn_W2"].rearrange("(e c p) d -> p e c d", e=8, p=P)).then_inc(f1_weights, 16)
            sp.dma_start(b1_all.rearrange("p e f -> p (e f)"), a["L1_ffn_b1"].partition_broadcast(P)).then_inc(f1_weights, 16)
            sp.dma_start(b2_all.rearrange("p e d -> p (e d)"), a["L1_ffn_b2"].partition_broadcast(P)).then_inc(f1_weights, 16)

        def experts1_sync(sp):
            sp.wait_ge(rows_sent[1], 16 * TILES * 2)
            sp.wait_ge(at_s_copied, BATCH)
            with sp.Fori(0, 5) as i:
                for n in range(2):
                    row = sp.snap((2 * i + n) * 4 * P)
                    sp.wait_ge(f1_turned, 2 * i + n + 1)
                    sp.dma_start(rows4[:, n, :, :], rows_in[1][bass.ds(row, 4 * P), :].rearrange("(j p) d -> p j d", p=P))\
                        .then_inc(f1_loaded[n], 16)

        def expert_of(eng, layer, tile):
            return eng.value_load(tile_expert[0:1, layer - 1, bass.ds(tile, 1)], min_val=0, max_val=EXPERTS[layer] - 1)

        def experts1_tensor(pe):
            pe.sem_inc(f1_turned, 2)
            pe.wait_ge(f1_weights, 64)
            pe.wait_ge(route_slots, 2)
            with pe.Fori(0, 5) as i:
                for n in range(2):
                    g = 2 * i + n
                    experts = [expert_of(pe, 1, 4 * g + j) for j in range(4)]
                    pe.wait_ge(f1_loaded[n], 16 * i + 16)
                    for j in range(4):
                        ins = pe.transpose(banks[:, 0, j * P:(j + 1) * P], rows4[:, n, j, :], C["ident"])
                    ins.then_inc(f1_turned, 1)
                    pe.wait_ge(f1_rowsT, g + 1)

                    def up(j):
                        if j >= 2:
                            pe.wait_ge(f1_hid, 4 * g + j - 1)
                        pe.matmul(banks[:, 1 + j % 2, :], rowsT[:, n, j, :],
                                  w1_all[:, bass.ds(experts[j], 1), :].rearrange("p a f -> p (a f)"), start=True, stop=True)\
                            .then_inc(f1_up, 1)

                    def turn(j):
                        pe.wait_ge(f1_hid, 4 * g + j + 1)
                        if j >= 2:
                            pe.wait_ge(f1_hidT, 4 * g + j - 1)
                        for c in range(F // P):
                            ins = pe.transpose(banks[:, 3 + j % 2, c * P:(c + 1) * P], hid[:, j % 2, c * P:(c + 1) * P], C["ident"])
                        ins.then_inc(f1_hid_turned, 1)

                    def down(j):
                        pe.wait_ge(f1_hidT, 4 * g + j + 1)
                        for c in range(F // P):
                            ins = pe.matmul(banks[:, 5, j * D:(j + 1) * D], hidT[:, j % 2, c * P:(c + 1) * P],
                                            w2_all[:, bass.ds(experts[j], 1), c, :].rearrange("p a d -> p (a d)"),
                                            start=(c == 0), stop=(c == F // P - 1))
                        ins.then_inc(f1_down, 1)

                    up(0)
                    for j in range(4):
                        if j + 1 < 4:
                            up(j + 1)
                        turn(j)
                        if j >= 1:
                            down(j - 1)
                    down(3)
                    pe.wait_ge(f1_out, 4 * g + 4)

        def experts1_vector(dve):
            with dve.Fori(0, 5) as i:
                for n in range(2):
                    g = 2 * i + n
                    experts = [expert_of(dve, 1, 4 * g + j) for j in range(4)]
                    for j in range(4):
                        dve.wait_ge(f1_up, 4 * g + j + 1)
                        dve.tensor_tensor(hid[:, j % 2, :], banks[:, 1 + j % 2, :],
                                          b1_all[:, bass.ds(experts[j], 1), :].rearrange("p a f -> p (a f)"), ALU.add)\
                            .then_inc(f1_hid, 1)
                        if j == 3:
                            dve.wait_ge(f1_down, 4 * g + 4)
                            for m in range(4):
                                dve.tensor_tensor(out4[:, n, m, :], banks[:, 5, m * D:(m + 1) * D],
                                                  b2_all[:, bass.ds(experts[m], 1), :].rearrange("p a d -> p (a d)"), ALU.add)\
                                    .then_inc(f1_out, 1)
                dve.wait_ge(rows_stored[1], 32 * i + 32)

        def experts1_scalar(act):
            with act.Fori(0, 5) as i:
                for n in range(2):
                    g = 2 * i + n
                    act.wait_ge(f1_turned, g + 3)
                    act.activation(rowsT[:, n, :, :].rearrange("p j s -> p (j s)"), banks[:, 0, :], ACT.Copy)\
                        .then_inc(f1_rowsT, 1)
                    for j in range(4):
                        act.wait_ge(f1_hid_turned, 4 * g + j + 1)
                        act.activation(hidT[:, j % 2, :], banks[:, 3 + j % 2, :], ACT.Relu).then_inc(f1_hidT, 1)

        def experts1_gpsimd(pool):
            with pool.Fori(0, 5) as i:
                for n in range(2):
                    pool.wait_ge(f1_out, 4 * (2 * i + n) + 4)
                    pool.dma_start(rows_out[1][bass.ds((2 * i + n) * 4 * P, 4 * P), :].rearrange("(j p) d -> p j d", p=P),
                                   out4[:, n, :, :]).then_inc(rows_stored[1], 16)


        gr = Region(0, LATE)
        gru_in = gr("gru_in", [P, BATCH, SEQ])
        centred = gr("centred", [P, BATCH, SEQ])
        spread = gr("spread", [P, BATCH, SEQ])
        z_gate = gr("z_gate", [P, BATCH, SEQ])
        keep_gate = gr("keep_gate", [P, BATCH, SEQ])
        hid_sig = gr("hid_sig", [P, BATCH, SEQ])
        cand = gr("cand", [P, BATCH, SEQ])
        gru_w = gr("gru_w", [P, 2, P])
        gru_p = gr("gru_p", [P, 5])
        gru_vars = gr("gru_vars", [P, BATCH, BT])
        gru_rstds = gr("gru_rstds", [P, BATCH, BT])
        gru_all = Region(LATE)("gru_all", [P, 3, 2 * P + 4])
        inv_d = sb("inv_d", [P, P])

        gru_loaded = sem("gru_loaded")
        gru_begun = sem("gru_begun")
        gru_set = sem("gru_set")
        gru_mean = sem("gru_mean")
        gru_centred = sem("gru_centred")
        gru_squared = sem("gru_squared")
        gru_var = sem("gru_var")
        gru_spread = sem("gru_spread")
        gru_var_eps = sem("gru_var_eps")
        gru_rstd = sem("gru_rstd")
        gru_normed = sem("gru_normed")
        gru_affine = sem("gru_affine")
        gru_gates = sem("gru_gates")
        gru_sig = sem("gru_sig")
        gru_cand = sem("gru_cand")
        gru_weighed = sem("gru_weighed")
        gru_out = sem("gru_out")
        gru_turned = sem("gru_turned")
        gru_copied = sem("gru_copied")

        def gru_tensor(pe):
            with pe.Fori(0, 3) as l:
                pe.wait_ge(gru_set, l + 1)
                for b in range(BATCH):
                    pe.wait_ge(gru_out, BATCH * l + b + 1)
                    pe.matmul(banks[:, b, :], inv_d[:, :], gru_in[:, b, :], start=True, stop=True).then_inc(gru_mean, 1)
                for b in range(BATCH):
                    pe.wait_ge(gru_squared, BATCH * l + b + 1)
                    for t in range(BT):
                        ins = pe.matmul(banks[:, 4 + b, t:t + 1], spread[:, b, t * P:(t + 1) * P], inv_d[:, 0:1],
                                        start=True, stop=True)
                    ins.then_inc(gru_var, 1)
                for b in range(BATCH):
                    pe.wait_ge(gru_rstd, BATCH * l + b + 1)
                    for t in range(BT):
                        ins = pe.matmul(banks[:, 4 + b, t * P:(t + 1) * P], bcast(gru_rstds[:, b, t:t + 1], (P, P)), C["ident"],
                                        start=True, stop=True)
                    ins.then_inc(gru_spread, 1)
                for b in range(BATCH):
                    pe.wait_ge(gru_affine, BATCH * l + b + 1)
                    pe.matmul(banks[:, b, :], gru_w[:, 0, :], centred[:, b, :], start=True, stop=True)
                    pe.matmul(banks[:, 4 + b, :], gru_w[:, 1, :], centred[:, b, :], start=True, stop=True).then_inc(gru_gates, 1)
            pe.wait_ge(gru_out, 4 * BATCH)
            for t in range(TILES):
                ins = pe.transpose(banks[:, t // 4, (t % 4) * P:(t % 4 + 1) * P], gru_in[:, t // BT, (t % BT) * P:(t % BT + 1) * P],
                                   C["ident"])
                if t % 4 == 3:
                    ins.then_inc(gru_turned, 1)

        def gru_vector(dve, step):
            dve.wait_ge(xnT_ready, 12)
            for b in range(BATCH):
                dve.tensor_copy(gru_in[:, b, :], xnT[:, b * SEQ:(b + 1) * SEQ]).then_inc(gru_out, 1)
            dve.wait_ge(gru_out, BATCH)
            with step.loop(3, 2 * BATCH) as l:
                for b in range(BATCH):
                    dve.wait_ge(gru_mean, BATCH * l + b + 1)
                    dve.tensor_tensor(centred[:, b, :], gru_in[:, b, :], banks[:, b, :], ALU.subtract).then_inc(gru_centred, 1)
                for b in range(BATCH):
                    dve.wait_ge(gru_var, BATCH * l + b + 1)
                    dve.tensor_scalar(gru_vars[:, b, :], banks[:, 4 + b, 0:BT], EPS, None, ALU.add).then_inc(gru_var_eps, 1)
                for b in range(BATCH):
                    dve.wait_ge(gru_spread, BATCH * l + b + 1)
                    dve.tensor_tensor(centred[:, b, :], centred[:, b, :], banks[:, 4 + b, :], ALU.mult).then_inc(gru_normed, 1)
                for b in range(BATCH):
                    dve.wait_ge(gru_sig, BATCH * l + b + 1)
                    step(dve.tensor_scalar(cand[:, b, :], banks[:, 4 + b, :], gru_p[:, 3:4], 0.0, ALU.add, ALU.max))
                    dve.scalar_tensor_tensor(cand[:, b, :], hid_sig[:, b, :], 0.5, cand[:, b, :], ALU.min, ALU.add)\
                        .then_inc(gru_cand, 1)
                for b in range(BATCH):
                    dve.wait_ge(gru_weighed, BATCH * l + b + 1)
                    step(dve.tensor_tensor_scan(hid_sig[:, b, :], keep_gate[:, b, :], cand[:, b, :], 0.5, ALU.mult, ALU.add))
                    dve.tensor_tensor(gru_in[:, b, :], gru_in[:, b, :], hid_sig[:, b, :], ALU.add).then_inc(gru_out, 1)
            for k in range(4):
                dve.wait_ge(gru_turned, k + 1)
                dve.tensor_copy(s_out[:, 4 * k:4 * k + 4, :], banks[:, k, :].rearrange("p (t d) -> p t d", d=D))\
                    .then_inc(gru_copied, 1)

        def gru_scalar(act):
            with act.Fori(0, 3) as l:
                for b in range(BATCH):
                    act.wait_ge(gru_centred, BATCH * l + b + 1)
                    act.activation(spread[:, b, :], centred[:, b, :], ACT.Square).then_inc(gru_squared, 1)
                for b in range(BATCH):
                    act.wait_ge(gru_normed, BATCH * l + b + 1)
                    act.activation(centred[:, b, :], centred[:, b, :], ACT.Identity, bias=gru_p[:, 1:2], scale=gru_p[:, 0:1])\
                        .then_inc(gru_affine, 1)
                for b in range(BATCH):
                    act.wait_ge(gru_gates, BATCH * l + b + 1)
                    act.activation(z_gate[:, b, :], banks[:, b, :], ACT.Sigmoid, bias=gru_p[:, 2:3])
                    act.activation(keep_gate[:, b, :], banks[:, b, :], ACT.Sigmoid, bias=gru_p[:, 4:5], scale=-1.0)
                    act.activation(hid_sig[:, b, :], banks[:, 4 + b, :], ACT.Sigmoid, bias=gru_p[:, 3:4]).then_inc(gru_sig, 1)

        def gru_gpsimd(pool, step):
            pool.wait_ge(gru_loaded, 16)
            with step.loop(3, 2) as l:
                pool.wait_ge(gru_out, BATCH * l + BATCH)
                step(pool.tensor_copy(gru_w.rearrange("p a e -> p (a e)"), gru_all[:, bass.ds(l, 1), 0:2 * P].rearrange("p a e -> p (a e)")))
                step(pool.tensor_copy(gru_p[:, 0:4], gru_all[:, bass.ds(l, 1), 2 * P:2 * P + 4].rearrange("p a e -> p (a e)")))
                pool.tensor_tensor(gru_p[:, 4:5], zeros[:, 0:1], gru_p[:, 2:3], ALU.subtract).then_inc(gru_set, 1)
                for b in range(BATCH):
                    pool.wait_ge(gru_var_eps, BATCH * l + b + 1)
                    pool.tensor_tensor(gru_rstds[:, b, :], gru_vars[:, b, :], minus_half[:, 0:BT], ALU.pow)\
                        .then_inc(gru_rstd, 1)
                for b in range(BATCH):
                    pool.wait_ge(gru_cand, BATCH * l + b + 1)
                    pool.tensor_tensor(cand[:, b, :], cand[:, b, :], z_gate[:, b, :], ALU.mult).then_inc(gru_weighed, 1)

        E2, F2 = 16, 64
        f2w = Region(LATE + 3 * (2 * P + 4))
        wgu_all = f2w("wgu_all", [P, E2, 2 * F2])
        wd_all = f2w("wd_all", [F2, E2, D])
        shared_w = f2w("shared_w", [P, 4, P])
        shared_d = f2w("shared_d", [P, 2, D])
        shared_sig = f2w("shared_sig", [P, TILES])
        f2 = Region(0, LATE)
        sh_sig = f2("sh_sig", [P, 2, SEQ])
        sh_h = f2("sh_h", [P, 2, SEQ])
        rows4b = f2("rows4b", [P, 2, 4, D])
        rowsTb = f2("rowsTb", [P, 2, 4, P])
        gu_sig = f2("gu_sig", [P, 2, 4, F2])
        hid2 = f2("hid2", [P, 2, 4, 2 * F2])
        hidT2 = f2("hidT2", [F2, 2, 4, P])
        out4b = f2("out4b", [P, 2, 4, D])
        f2_weights = sem("f2_weights")
        sh_gate_sig = sem("sh_gate_sig")
        sh_up = sem("sh_up")
        sh_sigmoid = sem("sh_sigmoid")
        sh_hidden = sem("sh_hidden")
        sh_down = sem("sh_down")
        sh_added = sem("sh_added")
        f2_loaded = [sem(f"f2_loaded{n}") for n in range(2)]
        f2_turned = sem("f2_turned")
        f2_rowsT = sem("f2_rowsT")
        f2_up = sem("f2_up")
        f2_sig = sem("f2_sig")
        f2_hid = sem("f2_hid")
        f2_hid_turned = sem("f2_hid_turned")
        f2_hidT = sem("f2_hidT")
        f2_down = sem("f2_down")
        f2_out = sem("f2_out")

        def shared_tensor(pe):
            pe.wait_ge(f2_weights, 16 * 4)
            pe.wait_ge(gru_copied, 4)
            with pe.Fori(0, BATCH) as b:
                for n in range(4):
                    ins = pe.matmul(banks[:, n, :], shared_w[:, n, :], xnT[:, bass.ds(b * SEQ, SEQ)], start=True, stop=True)
                ins.then_inc(sh_up, 1)
                pe.wait_ge(sh_hidden, b + 1)
                for t in range(BT):
                    for c in range(2):
                        ins = pe.matmul(banks[:, 4, t * D:(t + 1) * D], sh_h[:, c, t * P:(t + 1) * P], shared_d[:, c, :],
                                        start=(c == 0), stop=(c == 1))
                ins.then_inc(sh_down, 1)
                pe.wait_ge(sh_added, b + 1)

        def shared_scalar(act):
            act.activation(shared_sig, shared_logit[:, :], ACT.Sigmoid).then_inc(sh_gate_sig, 1)
            with act.Fori(0, BATCH) as b:
                act.wait_ge(sh_up, b + 1)
                act.activation(sh_sig, banks[:, 0:2, :], ACT.Sigmoid).then_inc(sh_sigmoid, 1)

        def shared_vector(dve, step):
            dve.wait_ge(sh_gate_sig, 1)
            with step.loop(BATCH, 1) as b:
                dve.wait_ge(sh_sigmoid, b + 1)
                step(dve.tensor_tensor(sh_h, banks[:, 0:2, :], sh_sig, ALU.mult))
                dve.tensor_tensor(sh_h, banks[:, 2:4, :], sh_h, ALU.mult).then_inc(sh_hidden, 1)
                dve.wait_ge(sh_down, b + 1)
                dve.tensor_tensor(g_out[:, bass.ds(b * BT, BT), :], banks[:, 4, :].rearrange("p (t d) -> p t d", d=D),
                                  bcast(shared_sig[:, bass.ds(b * BT, BT)].unsqueeze(2), (P, BT, D)), ALU.mult)\
                    .then_inc(sh_added, 1)

        def experts2_sync(sp):
            sp.wait_ge(rows_sent[2], 16 * TILES * 2)
            sp.wait_ge(sh_added, BATCH)
            with sp.Fori(0, 6) as i:
                for n in range(2):
                    row = sp.snap((2 * i + n) * 4 * P)
                    sp.wait_ge(f2_turned, 2 * i + n + 1)
                    sp.dma_start(rows4b[:, n, :, :], rows_in[2][bass.ds(row, 4 * P), :].rearrange("(j p) d -> p j d", p=P))\
                        .then_inc(f2_loaded[n], 16)

        def experts2_tensor(pe):
            pe.sem_inc(f2_turned, 2)
            pe.wait_ge(route_slots, 3)
            with pe.Fori(0, 6) as i:
                for n in range(2):
                    g = 2 * i + n
                    experts = [expert_of(pe, 2, 4 * g + j) for j in range(4)]
                    pe.wait_ge(f2_loaded[n], 16 * i + 16)
                    for j in range(4):
                        ins = pe.transpose(banks[:, 4 * n, j * P:(j + 1) * P], rows4b[:, n, j, :], C["ident"])
                    ins.then_inc(f2_turned, 1)
                    pe.wait_ge(f2_rowsT, g + 1)
                    for j in range(4):
                        ins = pe.matmul(banks[:, 4 * n + 1, j * P:(j + 1) * P], rowsTb[:, n, j, :],
                                        wgu_all[:, bass.ds(experts[j], 1), :].rearrange("p a f -> p (a f)"), start=True, stop=True)
                    ins.then_inc(f2_up, 1)
                    pe.wait_ge(f2_hid, g + 1)
                    for j in range(4):
                        ins = pe.transpose(banks[:, 4 * n + 2, j * P:(j + 1) * P], hid2[:, n, j, :], C["ident"])
                    ins.then_inc(f2_hid_turned, 1)
                    pe.wait_ge(f2_hidT, g + 1)
                    for j in range(4):
                        ins = pe.matmul(banks[:, 4 * n + 3, j * P:(j + 1) * P], hidT2[:, n, j, :],
                                        wd_all[:, bass.ds(experts[j], 1), :].rearrange("p a f -> p (a f)"), start=True, stop=True)
                    ins.then_inc(f2_down, 1)
                pe.wait_ge(f2_out, 2 * i + 2)

        def experts2_scalar(act):
            with act.Fori(0, 6) as i:
                for n in range(2):
                    g = 2 * i + n
                    act.wait_ge(f2_turned, g + 3)
                    act.activation(rowsTb[:, n, :, :].rearrange("p j s -> p (j s)"), banks[:, 4 * n, :], ACT.Copy)\
                        .then_inc(f2_rowsT, 1)
                    act.wait_ge(f2_up, g + 1)
                    gu = banks[:, 4 * n + 1, :].rearrange("p (j f) -> p j f", j=4)
                    act.activation(gu_sig[:, n, :, :], gu[:, :, 0:F2], ACT.Sigmoid).then_inc(f2_sig, 1)
                    act.wait_ge(f2_hid_turned, g + 1)
                    act.activation(hidT2[:, n, :, :].rearrange("p j s -> p (j s)"), banks[0:F2, 4 * n + 2, :], ACT.Copy)\
                        .then_inc(f2_hidT, 1)

        def experts2_vector(dve, step):
            step(dve.memset(hid2, 0.0))
            with step.loop(6, 2) as i:
                for n in range(2):
                    g = 2 * i + n
                    gu = banks[:, 4 * n + 1, :].rearrange("p (j f) -> p j f", j=4)
                    dve.wait_ge(f2_sig, g + 1)
                    step(dve.tensor_tensor(hid2[:, n, :, 0:F2], gu[:, :, 0:F2], gu_sig[:, n, :, :], ALU.mult))
                    dve.tensor_tensor(hid2[:, n, :, 0:F2], gu[:, :, F2:2 * F2], hid2[:, n, :, 0:F2], ALU.mult).then_inc(f2_hid, 1)
                    dve.wait_ge(f2_down, g + 1)
                    dve.tensor_copy(out4b[:, n, :, :], banks[:, 4 * n + 3, :].rearrange("p (j d) -> p j d", d=D)).then_inc(f2_out, 1)
                dve.wait_ge(rows_stored[2], 32 * i + 32)

        def experts2_gpsimd(pool):
            with pool.Fori(0, 6) as i:
                for n in range(2):
                    pool.wait_ge(f2_out, 2 * i + n + 1)
                    pool.dma_start(rows_out[2][bass.ds((2 * i + n) * 4 * P, 4 * P), :].rearrange("(j p) d -> p j d", p=P),
                                   out4b[:, n, :, :]).then_inc(rows_stored[2], 16)

        f3w = Region(LATE)
        up3T = f3w("up3T", [P, 8, F // P, D])
        down3 = f3w("down3", [P, 8, F // P, D])
        w3 = f3w("w3", [P, 8, D])
        chosen3 = f3w("chosen3", [P, 2, 8, D])
        f3_weights = sem("f3_weights")
        f3_product = sem("f3_product")
        f3_w3 = sem("f3_w3")
        f3_all = sem("f3_all")
        f3_masked = sem("f3_masked")

        def experts3_tensor(pe):
            pe.wait_ge(f3_weights, 32)
            for e in range(8):
                for c in range(F // P):
                    ins = pe.matmul(banks[:, e // 4, (e % 4) * D:(e % 4 + 1) * D], up3T[:, e, c, :], down3[:, e, c, :],
                                    start=(c == 0), stop=(c == F // P - 1))
            ins.then_inc(f3_product, 1)
            pe.wait_ge(f3_w3, 1)
            for t in range(TILES):
                if t >= 2:
                    pe.wait_ge(f3_masked, t - 1)
                for n in range(2):
                    ins = pe.matmul(banks[:, 2 + 2 * (t % 2) + n, :], xnT[:, t * P:(t + 1) * P], w3[:, 4 * n:4 * n + 4, :],
                                    start=True, stop=True)
                ins.then_inc(f3_all, 1)

        def experts3_scalar(act):
            act.wait_ge(f3_product, 1)
            act.activation(w3.rearrange("p e d -> p (e d)"), banks[:, 0:2, :].rearrange("p n c -> p (n c)"), ACT.Copy).then_inc(f3_w3, 1)

        def experts3_vector(dve):
            chosen = picks[:, 0:TILES * 8].rearrange("p (t e) -> p t e", e=8)
            for t in range(TILES):
                dve.wait_ge(f3_all, t + 1)
                dve.tensor_tensor(chosen3[:, t % 2, :, :],
                                  banks[:, 2 + 2 * (t % 2):4 + 2 * (t % 2), :].rearrange("p n (e d) -> p (n e) d", d=D),
                                  bcast(chosen[:, t, :].unsqueeze(2), (P, 8, D)), ALU.mult).then_inc(f3_masked, 1)
                dve.wait_ge(f3_masked, t + 1)
                ins = dve.tensor_reduce(g_out[:, t, :], chosen3[:, t % 2, :, :].rearrange("p e d -> p d e"), X, ALU.add)
            ins.then_inc(mix_ready, 1)
            dve.wait_ge(mix_ready, 4)

        block = ctx.enter_context(nc.Block())

        @block.sync
        def _(sp):
            sp.dma_start(x[:, :, :], a["L0_attn_X"].rearrange("(t p) d -> p t d", p=P)).then_inc(x_loaded, 16)
            sp.dma_start(const[:, :], a["const"]).then_inc(const_loaded, 16)
            sp.dma_start(w0[:, :, :], a["w0"]).then_inc(l0_weights, 16)
            sp.dma_start(w0vg[:, :, :], a["w0vg"]).then_inc(l0_weights, 16)
            sp.dma_start(w0o[:, :], a["L0_attn_W_O"]).then_inc(l0_weights, 16)
            sp.dma_start(gn_w[:, :], a["L0_attn_gn_weight"].partition_broadcast(P)).then_inc(l0_weights, 16)
            sp.dma_start(gn_b[:, :], a["L0_attn_gn_bias"].partition_broadcast(P)).then_inc(l0_weights, 16)
            for layer in range(4):
                sp.dma_start(router[layer][:, :], a[f"router{layer}"]).then_inc(routers_loaded, 16)
            sp.dma_start(gate_b1[:, :], a["L1_ffn_gate_b"].partition_broadcast(P)).then_inc(routers_loaded, 16)
            sp.wait_ge(zeros_set, 1)
            for layer in range(3):
                rows = rows_in[layer].shape[0]
                sp.dma_start(rows_in[layer].rearrange("(n p r) d -> p n (r d)", p=P, r=4),
                             bcast(zeros[:, :].unsqueeze(1), (P, rows // 512, 512))).then_inc(rows_zeroed, 16)
            experts1_weights(sp)
            experts0_sync(sp)
            attention_sync(sp, 0)
            experts1_sync(sp)
            sp.wait_ge(rows_stored[1], 160)
            sp.dma_start(gru_all, a["gru"]).then_inc(gru_loaded, 16)
            sp.dma_start(wgu_all, a["L2_gu"]).then_inc(f2_weights, 16)
            sp.dma_start(wd_all, a["L2_ffn_Wd"].rearrange("e f d -> f e d")).then_inc(f2_weights, 16)
            sp.dma_start(shared_w, a["L2_shared"]).then_inc(f2_weights, 16)
            sp.dma_start(shared_d, a["L2_ffn_Sd"].rearrange("(c p) d -> p c d", p=P)).then_inc(f2_weights, 16)
            experts2_sync(sp)
            sp.wait_ge(rows_stored[2], 192)
            sp.dma_start(up3T, a["L3_upT"].rearrange("e (c p) d -> p e c d", p=P)).then_inc(f3_weights, 16)
            sp.dma_start(down3, a["L3_ffn_w_down"].rearrange("e (c p) d -> p e c d", p=P)).then_inc(f3_weights, 16)
            attention_sync(sp, 1)
            sp.wait_ge(x_final, 1)
            sp.dma_start(out.rearrange("(t p) d -> p t d", p=P), x[:, :, :]).then_inc(out_stored, 16)
            sp.wait_ge(out_stored, 16)

        @block.gpsimd
        def _(pool):
            step = Steps(pool, pool_step)
            pool.memset(minus_half[:, :], -0.5).then_inc(pool_consts_set, 1)
            pool.memset(ones[:, :], 1.0).then_inc(pool_consts_set, 1)
            pool.memset(zeros[:, :], 0.0).then_inc(zeros_set, 1)
            pool.memset(inv_d[:, :], 1.0 / D).then_inc(pool_consts_set, 1)
            pool.wait_ge(pool_consts_set, 3)
            pool.wait_ge(const_loaded, 16)
            norm_gpsimd(pool, step, 0)
            send_rows(pool, 0)
            pool.wait_ge(xnT_ready, 4)
            retention_gpsimd(pool, step)
            experts0_gpsimd(pool)
            fetch_rows(pool, 0, 8)
            norm_gpsimd(pool, step, 1)
            send_rows(pool, 1)
            attention_gpsimd(pool, 0)
            experts1_gpsimd(pool)
            fetch_rows(pool, 1, 10)
            norm_gpsimd(pool, step, 2)
            send_rows(pool, 2)
            gru_gpsimd(pool, step)
            experts2_gpsimd(pool)
            fetch_rows(pool, 2, 12)
            norm_gpsimd(pool, step, 3)
            attention_gpsimd(pool, 1)

        @block.scalar
        def _(act):
            norm_scalar(act, 0)
            routing_scalar(act, 0)
            retention_scalar(act)
            experts0_scalar(act)
            mix_scalar(act, 0)
            norm_scalar(act, 1)
            routing_scalar(act, 1)
            attention_scalar(act, 0)
            experts1_scalar(act)
            mix_scalar(act, 1)
            norm_scalar(act, 2)
            routing_scalar(act, 2)
            gru_scalar(act)
            shared_scalar(act)
            experts2_scalar(act)
            mix_scalar(act, 2)
            norm_scalar(act, 3)
            attention_scalar(act, 1)
            experts3_scalar(act)
            mix_scalar(act, 3)

        @block.vector
        def _(dve):
            step = Steps(dve, dve_step)
            dve.wait_ge(x_loaded, 16)
            dve.wait_ge(const_loaded, 16)
            dve.wait_ge(pool_consts_set, 3)
            step(dve.tensor_copy(identb[:, :], C["ident"]))
            step(dve.tensor_copy(negb[:, :], C["neg"]))
            norm_vector(dve, step, 0)
            routing_vector(dve, step, 0)
            retention_vector(dve, step)
            experts0_vector(dve)
            mix_vector(dve, step, 0)
            norm_vector(dve, step, 1)
            routing_vector(dve, step, 1)
            attention_vector(dve, step, 0)
            experts1_vector(dve)
            mix_vector(dve, step, 1)
            norm_vector(dve, step, 2)
            routing_vector(dve, step, 2)
            gru_vector(dve, step)
            shared_vector(dve, step)
            experts2_vector(dve, step)
            mix_vector(dve, step, 2)
            norm_vector(dve, step, 3)
            routing_vector(dve, step, 3)
            attention_vector(dve, step, 1)
            experts3_vector(dve)
            mix_vector(dve, step, 3)

        @block.tensor
        def _(pe):
            pe.wait_ge(const_loaded, 16)
            pe.wait_ge(pool_consts_set, 3)
            norm_tensor(pe, 0)
            routing_tensor(pe, 0)
            retention_tensor(pe)
            experts0_tensor(pe)
            norm_tensor(pe, 1)
            routing_tensor(pe, 1)
            attention_tensor(pe, 0)
            experts1_tensor(pe)
            norm_tensor(pe, 2)
            routing_tensor(pe, 2)
            gru_tensor(pe)
            shared_tensor(pe)
            experts2_tensor(pe)
            norm_tensor(pe, 3)
            routing_tensor(pe, 3)
            attention_tensor(pe, 1)
            experts3_tensor(pe)


def laid_out(i):
    def blocks(w):
        full = np.zeros((D, D), w.dtype)
        for h in range(H0):
            full[h * D0:(h + 1) * D0, h * D0:(h + 1) * D0] = w[h]
        return full

    swap = np.arange(D) ^ 1
    q0, k0, v0 = (blocks(i[f"L0_attn_W_{n}"]) for n in "QKV")
    return {
        "const": constants(),
        "L0_attn_X": i["L0_attn_X"].reshape(T, D),
        "w0": np.stack([q0, q0[:, swap], k0, k0[:, swap]], axis=1),
        "w0vg": np.stack([v0, i["L0_attn_W_G"]], axis=1),
        "L0_attn_W_O": i["L0_attn_W_O"],
        "L0_attn_gn_weight": i["L0_attn_gn_weight"],
        "L0_attn_gn_bias": i["L0_attn_gn_bias"],
        "wqkv1": i["L1_attn_in_proj_weight"].reshape(3, D, D).transpose(2, 0, 1),
        "wout1": i["L1_attn_out_proj_weight"].T,
        "qk_bias1": np.zeros((D, 2), np.float32),
        "v_bias1": np.zeros(D, np.float32),
        "out_bias1": np.zeros(D, np.float32),
        "wqkv3": i["L3_attn_attn_W"].reshape(D, H1, 3, D1).transpose(0, 2, 1, 3).reshape(D, 3, D),
        "wout3": i["L3_attn_out_W"],
        "qk_bias3": i["L3_attn_attn_b"].reshape(H1, 3, D1).transpose(1, 0, 2).reshape(3, D)[:2].T,
        "v_bias3": i["L3_attn_attn_b"].reshape(H1, 3, D1).transpose(1, 0, 2).reshape(3, D)[2],
        "out_bias3": i["L3_attn_out_b"],
        "L1_ffn_W1": i["L1_ffn_W1"].reshape(8 * D, F),
        "L1_ffn_b1": i["L1_ffn_b1"].reshape(8 * F),
        "L1_ffn_W2": i["L1_ffn_W2"].reshape(8 * F, D),
        "L1_ffn_b2": i["L1_ffn_b2"].reshape(8 * D),
        "gru": np.concatenate([i["L2_attn_W"].transpose(1, 0, 2), i["L2_attn_ln_gamma"].T[:, :, None],
                               i["L2_attn_ln_beta"].T[:, :, None], i["L2_attn_b"].reshape(3, 2, D).transpose(2, 0, 1)], axis=2),
        "L2_gu": np.concatenate([i["L2_ffn_Wg"], i["L2_ffn_Wu"]], axis=2).transpose(1, 0, 2),
        "L2_ffn_Wd": i["L2_ffn_Wd"],
        "L2_shared": np.concatenate([i["L2_ffn_Sg"], i["L2_ffn_Su"]], axis=1).reshape(D, 4, P),
        "L2_ffn_Sd": i["L2_ffn_Sd"],
        "L3_upT": i["L3_ffn_w_up"].transpose(0, 2, 1),
        "L3_ffn_w_down": i["L3_ffn_w_down"],
        "router0": i["L0_ffn_Wr"],
        "router1": i["L1_ffn_gate_w"],
        "router2": np.concatenate([i["L2_ffn_router_w"].T, i["L2_ffn_shared_gate_w"]], axis=1),
        "router3": i["L3_ffn_gate_w"].T,
        "L1_ffn_gate_b": i["L1_ffn_gate_b"],
        "L0_ffn_W1": i["L0_ffn_W1"].reshape(8 * D, F),
        "L0_ffn_W2": i["L0_ffn_W2"].reshape(8 * F, D),
    }


def kernel(**inputs):
    import concourse.bacc as _bacc
    from concourse.bass_utils import run_bass_kernel_spmd as _run

    nc = _bacc.Bacc("TRN2", target_bir_lowering=False, num_devices=1)
    arrays, args = {}, {}
    for name, value in laid_out({k: np.asarray(v) for k, v in inputs.items()}).items():
        arrays[f"in_{name}"] = np.ascontiguousarray(value)
        args[name] = nc.dram_tensor(f"in_{name}", value.shape, mybir.dt.from_np(value.dtype), kind="ExternalInput").ap()
    out = nc.dram_tensor("out", (T, D), F32, kind="ExternalOutput").ap()
    scratch = {kind: [nc.dram_tensor(f"{kind}{n}", (rows, D), F32).ap()
                      for n, rows in enumerate((8 * CAP + dropped, 40 * P, 48 * P))]
               for kind, dropped in (("rows_in", T), ("rows_out", 0))}
    scratch["parts"] = nc.dram_tensor("parts", (6 * BATCH, P, SEQ), BF16).ap()
    build(nc, args, out, scratch)
    r = _run(nc, [arrays], core_ids=[0])
    return r.results[0]["out"].reshape(BATCH, SEQ, D)
```

```python
from contextlib import ExitStack, contextmanager

import numpy as np

import concourse.bass as bass
from concourse import mybir

P = 128
D = 128
BATCH, SEQ = 4, 512
T = BATCH * SEQ
TILES = T // P
BT = SEQ // P
EPS = 1e-5

F32 = mybir.dt.float32
BF16 = mybir.dt.bfloat16
I32 = mybir.dt.int32
U32 = mybir.dt.uint32
ALU = mybir.AluOpType
ACT = mybir.ActivationFunctionType
X = mybir.AxisListType.X

H0, D0 = 8, 16
H1, D1 = 16, 8
F = 512
CAP = T * 5 // 4 // 8
LATE = 19072
ARENA = LATE + 13 * 1024
PART = CAP // 4

WIDTHS = dict(ident=128, tri=128, neg=128, negT=128, decay=128, cosq=SEQ, sinq=SEQ, cosk=SEQ, sink=SEQ, heads=8,
              rev8=8, rev16=16, start320=8, dump=16, thr=128)
COLS = {}
_at = 0
for _k, _w in WIDTHS.items():
    COLS[_k] = (_at, _at + _w)
    _at += _w
CONST_W = _at


def constants():
    c = np.zeros((P, CONST_W), np.float32)

    def put(name, value):
        c[:, COLS[name][0]:COLS[name][1]] = value

    p = np.arange(P)
    put("ident", np.eye(P))
    put("tri", p[:, None] <= p[None, :])
    put("neg", np.where(p[None, :] > p[:, None], np.float32(-1e30), np.float32(0)))
    put("negT", np.where(p[:, None] > p[None, :], np.float32(-1e30), np.float32(0)))
    gammas = (1.0 - np.exp(np.linspace(np.log(1 / 32), np.log(1 / 512), H0))).astype(np.float32).astype(np.float64)
    head, j = p // D0, p % D0
    put("decay", (head[:, None] == head[None, :]) * (gammas[head] ** P)[:, None])
    pos = np.arange(SEQ)
    scale = ((np.arange(0, D0, 2) + 0.4 * D0) / (1.4 * D0))[j // 2]
    sc = scale[:, None] ** (pos / 512.0)[None, :]
    half = D0 // 2
    inv = (1.0 / np.float32(10000.0) ** (np.arange(half, dtype=np.float32) / np.float32(half))).astype(np.float32)
    angle = (pos[None, :].astype(np.float32) * inv[j // 2][:, None]).astype(np.float64)
    sign = np.where(j % 2 == 0, -1.0, 1.0)[:, None]
    grow = gammas[head][:, None] ** (pos % P)[None, :]
    put("cosq", np.cos(angle) * sc * grow)
    put("sinq", np.sin(angle) * sc * grow * sign)
    put("cosk", np.cos(angle) / sc / grow)
    put("sink", np.sin(angle) / sc / grow * sign)
    put("heads", head[:, None] == np.arange(H0)[None, :])
    put("rev8", 8 - np.arange(8)[None, :])
    put("rev16", 16 - np.arange(16)[None, :])
    put("start320", 320 * np.arange(8)[None, :])
    put("dump", 2560 + np.arange(16)[None, :] * P + p[:, None])
    put("thr", 128 * np.arange(128)[None, :])
    return c


class Steps:

    def __init__(self, eng, sem):
        self.eng, self.sem, self.count, self.turn = eng, sem, 0, 0

    def __call__(self, instruction):
        instruction.then_inc(self.sem, 1)
        self.count += 1
        self.eng.wait_ge(self.sem, self.count + self.turn)

    def loop(self, times, steps):
        return self.loop_from(0, times, steps)

    @contextmanager
    def loop_from(self, start, times, steps):
        first = self.count
        with self.eng.Fori(start, start + times) as i:
            self.turn = (i - start) * steps if start else i * steps
            yield i
        assert self.count == first + steps, self.count - first
        self.count, self.turn = first + times * steps, 0


def bcast(ap, shape):
    return ap.broadcast_to(list(shape))


def build(nc, a, out, scratch):
    ctx = ExitStack()
    with ctx:
        def sb(name, shape, dt=F32):
            return ctx.enter_context(nc.sbuf_tensor(name, shape, dt))

        def sem(name):
            return ctx.enter_context(nc.semaphore(name))

        banks = ctx.enter_context(nc.psum_tensor("banks", [P, 8, 512], F32))

        const = sb("const", [P, CONST_W])
        C = {k: const[:, lo:hi] for k, (lo, hi) in COLS.items()}
        x = sb("x", [P, TILES, D])
        xn = sb("xn", [P, TILES, D])
        xnT = sb("xnT", [P, T])
        s_out = sb("s_out", [P, TILES, D])
        g_out = sb("g_out", [P, TILES, D])
        squares = sb("squares", [P, TILES, D])
        mean = sb("mean", [P, 64])
        var = sb("var", [P, 64])
        rstd = sb("rstd", [P, 64])
        minus_half = sb("minus_half", [P, 64])
        ones = sb("ones", [P, P])

        const_loaded = sem("const_loaded")
        x_loaded = sem("x_loaded")
        out_stored = sem("out_stored")
        x_final = sem("x_final")
        pool_consts_set = sem("pool_consts_set")
        dve_step = sem("dve_step")
        act_step = sem("act_step")
        pool_step = sem("pool_step")

        norm_centered = sem("norm_centered")
        norm_squared = sem("norm_squared")
        norm_var = sem("norm_var")
        norm_rstd = sem("norm_rstd")
        norm_done = sem("norm_done")
        norm_transposed = sem("norm_transposed")
        xnT_ready = sem("xnT_ready")

        def norm_vector(dve, step, layer):
            step(dve.tensor_reduce(mean[:, 0:TILES], x[:, :, :], X, ALU.add))
            step(dve.tensor_scalar(mean[:, 0:TILES], mean[:, 0:TILES], 1.0 / D, None, ALU.mult))
            dve.tensor_tensor(xn[:, :, :], x[:, :, :], bcast(mean[:, 0:TILES].unsqueeze(2), (P, TILES, D)),
                              ALU.subtract).then_inc(norm_centered, 1)
            dve.wait_ge(norm_squared, layer + 1)
            step(dve.tensor_reduce(var[:, 0:TILES], squares[:, :, :], X, ALU.add))
            dve.tensor_scalar(var[:, 0:TILES], var[:, 0:TILES], 1.0 / D, EPS, ALU.mult, ALU.add).then_inc(norm_var, 1)
            dve.wait_ge(norm_rstd, layer + 1)
            dve.tensor_tensor(xn[:, :, :], xn[:, :, :], bcast(rstd[:, 0:TILES].unsqueeze(2), (P, TILES, D)),
                              ALU.mult).then_inc(norm_done, 1)

        def norm_scalar(act, layer):
            act.wait_ge(norm_centered, layer + 1)
            act.activation(squares[:, :, :], xn[:, :, :], ACT.Square).then_inc(norm_squared, 1)
            for k in range(4):
                act.wait_ge(norm_transposed, 4 * layer + k + 1)
                act.activation(xnT[:, k * 512:(k + 1) * 512], banks[:, k, :], ACT.Copy).then_inc(xnT_ready, 1)

        def norm_gpsimd(pool, step, layer):
            pool.wait_ge(norm_var, layer + 1)
            pool.tensor_tensor(rstd[:, 0:TILES], var[:, 0:TILES], minus_half[:, 0:TILES], ALU.pow).then_inc(norm_rstd, 1)

        def norm_tensor(pe, layer):
            pe.wait_ge(norm_done, layer + 1)
            for t in range(TILES):
                ins = pe.transpose(banks[:, t // 4, (t % 4) * P:(t % 4 + 1) * P], xn[:, t, :], C["ident"])
                if t % 4 == 3:
                    ins.then_inc(norm_transposed, 1)

        arena = sb("arena", [P, ARENA])

        class Region:

            def __init__(self, at, end=ARENA):
                self.at, self.end = at, end

            def __call__(self, name, shape, dt=F32):
                n = int(np.prod(shape[1:]))
                words = n if dt != BF16 else (n + 1) // 2
                ap = arena[0:shape[0], self.at:self.at + words]
                self.at += words
                assert self.at <= self.end, (name, self.at, self.end)
                if dt != F32:
                    ap = ap.bitcast(dt)
                if len(shape) > 2:
                    dims = "abcd"[:len(shape) - 1]
                    ap = ap.rearrange(f"p ({' '.join(dims)}) -> p {' '.join(dims)}", **dict(zip(dims, shape[1:])))
                return ap

        l0 = Region(0, LATE)
        w0 = l0("w0", [P, 4, P])
        w0vg = l0("w0vg", [P, 2, P])
        w0o = l0("w0o", [P, P])
        gn_w = l0("gn_w", [P, D])
        gn_b = l0("gn_b", [P, D])
        xb = l0("xb", [P, SEQ])
        qT = l0("qT", [P, SEQ])
        kT = l0("kT", [P, SEQ])
        rot = l0("rot", [P, SEQ])
        yT = rot
        v_tok = l0("v_tok", [P, BT, D])
        v_half = l0("v_half", [P, 2, BT, D])
        gate_sig = l0("gate_sig", [P, BT, D])
        gate = l0("gate", [P, BT, D])
        q_heads_at = l0.at
        q_heads = l0("q_heads", [P, H0, SEQ])
        q_heads_end = l0.at
        attT = l0("attT", [P, 2, H0, P])
        k_tok = l0("k_tok", [P, BT - 1, P])
        state = l0("state", [P, BT - 1, P])
        yc = l0("yc", [P, BT * H0, D0])
        zT = l0("zT", [P, SEQ])
        fetched_at = l0.at

        l0_weights = sem("l0_weights")
        l0_half_zero = sem("l0_half_zero")
        l0_x_copied = sem("l0_x_copied")
        l0_projected = sem("l0_projected")
        l0_v_copied = sem("l0_v_copied")
        l0_sig = sem("l0_sig")
        l0_q_ready = sem("l0_q_ready")
        l0_k_ready = sem("l0_k_ready")
        l0_q_heads = sem("l0_q_heads")
        l0_k_turned = sem("l0_k_turned")
        l0_k_tok = sem("l0_k_tok")
        l0_scores = sem("l0_scores")
        l0_att = sem("l0_att")
        l0_update = sem("l0_update")
        l0_state = sem("l0_state")
        l0_y = sem("l0_y")
        l0_yT = sem("l0_yT")
        l0_y_turned = sem("l0_y_turned")
        l0_centered = sem("l0_centered")
        l0_squared = sem("l0_squared")
        l0_var = sem("l0_var")
        l0_rstd = sem("l0_rstd")
        l0_z = sem("l0_z")
        l0_gate = sem("l0_gate")
        l0_z_turned = sem("l0_z_turned")
        l0_zT = sem("l0_zT")
        l0_s = sem("l0_s")
        l0_s_copied = sem("l0_s_copied")

        def retention_first_tensor(pe):
            pe.wait_ge(l0_weights, 16 * 5)
            pe.wait_ge(l0_half_zero, 1)
            retention_pass_tensor(pe, 0, head=True, tail=False)
            pe.sem_inc(l0_s_copied, 1)

        def retention_rest_tensor(pe):
            with pe.Fori(1, BATCH) as b:
                pe.wait_ge(l0_s_copied, b)
                retention_pass_tensor(pe, b, head=True, tail=True)
            retention_pass_tensor(pe, BATCH, head=False, tail=True)
            pe.wait_ge(l0_s_copied, BATCH + 1)

        def retention_pass_tensor(pe, b, head, tail):
            def scores(c):
                if c >= 2:
                    pe.wait_ge(l0_att, BT * b + c - 1)
                for n in range(2):
                    if c == 0:
                        pe.wait_ge(l0_q_heads, H0 * b + 4 * n + 4)
                    ins = pe.matmul(banks[:, 2 * (c % 2) + n, :], kT[:, c * P:(c + 1) * P],
                                    q_heads[:, 4 * n:4 * n + 4, c * P:(c + 1) * P], start=True, stop=True)
                ins.then_inc(l0_scores, 1)

            def sums(c):
                y = banks[:, 7, c * P:(c + 1) * P]
                if c >= 1:
                    pe.matmul(y, state[:, c - 1, :], qT[:, c * P:(c + 1) * P], start=True, stop=False)
                pe.wait_ge(l0_att, BT * b + c + 1)
                for h in range(H0):
                    pair = slice(32 * (h // 2), 32 * (h // 2) + 32)
                    ins = pe.matmul(y[pair, :], v_half[:, h % 2, c, pair], attT[:, c % 2, h, :],
                                    start=(c == 0 and h % 2 == 0), stop=(h % 2 == 1))
                ins.then_inc(l0_y, 1)

            if head:
                pe.wait_ge(l0_x_copied, b + 1)
                for n in range(4):
                    ins = pe.matmul(banks[:, n, :], w0[:, n, :], xb[:, :], start=True, stop=True)
                ins.then_inc(l0_projected, 1)
                if not tail:
                    pe.wait_ge(route_slots, 1)
                for t in range(BT):
                    ins = pe.matmul(banks[:, 4 + t // 2, (t % 2) * 256:(t % 2 + 1) * 256], xb[:, t * P:(t + 1) * P],
                                    w0vg[:, :, :], start=True, stop=True)
                ins.then_inc(l0_projected, 1)
                pe.wait_ge(l0_k_ready, b + 1)
                for c in range(BT - 1):
                    ins = pe.transpose(banks[:, 7, c * P:(c + 1) * P], kT[:, c * P:(c + 1) * P], C["ident"])
                ins.then_inc(l0_k_turned, 1)
                scores(0)
                scores(1)
                pe.wait_ge(l0_k_tok, b + 1)
                for c in range(BT - 1):
                    ins = pe.matmul(banks[:, 7, c * P:(c + 1) * P], k_tok[:, c, :], v_tok[:, c, :], start=True, stop=True)
                ins.then_inc(l0_update, 1)
                pe.wait_ge(l0_state, b + 1)
                pe.wait_ge(l0_v_copied, b + 1)
                sums(0)
                scores(2)
                sums(1)
                scores(3)
                sums(2)
            if tail:
                pe.wait_ge(l0_z, b)
                if head:
                    pe.wait_ge(l0_gate, b + 1)
                for t in range(BT):
                    ins = pe.transpose(banks[:, 4, t * P:(t + 1) * P],
                                       yc[:, t * H0:(t + 1) * H0, :].rearrange("p h d -> p (h d)"), C["ident"])
                ins.then_inc(l0_z_turned, 1)
            if head:
                sums(3)
            if tail:
                pe.wait_ge(l0_zT, b)
                for t in range(BT):
                    ins = pe.matmul(banks[:, 5, t * P:(t + 1) * P], zT[:, t * P:(t + 1) * P], w0o[:, :],
                                    start=True, stop=True)
                ins.then_inc(l0_s, 1)
            if head:
                pe.wait_ge(l0_yT, b + 1)
                for t in range(BT):
                    ins = pe.transpose(banks[:, 6, t * P:(t + 1) * P], yT[:, t * P:(t + 1) * P], C["ident"])
                ins.then_inc(l0_y_turned, 1)

        HEAD_STEPS, TAIL_STEPS = 8, 6

        def retention_first_vector(dve, step):
            dve.wait_ge(l0_weights, 16 * 5)
            retention_pass_vector(dve, step, 0, head=True, tail=False)

        def retention_rest_vector(dve, step):
            with step.loop_from(1, BATCH - 1, HEAD_STEPS + TAIL_STEPS) as b:
                retention_pass_vector(dve, step, b, head=True, tail=True)
            retention_pass_vector(dve, step, BATCH, head=False, tail=True)
            dve.wait_ge(l0_s_copied, BATCH + 1)

        def retention_pass_vector(dve, step, b, head, tail):
            def mask(c):
                dve.wait_ge(l0_scores, BT * b + c + 1)
                if c >= 2:
                    dve.wait_ge(l0_y, BT * b + c - 1)
                dve.tensor_tensor(attT[:, c % 2, :, :],
                                  banks[:, 2 * (c % 2):2 * (c % 2) + 2, :].rearrange("p n (h s) -> p (n h) s", h=4),
                                  bcast(C["tri"].unsqueeze(1), (P, H0, P)), ALU.mult).then_inc(l0_att, 1)

            if tail:
                dve.wait_ge(l0_y_turned, b)
                y = banks[:, 6, :].rearrange("p (g d) -> p g d", d=D0)
                step(dve.tensor_reduce(mean[:, 0:32], y, X, ALU.add))
                step(dve.tensor_scalar(mean[:, 0:32], mean[:, 0:32], 1.0 / D0, None, ALU.mult))
                dve.tensor_tensor(yc[:, :, :], y, bcast(mean[:, 0:32].unsqueeze(2), (P, 32, D0)), ALU.subtract)\
                    .then_inc(l0_centered, 1)
            if head:
                dve.wait_ge(l0_projected, 2 * b + 1)
                step(dve.tensor_tensor(rot[:, :], banks[:, 0, :], C["cosq"], ALU.mult))
                step(dve.tensor_tensor(qT[:, :], banks[:, 1, :], C["sinq"], ALU.mult))
                dve.tensor_tensor(qT[:, :], qT[:, :], rot[:, :], ALU.add).then_inc(l0_q_ready, 1)
                dve.wait_ge(l0_q_ready, b + 1)
                step(dve.tensor_tensor(rot[:, :], banks[:, 2, :], C["cosk"], ALU.mult))
                step(dve.tensor_tensor(kT[:, :], banks[:, 3, :], C["sink"], ALU.mult))
                dve.tensor_tensor(kT[:, :], kT[:, :], rot[:, :], ALU.add).then_inc(l0_k_ready, 1)
            if tail:
                dve.wait_ge(l0_squared, b)
                step(dve.tensor_reduce(var[:, 0:32], squares[:, 0:4, :].rearrange("p t (h d) -> p (t h) d", d=D0), X, ALU.add))
                dve.tensor_scalar(var[:, 0:32], var[:, 0:32], 1.0 / D0, EPS, ALU.mult, ALU.add).then_inc(l0_var, 1)
            if head:
                mask(0)
                dve.wait_ge(l0_update, b + 1)
                step(dve.tensor_tensor(state[:, 0, :], banks[:, 7, 0:P], C["decay"], ALU.mult))
                for c in range(1, BT - 1):
                    step(dve.tensor_tensor(state[:, c, :], state[:, c - 1, :], banks[:, 7, c * P:(c + 1) * P], ALU.add))
                    ins = dve.tensor_tensor(state[:, c, :], state[:, c, :], C["decay"], ALU.mult)
                    if c < BT - 2:
                        step(ins)
                ins.then_inc(l0_state, 1)
                mask(1)
                mask(2)
            if tail:
                dve.wait_ge(l0_rstd, b)
                step(dve.tensor_tensor(yc[:, :, :], yc[:, :, :], bcast(rstd[:, 0:32].unsqueeze(2), (P, 32, D0)), ALU.mult))
                y4 = yc[:, :, :].rearrange("p (t h) d -> p t h d", t=BT).rearrange("p t h d -> p t (h d)")
                step(dve.tensor_tensor(y4, y4, bcast(gn_w[:, :].unsqueeze(1), (P, BT, D)), ALU.mult))
                step(dve.tensor_tensor(y4, y4, bcast(gn_b[:, :].unsqueeze(1), (P, BT, D)), ALU.add))
                dve.tensor_tensor(y4, y4, gate[:, :, :], ALU.mult).then_inc(l0_z, 1)
            if head:
                if tail:
                    dve.wait_ge(l0_z, b)
                dve.wait_ge(l0_sig, b + 1)
                dve.tensor_tensor(gate[:, :, :],
                                  banks[:, 4:6, :].rearrange("p n (t w e) -> p (n t) w e", t=2, w=2)[:, :, 1, :],
                                  gate_sig[:, :, :], ALU.mult).then_inc(l0_gate, 1)
                mask(3)

        def retention_first_scalar(act):
            act.wait_ge(l0_half_zero, 1)
            act.activation(xb[:, :], xnT[:, 0:SEQ], ACT.Copy).then_inc(l0_x_copied, 1)
            retention_pass_scalar(act, 0, head=True, tail=False)

        def retention_rest_scalar(act):
            with act.Fori(1, BATCH) as b:
                act.activation(xb[:, :], xnT[:, bass.ds(b * SEQ, SEQ)], ACT.Copy).then_inc(l0_x_copied, 1)
                retention_pass_scalar(act, b, head=True, tail=True)
            retention_pass_scalar(act, BATCH, head=False, tail=True)

        def retention_pass_scalar(act, b, head, tail):
            if tail:
                act.wait_ge(l0_centered, b)
                act.activation(squares[:, 0:4, :], yc[:, :, :].rearrange("p (t h) d -> p t (h d)", t=BT), ACT.Square)\
                    .then_inc(l0_squared, 1)
            if head:
                act.wait_ge(l0_q_ready, b + 1)
                for h in range(H0):
                    act.activation(q_heads[:, h, :], qT[:, :], ACT.Copy, scale=C["heads"][:, h:h + 1]).then_inc(l0_q_heads, 1)
                act.wait_ge(l0_k_turned, b + 1)
                act.activation(k_tok[:, :, :], banks[:, 7, 0:(BT - 1) * P].rearrange("p (c e) -> p c e", e=P), ACT.Copy)
                act.wait_ge(l0_projected, 2 * b + 2)
                vg = banks[:, 4:6, :].rearrange("p n (t w e) -> p (n t) w e", t=2, w=2)
                act.activation(v_tok[:, :, :], vg[:, :, 0, :], ACT.Copy).then_inc(l0_k_tok, 1)
                for n in range(2):
                    ins = act.activation(v_half[:, n, :, :].rearrange("p t (j w e) -> p t j w e", w=2, e=D0)[:, :, :, n, :],
                                   vg[:, :, 0, :].rearrange("p t (j w e) -> p t j w e", w=2, e=D0)[:, :, :, n, :], ACT.Copy)
                ins.then_inc(l0_v_copied, 1)
                act.activation(gate_sig[:, :, :], vg[:, :, 1, :], ACT.Sigmoid).then_inc(l0_sig, 1)
            if tail:
                act.wait_ge(l0_z_turned, b)
                act.activation(zT[:, :], banks[:, 4, :], ACT.Copy).then_inc(l0_zT, 1)
            if head:
                act.wait_ge(l0_y, BT * b + BT)
                act.activation(yT[:, :], banks[:, 7, :], ACT.Copy).then_inc(l0_yT, 1)
            if tail:
                act.wait_ge(l0_s, b)
                tiles = slice((b - 1) * BT, b * BT) if isinstance(b, int) else bass.ds((b - 1) * BT, BT)
                act.activation(s_out[:, tiles, :], banks[:, 5, :].rearrange("p (t d) -> p t d", d=D), ACT.Copy)\
                    .then_inc(l0_s_copied, 1)

        def retention_gpsimd(pool):
            fetches = fetch_rows(pool, 0, 8)
            for b in range(BATCH):
                pool.wait_ge(l0_var, b + 1)
                pool.tensor_tensor(rstd[:, 0:32], var[:, 0:32], minus_half[:, 0:32], ALU.pow).then_inc(l0_rstd, 1)
                for _ in range((6, 5, 5, 0)[b]):
                    next(fetches)

        shared_logit = sb("shared_logit", [P, TILES])

        logits = sb("logits", [P, TILES, 16])
        second = sb("second", [P, TILES, 16])
        pick1 = sb("pick1", [P, TILES, 16])
        pick2 = sb("pick2", [P, TILES, 16])
        picks = sb("picks", [P, TILES * 16])
        match = sb("match", [P, TILES, 16])
        top = sb("top", [P, 8, TILES])
        totals = sb("totals", [P, 16 * TILES])
        prefix = sb("prefix", [P, 16 * TILES])
        place = sb("place", [P, TILES, 16])
        count = sb("count", [P, 4, 16])
        count_int = sb("count_int", [P, 16], I32)
        slots = sb("slots", [P, 3, TILES], I32)
        weights = sb("weights", [P, 2, TILES])
        tile_cmp = sb("tile_cmp", [P, 48 * 16])
        tile_sum = sb("tile_sum", [P, 48])
        tile_expert = sb("tile_expert", [P, 2, 48], I32)
        router = {0: sb("router0", [P, 8]), 1: sb("router1", [P, 8]), 2: sb("router2", [P, 17]), 3: sb("router3", [P, 8])}
        gate_b1 = sb("gate_b1", [P, 8])
        EXPERTS = {0: 8, 1: 8, 2: 16, 3: 8}
        FFN_TILES = {1: 40, 2: 48}

        routers_loaded = sem("routers_loaded")
        route_logits = sem("route_logits")
        route_gap = sem("route_gap")
        route_exp = sem("route_exp")
        route_picked = sem("route_picked")
        route_counted = sem("route_counted")
        route_slots = sem("route_slots")

        def routing_tensor(pe, layer):
            e = EXPERTS[layer]
            w = e + (layer == 2)
            if layer == 0:
                pe.wait_ge(routers_loaded, 16 * 5)
            pe.wait_ge(xnT_ready, 4 * layer + 4)
            for t in range(TILES):
                ins = pe.matmul(banks[:, 4, t * w:(t + 1) * w], xnT[:, t * P:(t + 1) * P], router[layer][:, 0:w],
                                start=True, stop=True)
            ins.then_inc(route_logits, 1)
            if layer < 3:
                pe.wait_ge(route_picked, layer + 1)
                pe.matmul(banks[:, 5, 0:TILES * e], C["tri"], picks[:, 0:TILES * e], start=True, stop=True)
                pe.matmul(banks[:, 6, 0:TILES * e], ones[:, :], picks[:, 0:TILES * e], start=True, stop=True)\
                    .then_inc(route_counted, 1)

        def routing_scalar(act, layer):
            e = EXPERTS[layer]
            act.wait_ge(route_gap, layer + 1)
            if layer == 0:
                act.activation(match[:, :, 0:e], match[:, :, 0:e], ACT.Exp).then_inc(route_exp, 1)
            else:
                act.activation(top[:, 2, :], top[:, 2, :], ACT.Exp).then_inc(route_exp, 1)

        def routing_vector(dve, step, layer):
            e = EXPERTS[layer]
            w = e + (layer == 2)
            shape = (P, TILES, e)
            lg, lg2, p1, p2, mt, pl = (v[:, :, 0:e] for v in (logits, second, pick1, pick2, match, place))
            rev = C["rev8" if e == 8 else "rev16"]
            rev3 = bcast(rev.unsqueeze(1), shape)

            def wide(v):
                return bcast(v.unsqueeze(2), shape)

            def pick(values, largest, chosen):
                step(dve.tensor_reduce(largest, values, X, ALU.max))
                step(dve.tensor_tensor(mt, values, wide(largest), ALU.is_equal))
                step(dve.tensor_tensor(mt, mt, rev3, ALU.mult))
                step(dve.tensor_reduce(top[:, 7, :], mt, X, ALU.max))
                step(dve.tensor_tensor(chosen, rev3, wide(top[:, 7, :]), ALU.is_equal))

            dve.wait_ge(route_logits, layer + 1)
            raw = banks[:, 4, 0:TILES * w].rearrange("p (t e) -> p t e", e=w)
            if layer == 1:
                step(dve.tensor_tensor(lg, raw[:, :, 0:e], bcast(gate_b1[:, :].unsqueeze(1), shape), ALU.add))
            else:
                step(dve.tensor_copy(lg, raw[:, :, 0:e]))
            if layer == 2:
                step(dve.tensor_copy(shared_logit[:, :], raw[:, :, e]))
            pick(lg, top[:, 0, :], p1)
            all_picks = picks[:, 0:TILES * e].rearrange("p (t e) -> p t e", e=e)
            if layer == 0:
                dve.tensor_copy(all_picks, p1).then_inc(route_picked, 1)
                dve.tensor_tensor(mt, lg, wide(top[:, 0, :]), ALU.subtract).then_inc(route_gap, 1)
            else:
                step(dve.scalar_tensor_tensor(lg2, p1, -1e30, lg, ALU.mult, ALU.add))
                pick(lg2, top[:, 1, :], p2)
                dve.tensor_tensor(all_picks, p1, p2, ALU.add).then_inc(route_picked, 1)
                if layer < 3:
                    dve.tensor_tensor(top[:, 2, :], top[:, 1, :], top[:, 0, :], ALU.subtract).then_inc(route_gap, 1)
                else:
                    return
            dve.wait_ge(route_exp, layer + 1)
            if layer == 0:
                step(dve.tensor_reduce(top[:, 3, :], mt, X, ALU.add))
                step(dve.reciprocal(top[:, 4, :], top[:, 3, :]))
            else:
                step(dve.tensor_scalar(top[:, 3, :], top[:, 2, :], 1.0, None, ALU.add))
                step(dve.reciprocal(weights[:, 0, :], top[:, 3, :]))
                step(dve.tensor_tensor(weights[:, 1, :], top[:, 2, :], weights[:, 0, :], ALU.mult))
            dve.wait_ge(route_counted, layer + 1)
            et = (P, e, TILES)
            tot = totals[:, 0:e * TILES]
            pre = prefix[:, 0:e * TILES]
            tot3, pre3 = (v.rearrange("p (e t) -> p e t", e=e) for v in (tot, pre))
            step(dve.tensor_copy(tot3, banks[:, 6, 0:TILES * e].rearrange("p (t e) -> p e t", e=e)))
            step(dve.tensor_tensor_scan(pre, bcast(ones[:, 0:1], (P, e * TILES)), tot, 0.0, ALU.mult, ALU.add))
            step(dve.tensor_tensor(pre, pre, tot, ALU.subtract))
            running = banks[:, 5, 0:TILES * e].rearrange("p (t e) -> p t e", e=e)
            start = count[:, 0, 0:e]
            if layer == 0:
                step(dve.tensor_copy(start, pre3[:, :, 0]))
                step(dve.tensor_tensor(pre3, pre3, bcast(start.unsqueeze(2), et), ALU.subtract))
                step(dve.tensor_tensor(pl, running, pre3.rearrange("p e t -> p t e"), ALU.add))
                step(dve.tensor_tensor(pl, pl, p1, ALU.mult))
                step(dve.tensor_reduce(top[:, 2, :], pl, X, ALU.add))
                step(dve.tensor_tensor(pl, p1, bcast(C["start320"].unsqueeze(1), shape), ALU.mult))
                step(dve.tensor_reduce(top[:, 3, :], pl, X, ALU.add))
                step(dve.tensor_scalar(top[:, 5, :], top[:, 2, :], float(CAP), None, ALU.is_le))
                step(dve.tensor_tensor(weights[:, 0, :], top[:, 4, :], top[:, 5, :], ALU.mult))
                step(dve.tensor_scalar(weights[:, 1, :], top[:, 5, :], -1.0, 1.0, ALU.mult, ALU.add))
                step(dve.scalar_tensor_tensor(top[:, 3, :], top[:, 2, :], -1.0, top[:, 3, :], ALU.add, ALU.add))
                step(dve.tensor_tensor(top[:, 2, :], top[:, 3, :], C["dump"], ALU.subtract))
                step(dve.tensor_tensor(top[:, 2, :], top[:, 2, :], top[:, 5, :], ALU.mult))
                step(dve.tensor_tensor(top[:, 2, :], top[:, 2, :], C["dump"], ALU.add))
                step(dve.tensor_scalar(top[:, 3, :], top[:, 3, :], float(8 * CAP - 1), None, ALU.min))
                step(dve.tensor_copy(slots[:, 2, :], top[:, 3, :]))
                dve.tensor_copy(slots[:, 0, :], top[:, 2, :]).then_inc(route_slots, 1)
            else:
                end, padded, shift = (count[:, n, 0:e] for n in (1, 2, 3))
                step(dve.tensor_copy(start, pre3[:, :, 0]))
                step(dve.tensor_tensor(end, pre3[:, :, TILES - 1], tot3[:, :, TILES - 1], ALU.add))
                step(dve.tensor_tensor(padded, end, start, ALU.subtract))
                step(dve.tensor_scalar(padded, padded, float(P - 1), None, ALU.add))
                step(dve.tensor_copy(count_int[:, 0:e], padded))
                step(dve.tensor_scalar(count_int[:, 0:e], count_int[:, 0:e], 7, None, ALU.arith_shift_right))
                step(dve.tensor_scalar(count_int[:, 0:e], count_int[:, 0:e], 7, None, ALU.logical_shift_left))
                step(dve.tensor_copy(padded, count_int[:, 0:e]))
                step(dve.tensor_tensor_scan(end, bcast(ones[:, 0:1], (P, e)), padded, 0.0, ALU.mult, ALU.add))
                step(dve.tensor_tensor(shift, end, padded, ALU.subtract))
                step(dve.tensor_tensor(shift, shift, start, ALU.subtract))
                step(dve.tensor_tensor(pre3, pre3, bcast(shift.unsqueeze(2), et), ALU.add))
                step(dve.tensor_tensor(pl, running, pre3.rearrange("p e t -> p t e"), ALU.add))
                for n, chosen in enumerate((p1, p2)):
                    step(dve.tensor_tensor(mt, pl, chosen, ALU.mult))
                    step(dve.tensor_reduce(top[:, 5, :], mt, X, ALU.add))
                    step(dve.tensor_scalar(slots[:, n, :], top[:, 5, :], -1.0, None, ALU.add))
                n_tiles = FFN_TILES[layer]
                cmp3 = tile_cmp[:, 0:n_tiles * e].rearrange("p (j e) -> p j e", e=e)
                step(dve.tensor_tensor(cmp3, bcast(end.unsqueeze(1), (P, n_tiles, e)),
                                       bcast(C["thr"][:, 0:n_tiles].unsqueeze(2), (P, n_tiles, e)), ALU.is_le))
                step(dve.tensor_reduce(tile_sum[:, 0:n_tiles], cmp3, X, ALU.add))
                step(dve.tensor_scalar(tile_sum[:, 0:n_tiles], tile_sum[:, 0:n_tiles], float(e - 1), None, ALU.min))
                dve.tensor_copy(tile_expert[:, layer - 1, 0:n_tiles], tile_sum[:, 0:n_tiles]).then_inc(route_slots, 1)

        fetched = {0: Region(fetched_at, LATE)("fetched0", [P, 1, TILES, D])}
        fetched[1] = fetched[2] = Region(ARENA - 2 * TILES * D)("fetched", [P, 2, TILES, D])
        rows_in, rows_out = scratch["rows_in"], scratch["rows_out"]
        zeros = sb("zeros", [P, 512])
        zerosb = zeros[:, 0:64].bitcast(BF16)
        zeros_set = sem("zeros_set")
        rows_zeroed = sem("rows_zeroed")
        rows_sent = [sem(f"rows_sent{n}") for n in range(3)]
        rows_back = [sem(f"rows_back{n}") for n in range(3)]
        rows_stored = [sem(f"rows_stored{n}") for n in range(3)]

        def send_rows(pool, layer):
            pool.wait_ge(route_slots, layer + 1)
            pool.wait_ge(rows_zeroed, 16 * 3)
            for k in range(1 if layer == 0 else 2):
                for t in range(TILES):
                    pool.indirect_dma_start(
                        out=rows_in[layer], out_offset=bass.IndirectOffsetOnAxis(ap=slots[:, k, t:t + 1].bitcast(U32), axis=0),
                        in_=xn[:, t, :], in_offset=None).then_inc(rows_sent[layer], 16)

        def fetch_rows(pool, layer, stores):
            pool.wait_ge(rows_stored[layer], 16 * stores)
            for k in range(1 if layer == 0 else 2):
                for t in range(TILES):
                    n = 2 if layer == 0 else k
                    pool.indirect_dma_start(
                        out=fetched[layer][:, k, t, :], out_offset=None,
                        in_=rows_out[layer], in_offset=bass.IndirectOffsetOnAxis(ap=slots[:, n, t:t + 1].bitcast(U32), axis=0))\
                        .then_inc(rows_back[layer], 16)
                    yield

        w1_buf = l0("w1_buf", [P, 2, F])
        w2_buf = l0("w2_buf", [P, 2, F // P, D])
        f0 = Region(q_heads_at, q_heads_end)
        x80 = f0("x80", [PART, 2, 4, D])
        x80T = f0("x80T", [P, 2, CAP])
        hT0 = f0("hT0", [P, F // P, CAP])
        y80 = f0("y80", [PART, 2, 4, D])
        f0_loaded = [sem(f"f0_loaded{n}") for n in range(2)]
        f0_turned = sem("f0_turned")
        f0_xT = sem("f0_xT")
        f0_up = sem("f0_up")
        f0_hidden = sem("f0_hidden")
        f0_down = [sem(f"f0_down{n}") for n in range(2)]
        f0_copied = sem("f0_copied")

        def experts0_sync(sp):
            sp.wait_ge(rows_sent[0], 16 * TILES)
            sp.wait_ge(l0_scores, BT)
            with sp.Fori(0, 4) as i:
                for n in range(2):
                    e = sp.snap(2 * i + n)
                    at = sp.snap(e * D)
                    sp.wait_ge(f0_down[n], i + 1)
                    sp.dma_start(w1_buf[:, n, :], a["L0_ffn_W1"][bass.ds(at, D), :]).then_inc(f0_loaded[n], 16)
                    sp.dma_start(w2_buf[:, n, :, :], a["L0_ffn_W2"][bass.ds(e * F, F), :].rearrange("(c p) d -> p c d", p=P))\
                        .then_inc(f0_loaded[n], 16)
                    sp.dma_start(x80[:, n, :, :], rows_in[0][bass.ds(e * CAP, CAP), :].rearrange("(j p) d -> p j d", p=PART))\
                        .then_inc(f0_loaded[n], 16)

        def experts0_tensor(pe):
            for n in range(2):
                pe.sem_inc(f0_down[n], 1)
            with pe.Fori(0, 4) as i:
                for n in range(2):
                    pe.wait_ge(f0_loaded[n], 48 * i + 48)
                    for j in range(4):
                        ins = pe.transpose(banks[:, 4, j * PART:(j + 1) * PART], x80[:, n, j, :], C["ident"][0:PART, 0:PART])
                    ins.then_inc(f0_turned, 1)
                    pe.wait_ge(f0_xT, 2 * i + n + 1)
                    for c in range(F // P):
                        pe.matmul(banks[:, c, 0:CAP], w1_buf[:, n, c * P:(c + 1) * P], x80T[:, n, :], start=True, stop=True)\
                            .then_inc(f0_up, 1)
                    pe.wait_ge(f0_hidden, 4 * (2 * i + n) + 4)
                    for j in range(4):
                        for c in range(F // P):
                            ins = pe.matmul(banks[0:PART, 5, j * D:(j + 1) * D], hT0[:, c, j * PART:(j + 1) * PART],
                                            w2_buf[:, n, c, :], start=(c == 0), stop=(c == F // P - 1))
                    ins.then_inc(f0_down[n], 1)
                    pe.wait_ge(f0_copied, 2 * i + n + 1)

        def experts0_scalar(act):
            with act.Fori(0, 4) as i:
                for n in range(2):
                    act.wait_ge(f0_turned, 2 * i + n + 1)
                    act.activation(x80T[:, n, :], banks[:, 4, 0:CAP], ACT.Copy).then_inc(f0_xT, 1)
                    for c in range(0, F // P):
                        act.wait_ge(f0_up, 4 * (2 * i + n) + c + 1)
                        act.activation(hT0[:, c, :], banks[:, c, 0:CAP], ACT.Relu).then_inc(f0_hidden, 1)

        def experts0_vector(dve):
            with dve.Fori(0, 4) as i:
                for n in range(2):
                    dve.wait_ge(f0_down[n], i + 2)
                    dve.tensor_copy(y80[:, n, :, :], banks[0:PART, 5, :].rearrange("p (j d) -> p j d", d=D))\
                        .then_inc(f0_copied, 1)
                dve.wait_ge(rows_stored[0], 32 * i + 32)

        def experts0_gpsimd(pool):
            with pool.Fori(0, 4) as i:
                for n in range(2):
                    pool.wait_ge(f0_copied, 2 * i + n + 1)
                    pool.dma_start(rows_out[0][bass.ds((2 * i + n) * CAP, CAP), :].rearrange("(j p) d -> p j d", p=PART),
                                   y80[:, n, :, :]).then_inc(rows_stored[0], 16)

        mix_ready = sem("mix_ready")
        mix_sigmoid = sem("mix_sigmoid")

        def mix_vector(dve, step, layer):
            def wide(v):
                return bcast(v.unsqueeze(2), (P, TILES, D))
            if layer < 3:
                dve.wait_ge(rows_back[layer], 16 * TILES * (1 if layer == 0 else 2))
                rows = fetched[layer]
                w = [wide(weights[:, n, :]) for n in range(2)]
                step(dve.tensor_tensor(rows[:, 0, :, :], rows[:, 0, :, :], w[0], ALU.mult))
                if layer == 2:
                    step(dve.tensor_tensor(rows[:, 0, :, :], rows[:, 0, :, :], g_out[:, :, :], ALU.add))
                other = xn[:, :, :] if layer == 0 else rows[:, 1, :, :]
                step(dve.tensor_tensor(g_out[:, :, :], other, w[1], ALU.mult))
                dve.tensor_tensor(g_out[:, :, :], g_out[:, :, :], rows[:, 0, :, :], ALU.add).then_inc(mix_ready, 1)
                dve.wait_ge(mix_ready, layer + 1)
            step(dve.tensor_tensor(s_out[:, :, :], s_out[:, :, :], g_out[:, :, :], ALU.mult))
            dve.wait_ge(mix_sigmoid, layer + 1)
            step(dve.tensor_tensor(s_out[:, :, :], s_out[:, :, :], squares[:, :, :], ALU.mult))
            ins = dve.tensor_tensor(x[:, :, :], x[:, :, :], s_out[:, :, :], ALU.add)
            if layer < 3:
                step(ins)
            else:
                ins.then_inc(x_final, 1)

        def mix_scalar(act, layer):
            act.wait_ge(mix_ready, layer + 1)
            act.activation(squares[:, :, :], g_out[:, :, :], ACT.Sigmoid).then_inc(mix_sigmoid, 1)


        at = Region(0, LATE)
        stack_q = at("stack_q", [P, H1, SEQ], BF16)
        stack_k = at("stack_k", [P, H1, SEQ], BF16)
        wqkv = at("wqkv", [P, 3, P])
        wout = at("wout", [P, P])
        qk_bias = at("qk_bias", [P, 2])
        v_bias = at("v_bias", [P, P])
        out_bias = at("out_bias", [P, P])
        v_all = at("v_all", [P, TILES, D])
        v_now = at("v_now", [P, 4, BT, 4, D1 + 1])
        neg_max = at("neg_max", [P, 2, BT, 4])
        max_parts = at("max_parts", [4, 3, SEQ], BF16)
        max_rest = at("max_rest", [4, SEQ])
        o_T = at("o_T", [P, SEQ])
        o_rec = at("o_rec", [P, BT, 4])
        oT = at("oT", [P, SEQ])
        loop_a = Region(at.at, LATE)
        prob_at = at.at
        prob = at("prob", [P, 4, 1280])
        xb1 = loop_a("xb1", [P, SEQ])
        qk = loop_a("qk", [P, 2, SEQ])
        parts = loop_a("parts", [P, 3, 2, SEQ], BF16)
        o_tok = squares
        identb = sb("identb", [P, P], BF16)
        negb = sb("negb", [P, 4, P], BF16)
        negTb = sb("negTb", [P, 2, P], BF16)
        q_rows, k_rows = scratch["q_rows"], scratch["k_rows"]
        Q_PARTS, K_PARTS = (0, 1, 0, 1, 0, 2), (0, 0, 1, 1, 2, 0)
        ROWS = len(Q_PARTS) * D1
        SHIFT = 3

        at_weights = sem("at_weights")
        at_x_copied = sem("at_x_copied")
        at_projected = sem("at_projected")
        at_biased = sem("at_biased")
        at_parts = sem("at_parts")
        at_zero_rows = sem("at_zero_rows")
        at_rows_stored = sem("at_rows_stored")
        at_stacks_set = sem("at_stacks_set")
        at_loaded = [sem(f"at_loaded{n}") for n in range(4)]
        at_filled = sem("at_filled")
        at_read = sem("at_read")
        at_own = sem("at_own")
        at_max_parts = sem("at_max_parts")
        at_max_moved = sem("at_max_moved")
        at_scores = sem("at_scores")
        at_exp = sem("at_exp")
        at_values = sem("at_values")
        at_v_now = sem("at_v_now")
        at_oT_copied = sem("at_oT_copied")
        at_o_turned = sem("at_o_turned")
        at_oT = sem("at_oT")
        at_s = sem("at_s")
        at_s_copied = sem("at_s_copied")

        GROUPS = 16
        FILLS = [(0, 0, 4), (1, 0, 2), (1, 2, 2)] + [(qt, h, 1) for qt in (2, 3) for h in range(4)]
        NF = len(FILLS)

        def fills_before(t):
            return NF * min(t, GROUPS) + min(max(t - 1, 0), GROUPS) + min(max(t - 3, 0), GROUPS)

        class Step:

            def __init__(self, t, turn, run):
                self.t, self.turn, self.run = t, turn, run
                self.has = {"A": t < GROUPS, "M": 1 <= t <= GROUPS, "B": 2 <= t <= GROUPS + 1, "O": 3 <= t}
                self.fill = fills_before(t)

            def count(self, of_run, rate):
                known = of_run + rate * GROUPS * self.run
                return known if self.turn is None else known + self.turn * (4 * rate)

            def next_fill(self):
                self.fill += 1
                return self.fill - 1

        def all_steps(eng, run):
            for t in range(3):
                yield Step(t, None, run)
            with eng.Fori(0, 3) as i:
                for t in range(3, 7):
                    yield Step(t, i, run)
            for t in range(15, GROUPS + 3):
                yield Step(t, None, run)

        def project_sync(sp, run):
            layer = 2 * run + 1
            sp.wait_ge(norm_done, layer + 1)
            sp.dma_start(wqkv, a[f"wqkv{layer}"]).then_inc(at_weights, 16)
            sp.dma_start(wout, a[f"wout{layer}"]).then_inc(at_weights, 16)
            sp.dma_start(qk_bias, a[f"qk_bias{layer}"]).then_inc(at_weights, 16)
            sp.dma_start(v_bias, a[f"v_bias{layer}"].partition_broadcast(P)).then_inc(at_weights, 16)
            sp.dma_start(out_bias, a[f"out_bias{layer}"].partition_broadcast(P)).then_inc(at_weights, 16)
            B0 = BATCH * run
            with sp.Fori(B0, B0 + BATCH) as b:
                row = sp.snap(b - B0)
                sp.wait_ge(at_parts, b + 1)
                for w, (which, rows) in enumerate(((Q_PARTS, q_rows), (K_PARTS, k_rows))):
                    for r, part in enumerate(which):
                        sp.dma_start(rows[bass.ds(row, 1), r * D1:(r + 1) * D1, :, :].rearrange("o i h s -> (o h) i s"),
                                     parts[:, part, w, :]).then_inc(at_rows_stored, 16)
            sp.wait_ge(at_rows_stored, 16 * 12 * (B0 + BATCH))

        def stack_loader(sp):
            def load(slot, batch):
                heads = slice(4 * slot, 4 * slot + 4)
                at_b = bass.ds(batch, 1) if not isinstance(batch, int) else slice(batch, batch + 1)
                sp.dma_start(stack_q[0:ROWS + SHIFT, heads, :], q_rows[at_b, :, heads, :].rearrange("o r h s -> (o r) h s"))\
                    .then_inc(at_loaded[slot], 16)
                sp.dma_start(stack_k[0:ROWS, heads, :], k_rows[at_b, :, heads, :].rearrange("o r h s -> (o r) h s"))\
                    .then_inc(at_loaded[slot], 16)
            return load

        def first_stacks_sync(sp, run):
            load = stack_loader(sp)
            sp.wait_ge(at_stacks_set, 2 * run + 2)
            for slot in range(4):
                load(slot, 0)

        def attend_sync(sp, run):
            load = stack_loader(sp)
            for st in all_steps(sp, run):
                t = st.t
                if st.turn is not None and t + 1 >= 4:
                    batch = sp.snap(st.turn + (t + 1) // 4)
                if st.has["M"]:
                    heads = slice(4 * ((t - 1) % 4), 4 * ((t - 1) % 4) + 4)
                    sp.wait_ge(at_max_parts, st.count(t, 1))
                    for n in range(SHIFT):
                        sp.dma_start(stack_q[ROWS + n:ROWS + n + 1, heads, :].rearrange("o h s -> o (h s)"),
                                     max_parts[:, n, :]).then_inc(at_max_moved, 16)
                if 4 <= t + 1 < GROUPS:
                    sp.wait_ge(at_exp, st.count(6 * (t - 2), 6))
                    load((t + 1) % 4, batch if st.turn is not None else (t + 1) // 4)

        def values_of(pool, batch, slot):
            pool.tensor_copy(v_now[:, slot, :, :, 0:D1],
                             v_all[:, bass.ds(batch * BT, BT), 4 * slot * D1:(4 * slot + 4) * D1]
                             .rearrange("p t (h e) -> p t h e", e=D1)).then_inc(at_v_now, 1)

        def project_gpsimd(pool, run):
            B0 = BATCH * run
            pool.memset(stack_q, 0.0).then_inc(at_stacks_set, 1)
            pool.memset(stack_k, 1.0).then_inc(at_stacks_set, 1)

            pool.wait_ge(at_biased, B0 + BATCH)
            for slot in range(4):
                values_of(pool, 0, slot)

        def attend_gpsimd(pool, run):
            with pool.Fori(1, BATCH) as b:
                for slot in range(4):
                    pool.wait_ge(at_values, 16 * (b - 1) + 4 * slot + 4 + 64 * run)
                    values_of(pool, b, slot)

        def project_tensor(pe, run):
            B0 = BATCH * run
            pe.wait_ge(at_weights, 80 * (run + 1))
            with pe.Fori(B0, B0 + BATCH) as b:
                pe.wait_ge(at_x_copied, b + 1)
                for n in range(2):
                    pe.matmul(banks[:, n, :], wqkv[:, n, :], xb1, start=True, stop=True)
                for t in range(BT):
                    ins = pe.matmul(banks[:, 2, t * P:(t + 1) * P], xb1[:, t * P:(t + 1) * P], wqkv[:, 2, :],
                                    start=True, stop=True)
                ins.then_inc(at_projected, 1)
                pe.wait_ge(at_biased, b + 1)

        def attend_tensor(pe, run):
            B0 = BATCH * run

            def fill_bank(st):
                n = st.next_fill()
                if n >= 2:
                    pe.wait_ge(at_read, st.count(n - 1, NF + 2))
                return n % 2

            def stage_a(st, which):
                slot = st.t % 4
                for qt, first, heads in FILLS[which]:
                    bank, length = fill_bank(st), (qt + 1) * P
                    if qt == 0:
                        pe.wait_ge(at_loaded[slot], 32 * (st.t // 4 + 1 + 4 * run) + (0 if st.turn is None else st.turn * 32))
                    for g in range(heads):
                        h = 4 * slot + first + g
                        pe.matmul(banks[:, bank, g * length:(g + 1) * length], stack_q[:, h, qt * P:(qt + 1) * P],
                                  stack_k[:, h, 0:length], start=(g == 0), stop=False)
                    diagonal = banks[:, bank, 0:heads * length].rearrange("p (g l) -> p g l", g=heads)[:, :, length - P:length]
                    pe.matmul(diagonal, identb[:, :], negb[:, 0:heads, :], start=False, stop=True).then_inc(at_filled, 1)

            def stage_m(st):
                bank = fill_bank(st)
                pe.wait_ge(at_read, st.count(st.fill - 1, NF + 2))
                for qt in range(BT):
                    ins = pe.transpose(banks[0:4, bank, qt * P:(qt + 1) * P], neg_max[:, (st.t - 1) % 2, qt, :], C["ident"])
                ins.then_inc(at_filled, 1)

            def scores_b(st, e):
                h = 4 * ((st.t - 2) % 4) + e
                if e == 0:
                    pe.wait_ge(at_max_moved, st.count(48 * (st.t - 1), 48))
                if st.t > 2 or e >= 2 or run:
                    pe.wait_ge(at_exp, st.count(6 * (st.t - 2) + (e - 5, e - 5, e - 1, e - 1)[e], 6))
                x1, x2 = 2 + 2 * (e % 2), 3 + 2 * (e % 2)

                def keys(kt, bank, col, start):
                    pe.matmul(banks[:, bank, col:col + SEQ - kt * P], stack_k[:, h, kt * P:(kt + 1) * P],
                              stack_q[:, h, kt * P:SEQ], start=start, stop=False)

                keys(0, x1, 0, True)
                pe.matmul(banks[:, x1, 0:P], identb[:, :], negTb[:, 0, :], start=False, stop=True)
                keys(1, x2, 0, True)
                keys(3, x2, 384, False)
                pe.matmul(banks[:, x2, :].rearrange("p (a c) -> p a c", c=P)[:, 0:4:3, :], identb[:, :], negTb[:, :, :],
                          start=False, stop=True).then_inc(at_scores, 1)

            def scores_c(st, pair):
                if st.t > 2 or pair or run:
                    pe.wait_ge(at_exp, st.count(6 * (st.t - 2) + 3 * pair, 6))
                for e in range(2):
                    h = 4 * ((st.t - 2) % 4) + 2 * pair + e
                    pe.matmul(banks[:, 6, e * 256:(e + 1) * 256], stack_k[:, h, 2 * P:3 * P], stack_q[:, h, 2 * P:SEQ],
                              start=(e == 0), stop=False)
                pe.matmul(banks[:, 6, :].rearrange("p (a c) -> p a c", c=P)[:, 0:4:2, :], identb[:, :], negTb[:, :, :],
                          start=False, stop=True).then_inc(at_scores, 1)

            def values(st, e):
                slot = (st.t - 2) % 4
                pe.wait_ge(at_exp, st.count(6 * (st.t - 2) + 3 * (e // 2) + 3, 6))
                if e == 0:
                    pe.wait_ge(at_v_now, st.count(st.t - 1, 1))
                    if st.t > 2 or run:
                        pe.wait_ge(at_oT_copied, st.count(st.t - 2, 1))
                for kt, col in ((0, 0), (1, 512), (2, 1024), (3, 896)):
                    ins = pe.matmul(banks[32 * e:32 * e + D1 + 1, 7, kt * P:SEQ], v_now[:, slot, kt, e, :],
                                    prob[:, e, col:col + SEQ - kt * P], start=(kt == 0), stop=(kt == 3))
                ins.then_inc(at_values, 1)

            def stage_o(st):
                bank = fill_bank(st)
                pe.wait_ge(at_oT_copied, st.count(st.t - 2, 1))
                for qt in range(BT):
                    ins = pe.transpose(banks[:, bank, qt * P:(qt + 1) * P], o_T[:, qt * P:(qt + 1) * P], C["ident"])
                ins.then_inc(at_filled, 1)

            for st in all_steps(pe, run):
                A, M, B, O = (st.has[k] for k in "AMBO")
                if M:
                    stage_m(st)
                if B:
                    scores_b(st, 0)
                    scores_b(st, 1)
                    scores_c(st, 0)
                if A:
                    stage_a(st, slice(0, 4))
                if O:
                    stage_o(st)
                if B:
                    scores_b(st, 2)
                    values(st, 0)
                    scores_b(st, 3)
                    scores_c(st, 1)
                    values(st, 1)
                if A:
                    stage_a(st, slice(4, 8))
                if B:
                    values(st, 2)
                if A:
                    stage_a(st, slice(8, NF))
                if B:
                    values(st, 3)
            for b in range(BATCH):
                if b == 0:
                    pe.wait_ge(at_read, (NF + 2) * GROUPS * (run + 1))
                else:
                    pe.wait_ge(at_oT, B0 + b)
                for t in range(BT):
                    ins = pe.transpose(banks[:, 2, t * P:(t + 1) * P], o_tok[:, BT * b + t, :], C["ident"])
                ins.then_inc(at_o_turned, 1)
                pe.wait_ge(at_oT, B0 + b + 1)
                if b >= 1:
                    pe.wait_ge(at_s_copied, B0 + b)
                for t in range(BT):
                    ins = pe.matmul(banks[:, 3, t * P:(t + 1) * P], oT[:, t * P:(t + 1) * P], wout, start=True, stop=True)
                ins.then_inc(at_s, 1)
            pe.wait_ge(at_s_copied, B0 + BATCH)

        def project_vector(dve, step, run):
            B0 = BATCH * run
            dve.wait_ge(at_weights, 80 * (run + 1))
            step(dve.memset(v_now, 1.0))
            step(dve.memset(banks[:, 7, :], 0.0))
            with step.loop_from(B0, BATCH, 4) as b:
                dve.wait_ge(at_projected, b + 1)
                dve.tensor_scalar(qk[:, 0, :], banks[:, 0, :], qk_bias[:, 0:1], float(D1) ** -0.5, ALU.add, ALU.mult)
                dve.tensor_scalar(qk[:, 1, :], banks[:, 1, :], qk_bias[:, 1:2], None, ALU.add)
                dve.tensor_tensor(v_all[:, bass.ds((b - B0) * BT, BT), :], banks[:, 2, :].rearrange("p (t d) -> p t d", d=D),
                                  bcast(v_bias.unsqueeze(1), (P, BT, D)), ALU.add).then_inc(at_biased, 1)
                dve.wait_ge(at_biased, b + 1)
                step(dve.tensor_copy(parts[:, 0, :, :], qk))
                step(dve.tensor_tensor(qk, qk, parts[:, 0, :, :], ALU.subtract))
                step(dve.tensor_copy(parts[:, 1, :, :], qk))
                step(dve.tensor_tensor(qk, qk, parts[:, 1, :, :], ALU.subtract))
                dve.tensor_copy(parts[:, 2, :, :], qk).then_inc(at_parts, 1)
                dve.wait_ge(at_rows_stored, 16 * 12 * b + 16 * 12)

        def attend_vector(dve, run):
            B0 = BATCH * run

            def filled(st):
                n = st.next_fill()
                dve.wait_ge(at_filled, st.count(n + 1, NF + 2))
                return n % 2

            def stage_a(st, which):
                for qt, first, heads in FILLS[which]:
                    bank, length = filled(st), (qt + 1) * P
                    dve.tensor_reduce(neg_max[:, st.t % 2, qt, first:first + heads],
                                      banks[:, bank, 0:heads * length].rearrange("p (g l) -> p g l", g=heads),
                                      X, ALU.max, negate=True).then_inc(at_read, 1)

            def stage_m(st, own):
                bank = filled(st)
                if st.t > 1 or run:
                    dve.wait_ge(at_max_moved, st.count(48 * (st.t - 1), 48))
                row = banks[0:4, bank, :]
                own(dve.tensor_copy(max_parts[:, 0, :], row))
                dve.tensor_tensor(max_rest, row, max_parts[:, 0, :], ALU.subtract).then_inc(at_read, 1)
                dve.wait_ge(at_read, st.count(st.fill, NF + 2))
                own(dve.tensor_copy(max_parts[:, 1, :], max_rest))
                own(dve.tensor_tensor(max_rest, max_rest, max_parts[:, 1, :], ALU.subtract))
                dve.tensor_copy(max_parts[:, 2, :], max_rest).then_inc(at_max_parts, 1)

            def stage_o(st, own):
                bank, t = filled(st), st.t - 3
                dve.wait_ge(at_read, st.count(st.fill - 1, NF + 2))
                o = banks[:, bank, :].rearrange("p (t h r) -> p t h r", t=BT, h=4)
                own(dve.reciprocal(o_rec, o[:, :, :, D1]))
                tiles = slice(BT * (t // 4), BT * (t // 4) + BT) if st.turn is None else bass.ds(BT * (t // 4 + st.turn), BT)
                dve.tensor_tensor(o_tok[:, tiles, 4 * (t % 4) * D1:(4 * (t % 4) + 4) * D1].rearrange("p t (h e) -> p t h e", e=D1),
                                  o[:, :, :, 0:D1], bcast(o_rec.unsqueeze(3), (P, BT, 4, D1)), ALU.mult).then_inc(at_read, 1)

            OWN = 4
            def before(t):
                return 3 * min(max(t - 1, 0), GROUPS) + min(max(t - 3, 0), GROUPS)

            for st in all_steps(dve, run):
                made = [before(st.t)]

                def own(ins):
                    ins.then_inc(at_own, 1)
                    made[0] += 1
                    dve.wait_ge(at_own, st.count(made[0], OWN))

                if st.has["M"]:
                    stage_m(st, own)
                if st.has["A"]:
                    stage_a(st, slice(0, 4))
                if st.has["O"]:
                    stage_o(st, own)
                if st.has["A"]:
                    stage_a(st, slice(4, NF))
            dve.wait_ge(at_read, (NF + 2) * GROUPS * (run + 1))
            for b in range(BATCH):
                dve.wait_ge(at_s, B0 + b + 1)
                dve.tensor_tensor(s_out[:, b * BT:(b + 1) * BT, :], banks[:, 3, :].rearrange("p (t d) -> p t d", d=D),
                                  bcast(out_bias.unsqueeze(1), (P, BT, D)), ALU.add).then_inc(at_s_copied, 1)

        def project_scalar(act, run):
            B0 = BATCH * run
            act.wait_ge(xnT_ready, 8 * run + 8)
            with act.Fori(B0, B0 + BATCH) as b:
                act.activation(xb1, xnT[:, bass.ds((b - B0) * SEQ, SEQ)], ACT.Copy).then_inc(at_x_copied, 1)
                act.wait_ge(at_projected, b + 1)

        def attend_scalar(act, run):
            B0 = BATCH * run
            for st in all_steps(act, run):
                if not st.has["B"]:
                    continue
                for pair in range(2):
                    for e in range(2):
                        act.wait_ge(at_scores, st.count(6 * (st.t - 2) + 3 * pair + e + 1, 6))
                        if st.t > 2 or run:
                            act.wait_ge(at_values, st.count(4 * (st.t - 3) + 2 * pair + e + 1, 4))
                        act.activation(prob[:, 2 * pair + e, 0:1024], banks[:, 2 + 2 * e:4 + 2 * e, :].rearrange("p a c -> p (a c)"),
                                       ACT.Exp).then_inc(at_exp, 1)
                    act.wait_ge(at_scores, st.count(6 * (st.t - 2) + 3 * pair + 3, 6))
                    act.activation(prob[:, 2 * pair:2 * pair + 2, 1024:1280], banks[:, 6, :].rearrange("p (e c) -> p e c", e=2),
                                   ACT.Exp).then_inc(at_exp, 1)
                act.wait_ge(at_values, st.count(4 * (st.t - 2) + 4, 4))
                if st.has["O"]:
                    act.wait_ge(at_filled, st.count(fills_before(st.t) + st.has["M"] + 4 * st.has["A"] + 1, NF + 2))
                act.activation(o_T, banks[:, 7, :], ACT.Copy).then_inc(at_oT_copied, 1)
            for b in range(BATCH):
                act.wait_ge(at_o_turned, B0 + b + 1)
                if b >= 1:
                    act.wait_ge(at_s, B0 + b)
                act.activation(oT, banks[:, 2, :], ACT.Copy).then_inc(at_oT, 1)

        f1w = Region(LATE)
        w1_all = f1w("w1_all", [P, 8, F])
        w2_all = f1w("w2_all", [P, 8, F // P, D])
        b1_all = f1w("b1_all", [P, 8, F])
        b2_all = f1w("b2_all", [P, 8, D])
        f1 = Region(prob_at, LATE)
        rows4 = f1("rows4", [P, 2, 4, D])
        rowsT = f1("rowsT", [P, 2, 4, P])
        hid = f1("hid", [P, 2, F])
        hidT = f1("hidT", [P, 2, F])
        out4 = f1("out4", [P, 2, 4, D])
        f1_weights = sem("f1_weights")
        f1_loaded = [sem(f"f1_loaded{n}") for n in range(2)]
        f1_turned = sem("f1_turned")
        f1_rowsT = sem("f1_rowsT")
        f1_up = sem("f1_up")
        f1_hid = sem("f1_hid")
        f1_hid_turned = sem("f1_hid_turned")
        f1_hidT = sem("f1_hidT")
        f1_down = sem("f1_down")
        f1_out = sem("f1_out")

        def experts1_weights(sp):
            sp.dma_start(w1_all, a["L1_ffn_W1"].rearrange("(e p) f -> p e f", p=P)).then_inc(f1_weights, 16)
            sp.dma_start(w2_all, a["L1_ffn_W2"].rearrange("(e c p) d -> p e c d", e=8, p=P)).then_inc(f1_weights, 16)
            sp.dma_start(b1_all.rearrange("p e f -> p (e f)"), a["L1_ffn_b1"].partition_broadcast(P)).then_inc(f1_weights, 16)
            sp.dma_start(b2_all.rearrange("p e d -> p (e d)"), a["L1_ffn_b2"].partition_broadcast(P)).then_inc(f1_weights, 16)

        def experts1_sync(sp):
            sp.wait_ge(rows_sent[1], 16 * TILES * 2)
            with sp.Fori(0, 5) as i:
                for n in range(2):
                    row = sp.snap((2 * i + n) * 4 * P)
                    sp.wait_ge(f1_turned, 2 * i + n + 1)
                    sp.dma_start(rows4[:, n, :, :], rows_in[1][bass.ds(row, 4 * P), :].rearrange("(j p) d -> p j d", p=P))\
                        .then_inc(f1_loaded[n], 16)

        def expert_of(eng, layer, tile):
            return eng.value_load(tile_expert[0:1, layer - 1, bass.ds(tile, 1)], min_val=0, max_val=EXPERTS[layer] - 1)

        def experts1_tensor(pe):
            pe.sem_inc(f1_turned, 2)
            pe.wait_ge(f1_weights, 64)
            pe.wait_ge(route_slots, 2)
            with pe.Fori(0, 5) as i:
                for n in range(2):
                    g = 2 * i + n
                    experts = [expert_of(pe, 1, 4 * g + j) for j in range(4)]
                    pe.wait_ge(f1_loaded[n], 16 * i + 16)
                    for j in range(4):
                        ins = pe.transpose(banks[:, 0, j * P:(j + 1) * P], rows4[:, n, j, :], C["ident"])
                    ins.then_inc(f1_turned, 1)
                    pe.wait_ge(f1_rowsT, g + 1)

                    def up(j):
                        if j >= 2:
                            pe.wait_ge(f1_hid, 4 * g + j - 1)
                        pe.matmul(banks[:, 1 + j % 2, :], rowsT[:, n, j, :],
                                  w1_all[:, bass.ds(experts[j], 1), :].rearrange("p a f -> p (a f)"), start=True, stop=True)\
                            .then_inc(f1_up, 1)

                    def turn(j):
                        pe.wait_ge(f1_hid, 4 * g + j + 1)
                        if j >= 2:
                            pe.wait_ge(f1_hidT, 4 * g + j - 1)
                        for c in range(F // P):
                            ins = pe.transpose(banks[:, 3 + j % 2, c * P:(c + 1) * P], hid[:, j % 2, c * P:(c + 1) * P], C["ident"])
                        ins.then_inc(f1_hid_turned, 1)

                    def down(j):
                        pe.wait_ge(f1_hidT, 4 * g + j + 1)
                        for c in range(F // P):
                            ins = pe.matmul(banks[:, 5, j * D:(j + 1) * D], hidT[:, j % 2, c * P:(c + 1) * P],
                                            w2_all[:, bass.ds(experts[j], 1), c, :].rearrange("p a d -> p (a d)"),
                                            start=(c == 0), stop=(c == F // P - 1))
                        ins.then_inc(f1_down, 1)

                    up(0)
                    for j in range(4):
                        if j + 1 < 4:
                            up(j + 1)
                        turn(j)
                        if j >= 1:
                            down(j - 1)
                    down(3)
                    pe.wait_ge(f1_out, 4 * g + 4)

        def experts1_vector(dve):
            with dve.Fori(0, 5) as i:
                for n in range(2):
                    g = 2 * i + n
                    experts = [expert_of(dve, 1, 4 * g + j) for j in range(4)]
                    for j in range(4):
                        dve.wait_ge(f1_up, 4 * g + j + 1)
                        dve.tensor_tensor(hid[:, j % 2, :], banks[:, 1 + j % 2, :],
                                          b1_all[:, bass.ds(experts[j], 1), :].rearrange("p a f -> p (a f)"), ALU.add)\
                            .then_inc(f1_hid, 1)
                        if j == 3:
                            dve.wait_ge(f1_down, 4 * g + 4)
                            for m in range(4):
                                dve.tensor_tensor(out4[:, n, m, :], banks[:, 5, m * D:(m + 1) * D],
                                                  b2_all[:, bass.ds(experts[m], 1), :].rearrange("p a d -> p (a d)"), ALU.add)\
                                    .then_inc(f1_out, 1)
                dve.wait_ge(rows_stored[1], 32 * i + 32)

        def experts1_scalar(act):
            with act.Fori(0, 5) as i:
                for n in range(2):
                    g = 2 * i + n
                    act.wait_ge(f1_turned, g + 3)
                    act.activation(rowsT[:, n, :, :].rearrange("p j s -> p (j s)"), banks[:, 0, :], ACT.Copy)\
                        .then_inc(f1_rowsT, 1)
                    for j in range(4):
                        act.wait_ge(f1_hid_turned, 4 * g + j + 1)
                        act.activation(hidT[:, j % 2, :], banks[:, 3 + j % 2, :], ACT.Relu).then_inc(f1_hidT, 1)

        def experts1_gpsimd(pool):
            with pool.Fori(0, 5) as i:
                for n in range(2):
                    pool.wait_ge(f1_out, 4 * (2 * i + n) + 4)
                    pool.dma_start(rows_out[1][bass.ds((2 * i + n) * 4 * P, 4 * P), :].rearrange("(j p) d -> p j d", p=P),
                                   out4[:, n, :, :]).then_inc(rows_stored[1], 16)


        gr = Region(0, LATE)
        gru_in = gr("gru_in", [P, BATCH, SEQ])
        centred = gr("centred", [P, BATCH, SEQ])
        spread = gr("spread", [P, BATCH, SEQ])
        z_gate = gr("z_gate", [P, BATCH, SEQ])
        keep_gate = gr("keep_gate", [P, BATCH, SEQ])
        hid_sig = gr("hid_sig", [P, BATCH, SEQ])
        cand = gr("cand", [P, BATCH, SEQ])
        gru_w = gr("gru_w", [P, 2, P])
        gru_p = gr("gru_p", [P, 5])
        gru_vars = gr("gru_vars", [P, BATCH, BT])
        gru_rstds = gr("gru_rstds", [P, BATCH, BT])
        gru_all = Region(LATE)("gru_all", [P, 3, 2 * P + 4])
        inv_d = sb("inv_d", [P, P])

        gru_loaded = sem("gru_loaded")
        gru_begun = sem("gru_begun")
        gru_set = sem("gru_set")
        gru_mean = sem("gru_mean")
        gru_centred = sem("gru_centred")
        gru_squared = sem("gru_squared")
        gru_var = sem("gru_var")
        gru_spread = sem("gru_spread")
        gru_var_eps = sem("gru_var_eps")
        gru_rstd = sem("gru_rstd")
        gru_normed = sem("gru_normed")
        gru_affine = sem("gru_affine")
        gru_gates = sem("gru_gates")
        gru_sig = sem("gru_sig")
        gru_cand = sem("gru_cand")
        gru_out = sem("gru_out")
        gru_turned = sem("gru_turned")
        gru_copied = sem("gru_copied")

        def gru_tensor(pe):
            with pe.Fori(0, 3) as l:
                pe.wait_ge(gru_set, l + 1)
                for b in range(BATCH):
                    pe.wait_ge(gru_out, BATCH * l + b + 1)
                    pe.matmul(banks[:, b, :], inv_d[:, :], gru_in[:, b, :], start=True, stop=True).then_inc(gru_mean, 1)
                for b in range(BATCH):
                    pe.wait_ge(gru_squared, BATCH * l + b + 1)
                    for t in range(BT):
                        ins = pe.matmul(banks[:, 4 + b, t:t + 1], spread[:, b, t * P:(t + 1) * P], inv_d[:, 0:1],
                                        start=True, stop=True)
                    ins.then_inc(gru_var, 1)
                for b in range(BATCH):
                    pe.wait_ge(gru_rstd, BATCH * l + b + 1)
                    for t in range(BT):
                        ins = pe.matmul(banks[:, 4 + b, t * P:(t + 1) * P], bcast(gru_rstds[:, b, t:t + 1], (P, P)), C["ident"],
                                        start=True, stop=True)
                    ins.then_inc(gru_spread, 1)
                for b in range(BATCH):
                    pe.wait_ge(gru_affine, BATCH * l + b + 1)
                    pe.matmul(banks[:, b, :], gru_w[:, 0, :], centred[:, b, :], start=True, stop=True)
                    pe.matmul(banks[:, 4 + b, :], gru_w[:, 1, :], centred[:, b, :], start=True, stop=True).then_inc(gru_gates, 1)
            pe.wait_ge(gru_out, 4 * BATCH)
            for t in range(TILES):
                ins = pe.transpose(banks[:, t // 4, (t % 4) * P:(t % 4 + 1) * P], gru_in[:, t // BT, (t % BT) * P:(t % BT + 1) * P],
                                   C["ident"])
                if t % 4 == 3:
                    ins.then_inc(gru_turned, 1)

        def gru_vector(dve, step):
            dve.wait_ge(xnT_ready, 12)
            for b in range(BATCH):
                dve.tensor_copy(gru_in[:, b, :], xnT[:, b * SEQ:(b + 1) * SEQ]).then_inc(gru_out, 1)
            dve.wait_ge(gru_out, BATCH)
            with step.loop(3, 3 * BATCH) as l:
                for b in range(BATCH):
                    dve.wait_ge(gru_mean, BATCH * l + b + 1)
                    dve.tensor_tensor(centred[:, b, :], gru_in[:, b, :], banks[:, b, :], ALU.subtract).then_inc(gru_centred, 1)
                for b in range(BATCH):
                    dve.wait_ge(gru_var, BATCH * l + b + 1)
                    dve.tensor_scalar(gru_vars[:, b, :], banks[:, 4 + b, 0:BT], EPS, None, ALU.add).then_inc(gru_var_eps, 1)
                for b in range(BATCH):
                    dve.wait_ge(gru_spread, BATCH * l + b + 1)
                    dve.tensor_tensor(centred[:, b, :], centred[:, b, :], banks[:, 4 + b, :], ALU.mult).then_inc(gru_normed, 1)
                for b in range(BATCH):
                    dve.wait_ge(gru_sig, BATCH * l + b + 1)
                    step(dve.tensor_scalar(cand[:, b, :], banks[:, 4 + b, :], gru_p[:, 3:4], 0.0, ALU.add, ALU.max))
                    dve.scalar_tensor_tensor(cand[:, b, :], hid_sig[:, b, :], 0.5, cand[:, b, :], ALU.min, ALU.add)\
                        .then_inc(gru_cand, 1)
                for b in range(BATCH):
                    dve.wait_ge(gru_cand, BATCH * l + b + 1)
                    step(dve.tensor_tensor(cand[:, b, :], cand[:, b, :], z_gate[:, b, :], ALU.mult))
                    step(dve.tensor_tensor_scan(hid_sig[:, b, :], keep_gate[:, b, :], cand[:, b, :], 0.5, ALU.mult, ALU.add))
                    dve.tensor_tensor(gru_in[:, b, :], gru_in[:, b, :], hid_sig[:, b, :], ALU.add).then_inc(gru_out, 1)
            for k in range(4):
                dve.wait_ge(gru_turned, k + 1)
                dve.tensor_copy(s_out[:, 4 * k:4 * k + 4, :], banks[:, k, :].rearrange("p (t d) -> p t d", d=D))\
                    .then_inc(gru_copied, 1)

        def gru_scalar(act):
            with act.Fori(0, 3) as l:
                for b in range(BATCH):
                    act.wait_ge(gru_centred, BATCH * l + b + 1)
                    act.activation(spread[:, b, :], centred[:, b, :], ACT.Square).then_inc(gru_squared, 1)
                for b in range(BATCH):
                    act.wait_ge(gru_normed, BATCH * l + b + 1)
                    act.activation(centred[:, b, :], centred[:, b, :], ACT.Identity, bias=gru_p[:, 1:2], scale=gru_p[:, 0:1])\
                        .then_inc(gru_affine, 1)
                for b in range(BATCH):
                    act.wait_ge(gru_gates, BATCH * l + b + 1)
                    act.activation(z_gate[:, b, :], banks[:, b, :], ACT.Sigmoid, bias=gru_p[:, 2:3])
                    act.activation(keep_gate[:, b, :], banks[:, b, :], ACT.Sigmoid, bias=gru_p[:, 4:5], scale=-1.0)
                    act.activation(hid_sig[:, b, :], banks[:, 4 + b, :], ACT.Sigmoid, bias=gru_p[:, 3:4]).then_inc(gru_sig, 1)

        def gru_gpsimd(pool, step):
            pool.wait_ge(gru_loaded, 16)
            fetches = fetch_rows(pool, 2, 12)
            for l in range(3):
                pool.wait_ge(gru_out, BATCH * l + BATCH)
                step(pool.tensor_copy(gru_w.rearrange("p a e -> p (a e)"), gru_all[:, l, 0:2 * P]))
                step(pool.tensor_copy(gru_p[:, 0:4], gru_all[:, l, 2 * P:2 * P + 4]))
                pool.tensor_tensor(gru_p[:, 4:5], zeros[:, 0:1], gru_p[:, 2:3], ALU.subtract).then_inc(gru_set, 1)
                for b in range(BATCH):
                    pool.wait_ge(gru_var_eps, BATCH * l + b + 1)
                    pool.tensor_tensor(gru_rstds[:, b, :], gru_vars[:, b, :], minus_half[:, 0:BT], ALU.pow)\
                        .then_inc(gru_rstd, 1)
                for _ in range(11 if l < 2 else 10):
                    next(fetches)

        E2, F2 = 16, 64
        f2w = Region(LATE + 3 * (2 * P + 4))
        wgu_all = f2w("wgu_all", [P, E2, 2 * F2])
        wd_all = f2w("wd_all", [F2, E2, D])
        shared_w = f2w("shared_w", [P, 4, P])
        shared_d = f2w("shared_d", [P, 2, D])
        shared_sig = f2w("shared_sig", [P, TILES])
        f2 = Region(0, LATE)
        sh_sig = f2("sh_sig", [P, 2, SEQ])
        sh_h = f2("sh_h", [P, 2, SEQ])
        rows4b = f2("rows4b", [P, 2, 4, D])
        rowsTb = f2("rowsTb", [P, 2, 4, P])
        gu_sig = f2("gu_sig", [P, 2, 4, F2])
        hid2 = f2("hid2", [P, 2, 4, 2 * F2])
        hidT2 = f2("hidT2", [F2, 2, 4, P])
        out4b = f2("out4b", [P, 2, 4, D])
        f2_weights = sem("f2_weights")
        sh_gate_sig = sem("sh_gate_sig")
        sh_up = sem("sh_up")
        sh_sigmoid = sem("sh_sigmoid")
        sh_hidden = sem("sh_hidden")
        sh_down = sem("sh_down")
        sh_added = sem("sh_added")
        f2_loaded = [sem(f"f2_loaded{n}") for n in range(2)]
        f2_turned = sem("f2_turned")
        f2_rowsT = sem("f2_rowsT")
        f2_up = sem("f2_up")
        f2_sig = sem("f2_sig")
        f2_hid = sem("f2_hid")
        f2_hid_turned = sem("f2_hid_turned")
        f2_hidT = sem("f2_hidT")
        f2_down = sem("f2_down")
        f2_out = sem("f2_out")

        def shared_tensor(pe):
            pe.wait_ge(f2_weights, 16 * 4)
            with pe.Fori(0, BATCH) as b:
                for n in range(4):
                    ins = pe.matmul(banks[:, n, :], shared_w[:, n, :], xnT[:, bass.ds(b * SEQ, SEQ)], start=True, stop=True)
                ins.then_inc(sh_up, 1)
                pe.wait_ge(sh_hidden, b + 1)
                for t in range(BT):
                    for c in range(2):
                        ins = pe.matmul(banks[:, 4, t * D:(t + 1) * D], sh_h[:, c, t * P:(t + 1) * P], shared_d[:, c, :],
                                        start=(c == 0), stop=(c == 1))
                ins.then_inc(sh_down, 1)
                pe.wait_ge(sh_added, b + 1)

        def shared_scalar(act):
            act.activation(shared_sig, shared_logit[:, :], ACT.Sigmoid).then_inc(sh_gate_sig, 1)
            with act.Fori(0, BATCH) as b:
                act.wait_ge(sh_up, b + 1)
                act.activation(sh_sig, banks[:, 0:2, :], ACT.Sigmoid).then_inc(sh_sigmoid, 1)

        def shared_vector(dve, step):
            dve.wait_ge(sh_gate_sig, 1)
            with step.loop(BATCH, 1) as b:
                dve.wait_ge(sh_sigmoid, b + 1)
                step(dve.tensor_tensor(sh_h, banks[:, 0:2, :], sh_sig, ALU.mult))
                dve.tensor_tensor(sh_h, banks[:, 2:4, :], sh_h, ALU.mult).then_inc(sh_hidden, 1)
                dve.wait_ge(sh_down, b + 1)
                dve.tensor_tensor(g_out[:, bass.ds(b * BT, BT), :], banks[:, 4, :].rearrange("p (t d) -> p t d", d=D),
                                  bcast(shared_sig[:, bass.ds(b * BT, BT)].unsqueeze(2), (P, BT, D)), ALU.mult)\
                    .then_inc(sh_added, 1)

        def experts2_sync(sp):
            sp.wait_ge(rows_sent[2], 16 * TILES * 2)
            sp.wait_ge(sh_added, BATCH)
            with sp.Fori(0, 6) as i:
                for n in range(2):
                    row = sp.snap((2 * i + n) * 4 * P)
                    sp.wait_ge(f2_turned, 2 * i + n + 1)
                    sp.dma_start(rows4b[:, n, :, :], rows_in[2][bass.ds(row, 4 * P), :].rearrange("(j p) d -> p j d", p=P))\
                        .then_inc(f2_loaded[n], 16)

        def experts2_tensor(pe):
            pe.sem_inc(f2_turned, 2)
            pe.wait_ge(route_slots, 3)
            with pe.Fori(0, 6) as i:
                for n in range(2):
                    g = 2 * i + n
                    experts = [expert_of(pe, 2, 4 * g + j) for j in range(4)]
                    pe.wait_ge(f2_loaded[n], 16 * i + 16)
                    for j in range(4):
                        ins = pe.transpose(banks[:, 4 * n, j * P:(j + 1) * P], rows4b[:, n, j, :], C["ident"])
                    ins.then_inc(f2_turned, 1)
                    pe.wait_ge(f2_rowsT, g + 1)
                    for j in range(4):
                        ins = pe.matmul(banks[:, 4 * n + 1, j * P:(j + 1) * P], rowsTb[:, n, j, :],
                                        wgu_all[:, bass.ds(experts[j], 1), :].rearrange("p a f -> p (a f)"), start=True, stop=True)
                    ins.then_inc(f2_up, 1)
                    pe.wait_ge(f2_hid, g + 1)
                    for j in range(4):
                        ins = pe.transpose(banks[:, 4 * n + 2, j * P:(j + 1) * P], hid2[:, n, j, :], C["ident"])
                    ins.then_inc(f2_hid_turned, 1)
                    pe.wait_ge(f2_hidT, g + 1)
                    for j in range(4):
                        ins = pe.matmul(banks[:, 4 * n + 3, j * P:(j + 1) * P], hidT2[:, n, j, :],
                                        wd_all[:, bass.ds(experts[j], 1), :].rearrange("p a f -> p (a f)"), start=True, stop=True)
                    ins.then_inc(f2_down, 1)
                pe.wait_ge(f2_out, 2 * i + 2)

        def experts2_scalar(act):
            with act.Fori(0, 6) as i:
                for n in range(2):
                    g = 2 * i + n
                    act.wait_ge(f2_turned, g + 3)
                    act.activation(rowsTb[:, n, :, :].rearrange("p j s -> p (j s)"), banks[:, 4 * n, :], ACT.Copy)\
                        .then_inc(f2_rowsT, 1)
                    act.wait_ge(f2_up, g + 1)
                    gu = banks[:, 4 * n + 1, :].rearrange("p (j f) -> p j f", j=4)
                    act.activation(gu_sig[:, n, :, :], gu[:, :, 0:F2], ACT.Sigmoid).then_inc(f2_sig, 1)
                    act.wait_ge(f2_hid_turned, g + 1)
                    act.activation(hidT2[:, n, :, :].rearrange("p j s -> p (j s)"), banks[0:F2, 4 * n + 2, :], ACT.Copy)\
                        .then_inc(f2_hidT, 1)

        def experts2_vector(dve, step):
            step(dve.memset(hid2, 0.0))
            with step.loop(6, 2) as i:
                for n in range(2):
                    g = 2 * i + n
                    gu = banks[:, 4 * n + 1, :].rearrange("p (j f) -> p j f", j=4)
                    dve.wait_ge(f2_sig, g + 1)
                    step(dve.tensor_tensor(hid2[:, n, :, 0:F2], gu[:, :, 0:F2], gu_sig[:, n, :, :], ALU.mult))
                    dve.tensor_tensor(hid2[:, n, :, 0:F2], gu[:, :, F2:2 * F2], hid2[:, n, :, 0:F2], ALU.mult).then_inc(f2_hid, 1)
                    dve.wait_ge(f2_down, g + 1)
                    dve.tensor_copy(out4b[:, n, :, :], banks[:, 4 * n + 3, :].rearrange("p (j d) -> p j d", d=D)).then_inc(f2_out, 1)
                dve.wait_ge(rows_stored[2], 32 * i + 32)

        def experts2_gpsimd(pool):
            with pool.Fori(0, 6) as i:
                for n in range(2):
                    pool.wait_ge(f2_out, 2 * i + n + 1)
                    pool.dma_start(rows_out[2][bass.ds((2 * i + n) * 4 * P, 4 * P), :].rearrange("(j p) d -> p j d", p=P),
                                   out4b[:, n, :, :]).then_inc(rows_stored[2], 16)

        f3w = Region(LATE)
        up3T = f3w("up3T", [P, 8, F // P, D])
        down3 = f3w("down3", [P, 8, F // P, D])
        w3 = f3w("w3", [P, 8, D])
        chosen3 = f3w("chosen3", [P, 2, 8, D])
        f3_weights = sem("f3_weights")
        f3_product = sem("f3_product")
        f3_w3 = sem("f3_w3")
        f3_all = sem("f3_all")
        f3_masked = sem("f3_masked")

        def experts3_tensor(pe):
            pe.wait_ge(f3_weights, 32)
            for e in range(8):
                for c in range(F // P):
                    ins = pe.matmul(banks[:, e // 4, (e % 4) * D:(e % 4 + 1) * D], up3T[:, e, c, :], down3[:, e, c, :],
                                    start=(c == 0), stop=(c == F // P - 1))
            ins.then_inc(f3_product, 1)
            pe.wait_ge(f3_w3, 1)
            for t in range(TILES):
                if t >= 2:
                    pe.wait_ge(f3_masked, t - 1)
                for n in range(2):
                    ins = pe.matmul(banks[:, 2 + 2 * (t % 2) + n, :], xnT[:, t * P:(t + 1) * P], w3[:, 4 * n:4 * n + 4, :],
                                    start=True, stop=True)
                ins.then_inc(f3_all, 1)

        def experts3_scalar(act):
            act.wait_ge(f3_product, 1)
            act.activation(w3.rearrange("p e d -> p (e d)"), banks[:, 0:2, :].rearrange("p n c -> p (n c)"), ACT.Copy).then_inc(f3_w3, 1)

        def experts3_vector(dve):
            chosen = picks[:, 0:TILES * 8].rearrange("p (t e) -> p t e", e=8)
            for t in range(TILES):
                dve.wait_ge(f3_all, t + 1)
                dve.tensor_tensor(chosen3[:, t % 2, :, :],
                                  banks[:, 2 + 2 * (t % 2):4 + 2 * (t % 2), :].rearrange("p n (e d) -> p (n e) d", d=D),
                                  bcast(chosen[:, t, :].unsqueeze(2), (P, 8, D)), ALU.mult).then_inc(f3_masked, 1)
                dve.wait_ge(f3_masked, t + 1)
                ins = dve.tensor_reduce(g_out[:, t, :], chosen3[:, t % 2, :, :].rearrange("p e d -> p d e"), X, ALU.add)
            ins.then_inc(mix_ready, 1)
            dve.wait_ge(mix_ready, 4)

        block = ctx.enter_context(nc.Block())

        @block.sync
        def _(sp):
            sp.dma_start(x[:, :, :], a["L0_attn_X"].rearrange("(t p) d -> p t d", p=P)).then_inc(x_loaded, 16)
            sp.dma_start(const[:, :], a["const"]).then_inc(const_loaded, 16)
            sp.dma_start(w0[:, :, :], a["w0"]).then_inc(l0_weights, 16)
            sp.dma_start(w0vg[:, :, :], a["w0vg"]).then_inc(l0_weights, 16)
            sp.dma_start(w0o[:, :], a["L0_attn_W_O"]).then_inc(l0_weights, 16)
            sp.dma_start(gn_w[:, :], a["L0_attn_gn_weight"].partition_broadcast(P)).then_inc(l0_weights, 16)
            sp.dma_start(gn_b[:, :], a["L0_attn_gn_bias"].partition_broadcast(P)).then_inc(l0_weights, 16)
            for layer in range(4):
                sp.dma_start(router[layer][:, :], a[f"router{layer}"]).then_inc(routers_loaded, 16)
            sp.dma_start(gate_b1[:, :], a["L1_ffn_gate_b"].partition_broadcast(P)).then_inc(routers_loaded, 16)
            sp.wait_ge(zeros_set, 1)
            for layer in range(3):
                rows = rows_in[layer].shape[0]
                sp.dma_start(rows_in[layer].rearrange("(n p r) d -> p n (r d)", p=P, r=4),
                             bcast(zeros[:, :].unsqueeze(1), (P, rows // 512, 512))).then_inc(rows_zeroed, 16)
            for b in range(BATCH):
                sp.dma_start(q_rows[b, 48:51, :, :].rearrange("r h (n c) -> (r h) n c", n=4), bcast(zerosb[0:48, :].unsqueeze(1), (48, 4, P)))\
                    .then_inc(at_zero_rows, 16)
            experts1_weights(sp)
            experts0_sync(sp)
            sp.wait_ge(at_zero_rows, 16 * BATCH)
            project_sync(sp, 0)
            experts1_sync(sp)
            first_stacks_sync(sp, 0)
            sp.wait_ge(rows_stored[1], 160)
            sp.dma_start(gru_all, a["gru"]).then_inc(gru_loaded, 16)
            sp.dma_start(wgu_all, a["L2_gu"]).then_inc(f2_weights, 16)
            sp.dma_start(wd_all, a["L2_ffn_Wd"].rearrange("e f d -> f e d")).then_inc(f2_weights, 16)
            sp.dma_start(shared_w, a["L2_shared"]).then_inc(f2_weights, 16)
            sp.dma_start(shared_d, a["L2_ffn_Sd"].rearrange("(c p) d -> p c d", p=P)).then_inc(f2_weights, 16)
            attend_sync(sp, 0)
            experts2_sync(sp)
            sp.wait_ge(rows_stored[2], 192)
            sp.wait_ge(gru_set, 3)
            sp.dma_start(up3T, a["L3_upT"].rearrange("e (c p) d -> p e c d", p=P)).then_inc(f3_weights, 16)
            sp.dma_start(down3, a["L3_ffn_w_down"].rearrange("e (c p) d -> p e c d", p=P)).then_inc(f3_weights, 16)
            project_sync(sp, 1)
            first_stacks_sync(sp, 1)
            attend_sync(sp, 1)
            sp.wait_ge(x_final, 1)
            sp.dma_start(out.rearrange("(t p) d -> p t d", p=P), x[:, :, :]).then_inc(out_stored, 16)
            sp.wait_ge(out_stored, 16)

        @block.gpsimd
        def _(pool):
            step = Steps(pool, pool_step)
            pool.memset(minus_half[:, :], -0.5).then_inc(pool_consts_set, 1)
            pool.memset(ones[:, :], 1.0).then_inc(pool_consts_set, 1)
            pool.memset(zeros[:, :], 0.0).then_inc(zeros_set, 1)
            pool.memset(inv_d[:, :], 1.0 / D).then_inc(pool_consts_set, 1)
            pool.memset(v_half, 0.0).then_inc(l0_half_zero, 1)
            pool.wait_ge(pool_consts_set, 3)
            pool.wait_ge(const_loaded, 16)
            norm_gpsimd(pool, step, 0)
            send_rows(pool, 0)
            experts0_gpsimd(pool)
            retention_gpsimd(pool)
            norm_gpsimd(pool, step, 1)
            send_rows(pool, 1)
            project_gpsimd(pool, 0)
            experts1_gpsimd(pool)
            for _ in fetch_rows(pool, 1, 10):
                pass
            attend_gpsimd(pool, 0)
            norm_gpsimd(pool, step, 2)
            send_rows(pool, 2)
            experts2_gpsimd(pool)
            gru_gpsimd(pool, step)
            norm_gpsimd(pool, step, 3)
            project_gpsimd(pool, 1)
            attend_gpsimd(pool, 1)

        @block.scalar
        def _(act):
            norm_scalar(act, 0)
            routing_scalar(act, 0)
            retention_first_scalar(act)
            experts0_scalar(act)
            retention_rest_scalar(act)
            mix_scalar(act, 0)
            norm_scalar(act, 1)
            routing_scalar(act, 1)
            project_scalar(act, 0)
            experts1_scalar(act)
            attend_scalar(act, 0)
            mix_scalar(act, 1)
            norm_scalar(act, 2)
            routing_scalar(act, 2)
            shared_scalar(act)
            experts2_scalar(act)
            gru_scalar(act)
            mix_scalar(act, 2)
            norm_scalar(act, 3)
            project_scalar(act, 1)
            attend_scalar(act, 1)
            experts3_scalar(act)
            mix_scalar(act, 3)

        @block.vector
        def _(dve):
            step = Steps(dve, dve_step)
            dve.wait_ge(x_loaded, 16)
            dve.wait_ge(const_loaded, 16)
            dve.wait_ge(pool_consts_set, 3)
            step(dve.tensor_copy(identb[:, :], C["ident"]))
            step(dve.tensor_copy(negb[:, :, :], bcast(C["neg"].unsqueeze(1), (P, 4, P))))
            step(dve.tensor_copy(negTb[:, :, :], bcast(C["negT"].unsqueeze(1), (P, 2, P))))
            norm_vector(dve, step, 0)
            routing_vector(dve, step, 0)
            retention_first_vector(dve, step)
            experts0_vector(dve)
            retention_rest_vector(dve, step)
            mix_vector(dve, step, 0)
            norm_vector(dve, step, 1)
            routing_vector(dve, step, 1)
            project_vector(dve, step, 0)
            experts1_vector(dve)
            attend_vector(dve, 0)
            mix_vector(dve, step, 1)
            norm_vector(dve, step, 2)
            routing_vector(dve, step, 2)
            shared_vector(dve, step)
            experts2_vector(dve, step)
            gru_vector(dve, step)
            mix_vector(dve, step, 2)
            norm_vector(dve, step, 3)
            routing_vector(dve, step, 3)
            project_vector(dve, step, 1)
            attend_vector(dve, 1)
            experts3_vector(dve)
            mix_vector(dve, step, 3)

        @block.tensor
        def _(pe):
            pe.wait_ge(const_loaded, 16)
            pe.wait_ge(pool_consts_set, 3)
            norm_tensor(pe, 0)
            routing_tensor(pe, 0)
            retention_first_tensor(pe)
            experts0_tensor(pe)
            retention_rest_tensor(pe)
            norm_tensor(pe, 1)
            routing_tensor(pe, 1)
            project_tensor(pe, 0)
            experts1_tensor(pe)
            attend_tensor(pe, 0)
            norm_tensor(pe, 2)
            routing_tensor(pe, 2)
            shared_tensor(pe)
            experts2_tensor(pe)
            gru_tensor(pe)
            pe.wait_ge(gru_copied, 4)
            norm_tensor(pe, 3)
            routing_tensor(pe, 3)
            project_tensor(pe, 1)
            attend_tensor(pe, 1)
            experts3_tensor(pe)


def laid_out(i):
    def blocks(w):
        full = np.zeros((D, D), w.dtype)
        for h in range(H0):
            full[h * D0:(h + 1) * D0, h * D0:(h + 1) * D0] = w[h]
        return full

    swap = np.arange(D) ^ 1
    q0, k0, v0 = (blocks(i[f"L0_attn_W_{n}"]) for n in "QKV")
    return {
        "const": constants(),
        "L0_attn_X": i["L0_attn_X"].reshape(T, D),
        "w0": np.stack([q0, q0[:, swap], k0, k0[:, swap]], axis=1),
        "w0vg": np.stack([v0, i["L0_attn_W_G"]], axis=1),
        "L0_attn_W_O": i["L0_attn_W_O"],
        "L0_attn_gn_weight": i["L0_attn_gn_weight"],
        "L0_attn_gn_bias": i["L0_attn_gn_bias"],
        "wqkv1": i["L1_attn_in_proj_weight"].reshape(3, D, D).transpose(2, 0, 1),
        "wout1": i["L1_attn_out_proj_weight"].T,
        "qk_bias1": np.zeros((D, 2), np.float32),
        "v_bias1": np.zeros(D, np.float32),
        "out_bias1": np.zeros(D, np.float32),
        "wqkv3": i["L3_attn_attn_W"].reshape(D, H1, 3, D1).transpose(0, 2, 1, 3).reshape(D, 3, D),
        "wout3": i["L3_attn_out_W"],
        "qk_bias3": i["L3_attn_attn_b"].reshape(H1, 3, D1).transpose(1, 0, 2).reshape(3, D)[:2].T,
        "v_bias3": i["L3_attn_attn_b"].reshape(H1, 3, D1).transpose(1, 0, 2).reshape(3, D)[2],
        "out_bias3": i["L3_attn_out_b"],
        "L1_ffn_W1": i["L1_ffn_W1"].reshape(8 * D, F),
        "L1_ffn_b1": i["L1_ffn_b1"].reshape(8 * F),
        "L1_ffn_W2": i["L1_ffn_W2"].reshape(8 * F, D),
        "L1_ffn_b2": i["L1_ffn_b2"].reshape(8 * D),
        "gru": np.concatenate([i["L2_attn_W"].transpose(1, 0, 2), i["L2_attn_ln_gamma"].T[:, :, None],
                               i["L2_attn_ln_beta"].T[:, :, None], i["L2_attn_b"].reshape(3, 2, D).transpose(2, 0, 1)], axis=2),
        "L2_gu": np.concatenate([i["L2_ffn_Wg"], i["L2_ffn_Wu"]], axis=2).transpose(1, 0, 2),
        "L2_ffn_Wd": i["L2_ffn_Wd"],
        "L2_shared": np.concatenate([i["L2_ffn_Sg"], i["L2_ffn_Su"]], axis=1).reshape(D, 4, P),
        "L2_ffn_Sd": i["L2_ffn_Sd"],
        "L3_upT": i["L3_ffn_w_up"].transpose(0, 2, 1),
        "L3_ffn_w_down": i["L3_ffn_w_down"],
        "router0": i["L0_ffn_Wr"],
        "router1": i["L1_ffn_gate_w"],
        "router2": np.concatenate([i["L2_ffn_router_w"].T, i["L2_ffn_shared_gate_w"]], axis=1),
        "router3": i["L3_ffn_gate_w"].T,
        "L1_ffn_gate_b": i["L1_ffn_gate_b"],
        "L0_ffn_W1": i["L0_ffn_W1"].reshape(8 * D, F),
        "L0_ffn_W2": i["L0_ffn_W2"].reshape(8 * F, D),
    }


def kernel(**inputs):
    import concourse.bacc as _bacc
    from concourse.bass_utils import run_bass_kernel_spmd as _run

    nc = _bacc.Bacc("TRN2", target_bir_lowering=False, num_devices=1)
    arrays, args = {}, {}
    for name, value in laid_out({k: np.asarray(v) for k, v in inputs.items()}).items():
        arrays[f"in_{name}"] = np.ascontiguousarray(value)
        args[name] = nc.dram_tensor(f"in_{name}", value.shape, mybir.dt.from_np(value.dtype), kind="ExternalInput").ap()
    out = nc.dram_tensor("out", (T, D), F32, kind="ExternalOutput").ap()
    scratch = {kind: [nc.dram_tensor(f"{kind}{n}", (rows, D), F32).ap()
                      for n, rows in enumerate((8 * CAP + dropped, 40 * P, 48 * P))]
               for kind, dropped in (("rows_in", T), ("rows_out", 0))}
    scratch["q_rows"] = nc.dram_tensor("q_rows", (BATCH, 51, H1, SEQ), BF16).ap()
    scratch["k_rows"] = nc.dram_tensor("k_rows", (BATCH, 48, H1, SEQ), BF16).ap()
    build(nc, args, out, scratch)
    r = _run(nc, [arrays], core_ids=[0])
    return r.results[0]["out"].reshape(BATCH, SEQ, D)
```

```python
from contextlib import ExitStack, contextmanager

import numpy as np

import concourse.bass as bass
from concourse import mybir

P = 128
D = 128
BATCH, SEQ = 4, 512
T = BATCH * SEQ
TILES = T // P
BT = SEQ // P
EPS = 1e-5

F32 = mybir.dt.float32
BF16 = mybir.dt.bfloat16
I32 = mybir.dt.int32
U32 = mybir.dt.uint32
ALU = mybir.AluOpType
ACT = mybir.ActivationFunctionType
X = mybir.AxisListType.X

H0, D0 = 8, 16
H1, D1 = 16, 8
F = 512
CAP = T * 5 // 4 // 8
LATE = 19072
ARENA = LATE + 13 * 1024 + 32
PART = CAP // 4

WIDTHS = dict(ident=128, tri=128, neg=128, negT=128, decay=128, cosq=SEQ, sinq=SEQ, cosk=SEQ, sink=SEQ, heads=8,
              rev8=8, rev16=16, start320=8, dump=16, thr=128)
COLS = {}
_at = 0
for _k, _w in WIDTHS.items():
    COLS[_k] = (_at, _at + _w)
    _at += _w
CONST_W = _at


def constants():
    c = np.zeros((P, CONST_W), np.float32)

    def put(name, value):
        c[:, COLS[name][0]:COLS[name][1]] = value

    p = np.arange(P)
    put("ident", np.eye(P))
    put("tri", p[:, None] <= p[None, :])
    put("neg", np.where(p[None, :] > p[:, None], np.float32(-1e30), np.float32(0)))
    put("negT", np.where(p[:, None] > p[None, :], np.float32(-1e30), np.float32(0)))
    gammas = (1.0 - np.exp(np.linspace(np.log(1 / 32), np.log(1 / 512), H0))).astype(np.float32).astype(np.float64)
    head, j = p // D0, p % D0
    put("decay", (head[:, None] == head[None, :]) * (gammas[head] ** P)[:, None])
    pos = np.arange(SEQ)
    scale = ((np.arange(0, D0, 2) + 0.4 * D0) / (1.4 * D0))[j // 2]
    sc = scale[:, None] ** (pos / 512.0)[None, :]
    half = D0 // 2
    inv = (1.0 / np.float32(10000.0) ** (np.arange(half, dtype=np.float32) / np.float32(half))).astype(np.float32)
    angle = (pos[None, :].astype(np.float32) * inv[j // 2][:, None]).astype(np.float64)
    sign = np.where(j % 2 == 0, -1.0, 1.0)[:, None]
    grow = gammas[head][:, None] ** (pos % P)[None, :]
    put("cosq", np.cos(angle) * sc * grow)
    put("sinq", np.sin(angle) * sc * grow * sign)
    put("cosk", np.cos(angle) / sc / grow)
    put("sink", np.sin(angle) / sc / grow * sign)
    put("heads", head[:, None] == np.arange(H0)[None, :])
    put("rev8", 8 - np.arange(8)[None, :])
    put("rev16", 16 - np.arange(16)[None, :])
    put("start320", 320 * np.arange(8)[None, :])
    put("dump", 2560 + np.arange(16)[None, :] * P + p[:, None])
    put("thr", 128 * np.arange(128)[None, :])
    return c


class Steps:

    def __init__(self, eng, sem):
        self.eng, self.sem, self.count, self.turn = eng, sem, 0, 0

    def __call__(self, instruction):
        instruction.then_inc(self.sem, 1)
        self.count += 1
        self.eng.wait_ge(self.sem, self.count + self.turn)

    def loop(self, times, steps):
        return self.loop_from(0, times, steps)

    @contextmanager
    def loop_from(self, start, times, steps):
        first = self.count
        with self.eng.Fori(start, start + times) as i:
            self.turn = (i - start) * steps if start else i * steps
            yield i
        assert self.count == first + steps, self.count - first
        self.count, self.turn = first + times * steps, 0


def bcast(ap, shape):
    return ap.broadcast_to(list(shape))


def build(nc, a, out, scratch):
    ctx = ExitStack()
    with ctx:
        def sb(name, shape, dt=F32):
            return ctx.enter_context(nc.sbuf_tensor(name, shape, dt))

        def sem(name):
            return ctx.enter_context(nc.semaphore(name))

        banks = ctx.enter_context(nc.psum_tensor("banks", [P, 8, 512], F32))

        const = sb("const", [P, CONST_W])
        C = {k: const[:, lo:hi] for k, (lo, hi) in COLS.items()}
        x = sb("x", [P, TILES, D])
        xn = sb("xn", [P, TILES, D])
        xnT = sb("xnT", [P, T])
        s_out = sb("s_out", [P, TILES, D])
        g_out = sb("g_out", [P, TILES, D])
        squares = sb("squares", [P, TILES, D])
        mean = sb("mean", [P, 64])
        var = sb("var", [P, 64])
        rstd = sb("rstd", [P, 64])
        minus_half = sb("minus_half", [P, 64])
        ones = sb("ones", [P, P])

        const_loaded = sem("const_loaded")
        x_loaded = sem("x_loaded")
        out_stored = sem("out_stored")
        x_final = sem("x_final")
        pool_consts_set = sem("pool_consts_set")
        dve_step = sem("dve_step")
        pool_step = sem("pool_step")

        norm_centered = sem("norm_centered")
        norm_squared = sem("norm_squared")
        norm_var = sem("norm_var")
        norm_rstd = sem("norm_rstd")
        norm_done = sem("norm_done")
        norm_transposed = sem("norm_transposed")
        xnT_ready = sem("xnT_ready")

        def norm_vector(dve, step, layer, new_x=None):
            first = BATCH * layer

            def variances(b):
                tiles = slice(BT * b, BT * b + BT)
                dve.wait_ge(norm_squared, first + b + 1)
                dve.tensor_scalar(var[:, tiles], var[:, tiles], 1.0 / D, EPS, ALU.mult, ALU.add).then_inc(norm_var, 1)

            def scale(b):
                tiles = slice(BT * b, BT * b + BT)
                dve.wait_ge(norm_rstd, first + b + 1)
                dve.tensor_tensor(xn[:, tiles, :], xn[:, tiles, :], bcast(rstd[:, tiles].unsqueeze(2), (P, BT, D)),
                                  ALU.mult).then_inc(norm_done, 1)

            for b in range(BATCH):
                tiles = slice(BT * b, BT * b + BT)
                if new_x:
                    new_x(b)
                step(dve.tensor_reduce(mean[:, tiles], x[:, tiles, :], X, ALU.add))
                step(dve.tensor_scalar(mean[:, tiles], mean[:, tiles], 1.0 / D, None, ALU.mult))
                dve.tensor_tensor(xn[:, tiles, :], x[:, tiles, :], bcast(mean[:, tiles].unsqueeze(2), (P, BT, D)),
                                  ALU.subtract).then_inc(norm_centered, 1)
                if b > 0:
                    variances(b - 1)
                if layer == 0 and b > 1:
                    scale(b - 2)
            variances(BATCH - 1)
            if layer == 0:
                scale(BATCH - 2)
                scale(BATCH - 1)

        def norm_scalar(act, layer):
            first = BATCH * layer

            def sum_squares(b):
                act.wait_ge(norm_centered, first + b + 1)
                for t in range(BT * b, BT * b + BT):
                    ins = act.activation(squares[:, t, :], xn[:, t, :], ACT.Square, accum_out=var[:, t:t + 1])
                ins.then_inc(norm_squared, 1)

            def scale(b):
                act.wait_ge(norm_rstd, first + b + 1)
                for t in range(BT * b, BT * b + BT):
                    ins = act.activation(xn[:, t, :], xn[:, t, :], ACT.Copy, scale=rstd[:, t:t + 1])
                ins.then_inc(norm_done, 1)

            def copy_turned(b):
                act.wait_ge(norm_transposed, first + b + 1)
                act.activation(xnT[:, b * SEQ:(b + 1) * SEQ], banks[:, b, :], ACT.Copy).then_inc(xnT_ready, 1)

            for b in range(BATCH):
                sum_squares(b)
                if b > 0 and layer > 0:
                    scale(b - 1)
                if b > 1:
                    copy_turned(b - 2)
            if layer > 0:
                scale(BATCH - 1)
            copy_turned(BATCH - 2)
            if layer == 3:
                act.wait_ge(xnT_ready, first + 1)
                act.activation(xb1, xnT[:, 0:SEQ], ACT.Copy).then_inc(at_x_copied, 1)
            copy_turned(BATCH - 1)

        def norm_gpsimd(pool, layer):
            for b in range(BATCH):
                tiles = slice(BT * b, BT * b + BT)
                pool.wait_ge(norm_var, BATCH * layer + b + 1)
                pool.tensor_tensor(rstd[:, tiles], var[:, tiles], minus_half[:, tiles], ALU.pow).then_inc(norm_rstd, 1)

        def norm_tensor(pe, layer):
            def turn(b):
                pe.wait_ge(norm_done, BATCH * layer + b + 1)
                for t in range(BT):
                    ins = pe.transpose(banks[:, b, t * P:(t + 1) * P], xn[:, BT * b + t, :], C["ident"])
                ins.then_inc(norm_transposed, 1)

            def logits(b):
                pe.wait_ge(xnT_ready, BATCH * layer + b + 1)
                routing_logits(pe, layer, b)

            if layer == 0:
                pe.wait_ge(routers_loaded, 16 * 5)
            for b in range(BATCH):
                turn(b)
                if b > 0 and layer < 3:
                    logits(b - 1)
            if layer < 3:
                logits(BATCH - 1)

        arena = sb("arena", [P, ARENA])

        class Region:

            def __init__(self, at, end=ARENA):
                self.at, self.end = at, end

            def __call__(self, name, shape, dt=F32):
                n = int(np.prod(shape[1:]))
                words = n if dt != BF16 else (n + 1) // 2
                ap = arena[0:shape[0], self.at:self.at + words]
                self.at += words
                assert self.at <= self.end, (name, self.at, self.end)
                if dt != F32:
                    ap = ap.bitcast(dt)
                if len(shape) > 2:
                    dims = "abcd"[:len(shape) - 1]
                    ap = ap.rearrange(f"p ({' '.join(dims)}) -> p {' '.join(dims)}", **dict(zip(dims, shape[1:])))
                return ap

        l0 = Region(0, LATE)
        w0 = l0("w0", [P, 4, P])
        w0vg = l0("w0vg", [P, 2, P])
        w0o = l0("w0o", [P, P])
        gn_w = l0("gn_w", [P, D])
        gn_b = l0("gn_b", [P, D])
        xb = l0("xb", [P, SEQ])
        qT = l0("qT", [P, SEQ])
        kT = l0("kT", [P, SEQ])
        rot = l0("rot", [P, SEQ])
        yT = rot
        v_tok = l0("v_tok", [P, BT, D])
        v_half = l0("v_half", [P, 2, BT, D])
        gate_sig = l0("gate_sig", [P, BT, D])
        gate = l0("gate", [P, BT, D])
        q_heads_at = l0.at
        q_heads = l0("q_heads", [P, H0, SEQ])
        attT = l0("attT", [P, 2, H0, P])
        attT_end = l0.at
        k_tok = l0("k_tok", [P, BT - 1, P])
        state = l0("state", [P, BT - 1, P])
        yc = l0("yc", [P, BT * H0, D0])
        zT = l0("zT", [P, SEQ])
        fetched_at = l0.at

        l0_weights = sem("l0_weights")
        l0_x_copied = sem("l0_x_copied")
        l0_projected = sem("l0_projected")
        l0_v_copied = sem("l0_v_copied")
        l0_sig = sem("l0_sig")
        l0_q_ready = sem("l0_q_ready")
        l0_k_ready = sem("l0_k_ready")
        l0_q_heads = sem("l0_q_heads")
        l0_k_turned = sem("l0_k_turned")
        l0_k_tok = sem("l0_k_tok")
        l0_scores = sem("l0_scores")
        l0_att = sem("l0_att")
        l0_update = sem("l0_update")
        l0_state = sem("l0_state")
        l0_y = sem("l0_y")
        l0_yT = sem("l0_yT")
        l0_y_turned = sem("l0_y_turned")
        l0_centered = sem("l0_centered")
        l0_squared = sem("l0_squared")
        l0_var = sem("l0_var")
        l0_rstd = sem("l0_rstd")
        l0_z = sem("l0_z")
        l0_gate = sem("l0_gate")
        l0_z_turned = sem("l0_z_turned")
        l0_zT = sem("l0_zT")
        l0_s = sem("l0_s")
        l0_s_copied = sem("l0_s_copied")

        HEAD_SETS = (range(0, 4), range(4, 6), range(6, 8))

        def retention_first_tensor(pe):
            pe.wait_ge(l0_weights, 16 * 5)
            retention_pass_tensor(pe, 0, head=True, tail=False)
            pe.sem_inc(l0_s_copied, 1)

        def retention_rest_tensor(pe):
            with pe.Fori(1, BATCH) as b:
                pe.wait_ge(l0_s_copied, b)
                retention_pass_tensor(pe, b, head=True, tail=True)
            retention_pass_tensor(pe, BATCH, head=False, tail=True)
            pe.wait_ge(l0_s_copied, BATCH + 1)

        def retention_pass_tensor(pe, b, head, tail):
            def scores(c):
                if c >= 2:
                    pe.wait_ge(l0_att, BT * b + c - 1)
                for n in range(2):
                    if c == 0 and n == 0:
                        pe.wait_ge(l0_q_heads, 3 * b + 3)
                    ins = pe.matmul(banks[:, 2 * (c % 2) + n, :], kT[:, c * P:(c + 1) * P],
                                    q_heads[:, 4 * n:4 * n + 4, c * P:(c + 1) * P], start=True, stop=True)
                ins.then_inc(l0_scores, 1)

            def sums(c):
                y = banks[:, 7, c * P:(c + 1) * P]
                if c >= 1:
                    pe.matmul(y, state[:, c - 1, :], qT[:, c * P:(c + 1) * P], start=True, stop=False)
                pe.wait_ge(l0_att, BT * b + c + 1)
                for h in range(H0):
                    pair = slice(32 * (h // 2), 32 * (h // 2) + 32)
                    ins = pe.matmul(y[pair, :], v_half[:, h % 2, c, pair], attT[:, c % 2, h, :],
                                    start=(c == 0 and h % 2 == 0), stop=(h % 2 == 1))
                ins.then_inc(l0_y, 1)

            if head:
                pe.wait_ge(l0_x_copied, b + 1)
                for n in range(4):
                    ins = pe.matmul(banks[:, n, :], w0[:, n, :], xb[:, :], start=True, stop=True)
                ins.then_inc(l0_projected, 1)
                if not tail:
                    pe.wait_ge(route_slots, 1)
                for t in range(BT):
                    ins = pe.matmul(banks[:, 4 + t // 2, (t % 2) * 256:(t % 2 + 1) * 256], xb[:, t * P:(t + 1) * P],
                                    w0vg[:, :, :], start=True, stop=True)
                ins.then_inc(l0_projected, 1)
                pe.wait_ge(l0_k_ready, b + 1)
                for c in range(BT - 1):
                    ins = pe.transpose(banks[:, 7, c * P:(c + 1) * P], kT[:, c * P:(c + 1) * P], C["ident"])
                ins.then_inc(l0_k_turned, 1)
                scores(0)
                pe.wait_ge(l0_k_tok, b + 1)
                for c in range(BT - 1):
                    ins = pe.matmul(banks[:, 7, c * P:(c + 1) * P], k_tok[:, c, :], v_tok[:, c, :], start=True, stop=True)
                ins.then_inc(l0_update, 1)
                scores(1)
                pe.wait_ge(l0_state, b + 1)
                pe.wait_ge(l0_v_copied, b + 1)
                sums(0)
                scores(2)
                sums(1)
                scores(3)
                sums(2)
            if tail:
                pe.wait_ge(l0_z, b)
                if head:
                    pe.wait_ge(l0_gate, b + 1)
                for t in range(BT):
                    ins = pe.transpose(banks[:, 4, t * P:(t + 1) * P],
                                       yc[:, t * H0:(t + 1) * H0, :].rearrange("p h d -> p (h d)"), C["ident"])
                ins.then_inc(l0_z_turned, 1)
            if head:
                sums(3)
            if tail:
                pe.wait_ge(l0_zT, b)
                for t in range(BT):
                    ins = pe.matmul(banks[:, 5, t * P:(t + 1) * P], zT[:, t * P:(t + 1) * P], w0o[:, :],
                                    start=True, stop=True)
                ins.then_inc(l0_s, 1)
            if head:
                pe.wait_ge(l0_yT, b + 1)
                for t in range(BT):
                    ins = pe.transpose(banks[:, 6, t * P:(t + 1) * P], yT[:, t * P:(t + 1) * P], C["ident"])
                ins.then_inc(l0_y_turned, 1)

        HEAD_STEPS, TAIL_STEPS = 8, 6

        def retention_first_vector(dve, step):
            dve.wait_ge(l0_weights, 16 * 5)
            retention_pass_vector(dve, step, 0, head=True, tail=False)

        def retention_rest_vector(dve, step):
            dve.wait_ge(rows_stored[0], 16 * 8)
            with step.loop_from(1, BATCH - 1, HEAD_STEPS + TAIL_STEPS) as b:
                retention_pass_vector(dve, step, b, head=True, tail=True)
            retention_pass_vector(dve, step, BATCH, head=False, tail=True)
            gate_silu_vector(dve, step, 0)

        def retention_s(dve, b):
            dve.wait_ge(l0_s_copied, b + 2)
            return s_out[:, BT * b:BT * b + BT, :], None, None

        def retention_pass_vector(dve, step, b, head, tail):
            def mask(c):
                dve.wait_ge(l0_scores, BT * b + c + 1)
                if c >= 2:
                    dve.wait_ge(l0_y, BT * b + c - 1)
                dve.tensor_tensor(attT[:, c % 2, :, :],
                                  banks[:, 2 * (c % 2):2 * (c % 2) + 2, :].rearrange("p n (h s) -> p (n h) s", h=4),
                                  bcast(C["tri"].unsqueeze(1), (P, H0, P)), ALU.mult).then_inc(l0_att, 1)

            if tail:
                dve.wait_ge(l0_y_turned, b)
                y = banks[:, 6, :].rearrange("p (g d) -> p g d", d=D0)
                step(dve.tensor_reduce(mean[:, 0:32], y, X, ALU.add))
                step(dve.tensor_scalar(mean[:, 0:32], mean[:, 0:32], 1.0 / D0, None, ALU.mult))
                dve.tensor_tensor(yc[:, :, :], y, bcast(mean[:, 0:32].unsqueeze(2), (P, 32, D0)), ALU.subtract)\
                    .then_inc(l0_centered, 1)
            if head:
                dve.wait_ge(l0_projected, 2 * b + 1)
                step(dve.tensor_tensor(rot[:, :], banks[:, 0, :], C["cosq"], ALU.mult))
                step(dve.tensor_tensor(qT[:, :], banks[:, 1, :], C["sinq"], ALU.mult))
                dve.tensor_tensor(qT[:, :], qT[:, :], rot[:, :], ALU.add).then_inc(l0_q_ready, 1)
                dve.wait_ge(l0_q_ready, b + 1)
                step(dve.tensor_tensor(rot[:, :], banks[:, 2, :], C["cosk"], ALU.mult))
                step(dve.tensor_tensor(kT[:, :], banks[:, 3, :], C["sink"], ALU.mult))
                dve.tensor_tensor(kT[:, :], kT[:, :], rot[:, :], ALU.add).then_inc(l0_k_ready, 1)
                for h in HEAD_SETS[1]:
                    ins = dve.tensor_scalar(q_heads[:, h, :], qT[:, :], C["heads"][:, h:h + 1], None, ALU.mult)
                ins.then_inc(l0_q_heads, 1)
            if tail:
                dve.wait_ge(l0_squared, b)
                step(dve.tensor_reduce(var[:, 0:32], squares[:, 0:4, :].rearrange("p t (h d) -> p (t h) d", d=D0), X, ALU.add))
                dve.tensor_scalar(var[:, 0:32], var[:, 0:32], 1.0 / D0, EPS, ALU.mult, ALU.add).then_inc(l0_var, 1)
            if head:
                mask(0)
                dve.wait_ge(l0_update, b + 1)
                step(dve.tensor_tensor(state[:, 0, :], banks[:, 7, 0:P], C["decay"], ALU.mult))
                for c in range(1, BT - 1):
                    step(dve.tensor_tensor(state[:, c, :], state[:, c - 1, :], banks[:, 7, c * P:(c + 1) * P], ALU.add))
                    ins = dve.tensor_tensor(state[:, c, :], state[:, c, :], C["decay"], ALU.mult)
                    if c < BT - 2:
                        step(ins)
                ins.then_inc(l0_state, 1)
                mask(1)
                mask(2)
            if tail:
                if not head:
                    gate_vector(dve, step, 0)
                dve.wait_ge(l0_rstd, b)
                step(dve.tensor_tensor(yc[:, :, :], yc[:, :, :], bcast(rstd[:, 0:32].unsqueeze(2), (P, 32, D0)), ALU.mult))
                y4 = yc[:, :, :].rearrange("p (t h) d -> p t h d", t=BT).rearrange("p t h d -> p t (h d)")
                step(dve.tensor_tensor(y4, y4, bcast(gn_w[:, :].unsqueeze(1), (P, BT, D)), ALU.mult))
                step(dve.tensor_tensor(y4, y4, bcast(gn_b[:, :].unsqueeze(1), (P, BT, D)), ALU.add))
                dve.tensor_tensor(y4, y4, gate[:, :, :], ALU.mult).then_inc(l0_z, 1)
            if head:
                if tail:
                    dve.wait_ge(l0_z, b)
                dve.wait_ge(l0_sig, b + 1)
                dve.tensor_tensor(gate[:, :, :],
                                  banks[:, 4:6, :].rearrange("p n (t w e) -> p (n t) w e", t=2, w=2)[:, :, 1, :],
                                  gate_sig[:, :, :], ALU.mult).then_inc(l0_gate, 1)
                mask(3)

        def retention_first_scalar(act):
            act.wait_ge(pool_consts_set, 4)
            act.activation(xb[:, :], xnT[:, 0:SEQ], ACT.Copy).then_inc(l0_x_copied, 1)
            retention_pass_scalar(act, 0, head=True, tail=False)

        def retention_rest_scalar(act):
            with act.Fori(1, BATCH) as b:
                act.activation(xb[:, :], xnT[:, bass.ds(b * SEQ, SEQ)], ACT.Copy).then_inc(l0_x_copied, 1)
                retention_pass_scalar(act, b, head=True, tail=True)
            retention_pass_scalar(act, BATCH, head=False, tail=True)

        def retention_pass_scalar(act, b, head, tail):
            if tail:
                act.wait_ge(l0_centered, b)
                act.activation(squares[:, 0:4, :], yc[:, :, :].rearrange("p (t h) d -> p t (h d)", t=BT), ACT.Square)\
                    .then_inc(l0_squared, 1)
            if head:
                act.wait_ge(l0_q_ready, b + 1)
                for heads in (HEAD_SETS[0],) if tail else (HEAD_SETS[0], HEAD_SETS[2]):
                    for h in heads:
                        ins = act.activation(q_heads[:, h, :], qT[:, :], ACT.Copy, scale=C["heads"][:, h:h + 1])
                    ins.then_inc(l0_q_heads, 1)
                act.wait_ge(l0_k_turned, b + 1)
                act.activation(k_tok[:, :, :], banks[:, 7, 0:(BT - 1) * P].rearrange("p (c e) -> p c e", e=P), ACT.Copy)
                act.wait_ge(l0_projected, 2 * b + 2)
                vg = banks[:, 4:6, :].rearrange("p n (t w e) -> p (n t) w e", t=2, w=2)
                act.activation(v_tok[:, :, :], vg[:, :, 0, :], ACT.Copy).then_inc(l0_k_tok, 1)
                for n in range(2):
                    ins = act.activation(v_half[:, n, :, :].rearrange("p t (j w e) -> p t j w e", w=2, e=D0)[:, :, :, n, :],
                                   vg[:, :, 0, :].rearrange("p t (j w e) -> p t j w e", w=2, e=D0)[:, :, :, n, :], ACT.Copy)
                ins.then_inc(l0_v_copied, 1)
                act.activation(gate_sig[:, :, :], vg[:, :, 1, :], ACT.Sigmoid).then_inc(l0_sig, 1)
            if tail and not head:
                gate_scalar(act, 0)
            if tail:
                act.wait_ge(l0_z_turned, b)
                act.activation(zT[:, :], banks[:, 4, :], ACT.Copy).then_inc(l0_zT, 1)
            if head:
                act.wait_ge(l0_y, BT * b + BT)
                act.activation(yT[:, :], banks[:, 7, :], ACT.Copy).then_inc(l0_yT, 1)
            if tail:
                act.wait_ge(l0_s, b)
                tiles = slice((b - 1) * BT, b * BT) if isinstance(b, int) else bass.ds((b - 1) * BT, BT)
                act.activation(s_out[:, tiles, :], banks[:, 5, :].rearrange("p (t d) -> p t d", d=D), ACT.Copy)\
                    .then_inc(l0_s_copied, 1)

        def retention_gpsimd(pool):
            fetches = fetch_rows(pool, 0, 8)
            heads = slice(HEAD_SETS[2][0], HEAD_SETS[2][-1] + 1)
            for b in range(BATCH):
                if b + 1 < BATCH:
                    pool.wait_ge(l0_q_ready, b + 2)
                    pool.tensor_tensor(q_heads[:, heads, :], bcast(qT[:, :].unsqueeze(1), (P, 2, SEQ)),
                                       bcast(C["heads"][:, heads].unsqueeze(2), (P, 2, SEQ)), ALU.mult).then_inc(l0_q_heads, 1)
                pool.wait_ge(l0_var, b + 1)
                pool.tensor_tensor(rstd[:, 0:32], var[:, 0:32], minus_half[:, 0:32], ALU.pow).then_inc(l0_rstd, 1)
                for _ in range((6, 5, 5, 0)[b]):
                    next(fetches)

        shared_logit = sb("shared_logit", [P, TILES])

        logits = sb("logits", [P, TILES, 16])
        second = sb("second", [P, TILES, 16])
        pick1 = sb("pick1", [P, TILES, 16])
        pick2 = sb("pick2", [P, TILES, 16])
        picks = sb("picks", [P, TILES * 16])
        match = sb("match", [P, TILES, 16])
        top = sb("top", [P, 8, TILES])
        totals = sb("totals", [P, 16 * TILES])
        prefix = sb("prefix", [P, 16 * TILES])
        place = sb("place", [P, TILES, 16])
        count = sb("count", [P, 4, 16])
        count_int = sb("count_int", [P, 16], I32)
        slots = sb("slots", [P, 3, TILES], I32)
        weights = sb("weights", [P, 2, TILES])
        tile_cmp = sb("tile_cmp", [P, 48 * 16])
        tile_sum = sb("tile_sum", [P, 48])
        tile_expert = sb("tile_expert", [P, 2, 48], I32)
        router = {0: sb("router0", [P, 8]), 1: sb("router1", [P, 8]), 2: sb("router2", [P, 17]), 3: sb("router3", [P, 8])}
        gate_b1 = sb("gate_b1", [P, 8])
        EXPERTS = {0: 8, 1: 8, 2: 16, 3: 8}
        FFN_TILES = {1: 40, 2: 48}

        routers_loaded = sem("routers_loaded")
        route_logits = sem("route_logits")
        route_gap = sem("route_gap")
        route_exp = sem("route_exp")
        route_picked = sem("route_picked")
        route_counted = sem("route_counted")
        route_slots = sem("route_slots")
        route_first = sem("route_first")
        route_read = sem("route_read")

        def routing_logits(pe, layer, b):
            w = EXPERTS[layer] + (layer == 2)
            for t in range(BT * b, BT * b + BT):
                ins = pe.matmul(banks[:, 4, t * w:(t + 1) * w], xnT[:, t * P:(t + 1) * P], router[layer][:, 0:w],
                                start=True, stop=True)
            if b == BATCH - 1:
                ins.then_inc(route_logits, 1)

        def routing_tensor(pe, layer):
            e = EXPERTS[layer]
            pe.wait_ge(route_picked, layer + 1)
            pe.matmul(banks[:, 5, 0:TILES * e], C["tri"], picks[:, 0:TILES * e], start=True, stop=True)
            pe.matmul(banks[:, 6, 0:TILES * e], ones[:, :], picks[:, 0:TILES * e], start=True, stop=True)\
                .then_inc(route_counted, 1)

        def routing_scalar(act, layer):
            e = EXPERTS[layer]
            act.wait_ge(route_gap, layer + 1)
            if layer == 0:
                act.activation(match[:, :, 0:e], match[:, :, 0:e], ACT.Exp).then_inc(route_exp, 1)
            else:
                act.activation(top[:, 2, :], top[:, 2, :], ACT.Exp).then_inc(route_exp, 1)

        def routing_vector(dve, step, layer, read=True, rest=True):
            e = EXPERTS[layer]
            w = e + (layer == 2)
            shape = (P, TILES, e)
            lg, lg2, p1, p2, mt, pl = (v[:, :, 0:e] for v in (logits, second, pick1, pick2, match, place))
            rev = C["rev8" if e == 8 else "rev16"]
            rev3 = bcast(rev.unsqueeze(1), shape)

            def wide(v):
                return bcast(v.unsqueeze(2), shape)

            def pick(values, largest, chosen):
                step(dve.tensor_reduce(largest, values, X, ALU.max))
                step(dve.tensor_tensor(mt, values, wide(largest), ALU.is_equal))
                step(dve.tensor_tensor(mt, mt, rev3, ALU.mult))
                step(dve.tensor_reduce(top[:, 7, :], mt, X, ALU.max))
                step(dve.tensor_tensor(chosen, rev3, wide(top[:, 7, :]), ALU.is_equal))

            if read:
                dve.wait_ge(route_logits, layer + 1)
                raw = banks[:, 4, 0:TILES * w].rearrange("p (t e) -> p t e", e=w)
                if layer == 1:
                    ins = dve.tensor_tensor(lg, raw[:, :, 0:e], bcast(gate_b1[:, :].unsqueeze(1), shape), ALU.add)
                else:
                    ins = dve.tensor_copy(lg, raw[:, :, 0:e])
                if layer in (1, 3):
                    ins.then_inc(route_read, 1)
                    dve.wait_ge(route_read, (layer + 1) // 2)
                else:
                    step(ins)
            if not rest:
                return
            if layer == 2:
                step(dve.tensor_copy(shared_logit[:, :], raw[:, :, e]))
            pick(lg, top[:, 0, :], p1)
            all_picks = picks[:, 0:TILES * e].rearrange("p (t e) -> p t e", e=e)
            if layer == 0:
                dve.tensor_copy(all_picks, p1).then_inc(route_picked, 1)
                dve.tensor_tensor(mt, lg, wide(top[:, 0, :]), ALU.subtract).then_inc(route_gap, 1)
            else:
                step(dve.scalar_tensor_tensor(lg2, p1, -1e30, lg, ALU.mult, ALU.add))
                pick(lg2, top[:, 1, :], p2)
                dve.tensor_tensor(all_picks, p1, p2, ALU.add).then_inc(route_picked, 1)
                if layer < 3:
                    dve.tensor_tensor(top[:, 2, :], top[:, 1, :], top[:, 0, :], ALU.subtract).then_inc(route_gap, 1)
                else:
                    return
            dve.wait_ge(route_exp, layer + 1)
            if layer == 0:
                step(dve.tensor_reduce(top[:, 3, :], mt, X, ALU.add))
                step(dve.reciprocal(top[:, 4, :], top[:, 3, :]))
            else:
                step(dve.tensor_scalar(top[:, 3, :], top[:, 2, :], 1.0, None, ALU.add))
                step(dve.reciprocal(weights[:, 0, :], top[:, 3, :]))
                step(dve.tensor_tensor(weights[:, 1, :], top[:, 2, :], weights[:, 0, :], ALU.mult))
            dve.wait_ge(route_counted, layer + 1)
            et = (P, e, TILES)
            tot = totals[:, 0:e * TILES]
            pre = prefix[:, 0:e * TILES]
            tot3, pre3 = (v.rearrange("p (e t) -> p e t", e=e) for v in (tot, pre))
            step(dve.tensor_copy(tot3, banks[:, 6, 0:TILES * e].rearrange("p (t e) -> p e t", e=e)))
            step(dve.tensor_tensor_scan(pre, bcast(ones[:, 0:1], (P, e * TILES)), tot, 0.0, ALU.mult, ALU.add))
            step(dve.tensor_tensor(pre, pre, tot, ALU.subtract))
            running = banks[:, 5, 0:TILES * e].rearrange("p (t e) -> p t e", e=e)
            start = count[:, 0, 0:e]
            if layer == 0:
                step(dve.tensor_copy(start, pre3[:, :, 0]))
                step(dve.tensor_tensor(pre3, pre3, bcast(start.unsqueeze(2), et), ALU.subtract))
                step(dve.tensor_tensor(pl, running, pre3.rearrange("p e t -> p t e"), ALU.add))
                step(dve.tensor_tensor(pl, pl, p1, ALU.mult))
                step(dve.tensor_reduce(top[:, 2, :], pl, X, ALU.add))
                step(dve.tensor_tensor(pl, p1, bcast(C["start320"].unsqueeze(1), shape), ALU.mult))
                step(dve.tensor_reduce(top[:, 3, :], pl, X, ALU.add))
                step(dve.tensor_scalar(top[:, 5, :], top[:, 2, :], float(CAP), None, ALU.is_le))
                step(dve.tensor_tensor(weights[:, 0, :], top[:, 4, :], top[:, 5, :], ALU.mult))
                step(dve.tensor_scalar(weights[:, 1, :], top[:, 5, :], -1.0, 1.0, ALU.mult, ALU.add))
                step(dve.scalar_tensor_tensor(top[:, 3, :], top[:, 2, :], -1.0, top[:, 3, :], ALU.add, ALU.add))
                step(dve.tensor_tensor(top[:, 2, :], top[:, 3, :], C["dump"], ALU.subtract))
                step(dve.tensor_tensor(top[:, 2, :], top[:, 2, :], top[:, 5, :], ALU.mult))
                step(dve.tensor_tensor(top[:, 2, :], top[:, 2, :], C["dump"], ALU.add))
                step(dve.tensor_scalar(top[:, 3, :], top[:, 3, :], float(8 * CAP - 1), None, ALU.min))
                step(dve.tensor_copy(slots[:, 2, :], top[:, 3, :]))
                dve.tensor_copy(slots[:, 0, :], top[:, 2, :]).then_inc(route_slots, 1)
            else:
                end, padded, shift = (count[:, n, 0:e] for n in (1, 2, 3))
                step(dve.tensor_copy(start, pre3[:, :, 0]))
                step(dve.tensor_tensor(end, pre3[:, :, TILES - 1], tot3[:, :, TILES - 1], ALU.add))
                step(dve.tensor_tensor(padded, end, start, ALU.subtract))
                step(dve.tensor_scalar(padded, padded, float(P - 1), None, ALU.add))
                step(dve.tensor_copy(count_int[:, 0:e], padded))
                step(dve.tensor_scalar(count_int[:, 0:e], count_int[:, 0:e], 7, None, ALU.arith_shift_right))
                step(dve.tensor_scalar(count_int[:, 0:e], count_int[:, 0:e], 7, None, ALU.logical_shift_left))
                step(dve.tensor_copy(padded, count_int[:, 0:e]))
                step(dve.tensor_tensor_scan(end, bcast(ones[:, 0:1], (P, e)), padded, 0.0, ALU.mult, ALU.add))
                step(dve.tensor_tensor(shift, end, padded, ALU.subtract))
                step(dve.tensor_tensor(shift, shift, start, ALU.subtract))
                step(dve.tensor_tensor(pre3, pre3, bcast(shift.unsqueeze(2), et), ALU.add))
                step(dve.tensor_tensor(pl, running, pre3.rearrange("p e t -> p t e"), ALU.add))
                for n, chosen in enumerate((p1, p2)):
                    step(dve.tensor_tensor(mt, pl, chosen, ALU.mult))
                    step(dve.tensor_reduce(top[:, 5, :], mt, X, ALU.add))
                    ins = dve.tensor_scalar(slots[:, n, :], top[:, 5, :], -1.0, None, ALU.add)
                    if n == 0:
                        ins.then_inc(route_first, 1)
                        dve.wait_ge(route_first, layer)
                    else:
                        step(ins)
                n_tiles = FFN_TILES[layer]
                cmp3 = tile_cmp[:, 0:n_tiles * e].rearrange("p (j e) -> p j e", e=e)
                step(dve.tensor_tensor(cmp3, bcast(end.unsqueeze(1), (P, n_tiles, e)),
                                       bcast(C["thr"][:, 0:n_tiles].unsqueeze(2), (P, n_tiles, e)), ALU.is_le))
                step(dve.tensor_reduce(tile_sum[:, 0:n_tiles], cmp3, X, ALU.add))
                step(dve.tensor_scalar(tile_sum[:, 0:n_tiles], tile_sum[:, 0:n_tiles], float(e - 1), None, ALU.min))
                dve.tensor_copy(tile_expert[:, layer - 1, 0:n_tiles], tile_sum[:, 0:n_tiles]).then_inc(route_slots, 1)

        fetched = {0: Region(fetched_at, LATE)("fetched0", [P, 1, TILES, D])}
        fetched[1] = fetched[2] = Region(ARENA - 2 * TILES * D)("fetched", [P, 2, TILES, D])
        rows_in, rows_out = scratch["rows_in"], scratch["rows_out"]
        zeros = sb("zeros", [P, 512])
        zeros_set = sem("zeros_set")
        outputs_free = sem("outputs_free")
        PASSES = {0: 4, 1: 2, 2: 3}
        GROUPS1 = 5
        stored_before = {0: 0, 1: 4, 2: 4 + 2 * GROUPS1}
        rows_zeroed = sem("rows_zeroed")
        scratch_filled = sem("scratch_filled")
        SCRATCH_FILLED = 16 * (2 + 2 * BATCH)
        rows_sent = [sem(f"rows_sent{n}") for n in range(3)]
        rows_back = [sem(f"rows_back{n}") for n in range(3)]
        rows_stored = [sem(f"rows_stored{n}") for n in range(3)]

        def send_rows(pool, layer):
            if layer == 0:
                pool.wait_ge(rows_zeroed, 16)
            else:
                pool.wait_ge(scratch_filled, SCRATCH_FILLED)
            for k in range(1 if layer == 0 else 2):
                if layer > 0 and k == 0:
                    pool.wait_ge(route_first, layer)
                else:
                    pool.wait_ge(route_slots, layer + 1)
                for t in range(TILES):
                    pool.indirect_dma_start(
                        out=rows_in[layer], out_offset=bass.IndirectOffsetOnAxis(ap=slots[:, k, t:t + 1].bitcast(U32), axis=0),
                        in_=xn[:, t, :], in_offset=None).then_inc(rows_sent[layer], 16)

        def fetch_rows(pool, layer, stores):
            pool.wait_ge(rows_stored[layer], 16 * stores)
            for k in range(1 if layer == 0 else 2):
                for t in range(TILES):
                    n = 2 if layer == 0 else k
                    pool.indirect_dma_start(
                        out=fetched[layer][:, k, t, :], out_offset=None,
                        in_=rows_out[layer], in_offset=bass.IndirectOffsetOnAxis(ap=slots[:, n, t:t + 1].bitcast(U32), axis=0))\
                        .then_inc(rows_back[layer], 16)
                    yield

        loaded = [sem(f"loaded{n}") for n in range(4)]
        LOADED_BEFORE = {1: 96, 2: (96 + 64, 96 + 32, 96 + 32, 96 + 32)}

        w1_buf = l0("w1_buf", [P, 4, F])
        w2_buf = l0("w2_buf", [P, 4, F // P, D])
        y80 = l0("y80", [PART, 2, 4, D])
        f0 = Region(q_heads_at, attT_end)
        x80 = f0("x80", [PART, 4, 4, D])
        x80T = f0("x80T", [P, 2, CAP])
        hT0 = f0("hT0", [P, 2, F // P, CAP])
        f0_turned = sem("f0_turned")
        f0_xT = sem("f0_xT")
        f0_up = sem("f0_up")
        f0_hidden = sem("f0_hidden")
        f0_down = sem("f0_down")
        f0_copied = sem("f0_copied")

        def experts0_sync(sp):
            sp.wait_ge(rows_sent[0], 16 * TILES)
            sp.wait_ge(l0_scores, BT)
            with sp.Fori(0, 2) as i:
                for n in range(4):
                    e = sp.snap(4 * i + n)
                    at = sp.snap(e * D)
                    sp.wait_ge(f0_down, 4 * i + n + 1)
                    sp.dma_start(x80[:, n, :, :], rows_in[0][bass.ds(e * CAP, CAP), :].rearrange("(j p) d -> p j d", p=PART))\
                        .then_inc(loaded[n], 16)
                    sp.dma_start(w1_buf[:, n, :], a["L0_ffn_W1"][bass.ds(at, D), :]).then_inc(loaded[n], 16)
                    sp.dma_start(w2_buf[:, n, :, :], a["L0_ffn_W2"][bass.ds(e * F, F), :].rearrange("(c p) d -> p c d", p=P))\
                        .then_inc(loaded[n], 16)

        def experts0_tensor(pe):
            pe.sem_inc(f0_down, 4)
            pe.sem_inc(f0_copied, 2)
            with pe.Fori(0, 2) as i:
                for pair in range(2):
                    e = 4 * i + 2 * pair
                    for n in range(2):
                        m = 2 * pair + n
                        pe.wait_ge(loaded[m], 48 * i + 48)
                        if n == 1:
                            pe.wait_ge(f0_copied, e + 2)
                        for j in range(4):
                            ins = pe.transpose(banks[:, (4, 7)[n], j * PART:(j + 1) * PART], x80[:, m, j, :], C["ident"][0:PART, 0:PART])
                        ins.then_inc(f0_turned, 1)
                        pe.wait_ge(f0_xT, e + n + 1)
                        if n == 1:
                            pe.wait_ge(f0_hidden, 4 * e + 4)
                        for c in range(F // P):
                            pe.matmul(banks[:, c, 0:CAP], w1_buf[:, 2 * pair + n, c * P:(c + 1) * P], x80T[:, n, :],
                                      start=True, stop=True).then_inc(f0_up, 1)
                    for n in range(2):
                        if n == 1:
                            pe.wait_ge(f0_hidden, 4 * e + 8)
                        for j in range(4):
                            for c in range(F // P):
                                ins = pe.matmul(banks[0:PART, (5, 7)[n], j * D:(j + 1) * D], hT0[:, n, c, j * PART:(j + 1) * PART],
                                                w2_buf[:, 2 * pair + n, c, :], start=(c == 0), stop=(c == F // P - 1))
                        ins.then_inc(f0_down, 1)
            pe.wait_ge(f0_copied, 8 + 2)

        def experts0_scalar(act):
            with act.Fori(0, 4) as i:
                for n in range(2):
                    act.wait_ge(f0_turned, 2 * i + n + 1)
                    act.activation(x80T[:, n, :], banks[:, (4, 7)[n], 0:CAP], ACT.Copy).then_inc(f0_xT, 1)
                    for c in (0, 2):
                        act.wait_ge(f0_up, 4 * (2 * i + n) + c + 1)
                        act.activation(hT0[:, n, c, :], banks[:, c, 0:CAP], ACT.Relu).then_inc(f0_hidden, 1)

        def experts0_vector(dve):
            dve.sem_inc(outputs_free, 1)
            with dve.Fori(0, 4) as i:
                for n in range(2):
                    for c in (1, 3):
                        dve.wait_ge(f0_up, 4 * (2 * i + n) + c + 1)
                        dve.tensor_scalar(hT0[:, n, c, :], banks[:, c, 0:CAP], 0.0, None, ALU.max).then_inc(f0_hidden, 1)
                dve.wait_ge(outputs_free, stored_before[0] + i + 1)
                for n in range(2):
                    dve.wait_ge(f0_down, 2 * i + n + 5)
                    dve.tensor_copy(y80[:, n, :, :], banks[0:PART, (5, 7)[n], :].rearrange("p (j d) -> p j d", d=D))\
                        .then_inc(f0_copied, 1)

        def experts0_gpsimd(pool):
            with pool.Fori(0, 4) as i:
                for n in range(2):
                    pool.wait_ge(f0_copied, 2 * i + n + 3)
                    pool.dma_start(rows_out[0][bass.ds((2 * i + n) * CAP, CAP), :].rearrange("(j p) d -> p j d", p=PART),
                                   y80[:, n, :, :]).then_inc(rows_stored[0], 16)
                pool.wait_ge(rows_stored[0], 32 * i + 32)
                pool.sem_inc(outputs_free, 1)

        mix_ready = sem("mix_ready")
        mix_sigmoid = sem("mix_sigmoid")

        def gate_vector(dve, step, layer):
            gate_first_vector(dve, step, layer)
            gate_second_vector(dve, step, layer)
            gate_sum_vector(dve, layer)

        def expert_weight(n):
            return bcast(weights[:, n, :].unsqueeze(2), (P, TILES, D))

        def gate_first_vector(dve, step, layer):
            dve.wait_ge(rows_back[layer], 16 * TILES * (1 if layer == 0 else 2))
            rows = fetched[layer]
            step(dve.tensor_tensor(rows[:, 0, :, :], rows[:, 0, :, :], expert_weight(0), ALU.mult))

        def gate_second_vector(dve, step, layer):
            rows = fetched[layer]
            if layer == 2:
                step(dve.tensor_tensor(rows[:, 0, :, :], rows[:, 0, :, :], g_out[:, :, :], ALU.add))
            other = xn[:, :, :] if layer == 0 else rows[:, 1, :, :]
            step(dve.tensor_tensor(g_out[:, :, :], other, expert_weight(1), ALU.mult))

        def gate_sum_vector(dve, layer):
            dve.tensor_tensor(g_out[:, :, :], g_out[:, :, :], fetched[layer][:, 0, :, :], ALU.add).then_inc(mix_ready, 1)

        def gate_scalar(act, layer):
            act.wait_ge(mix_ready, layer + 1)
            act.activation(xn[:, :, :], g_out[:, :, :], ACT.Sigmoid).then_inc(mix_sigmoid, 1)

        def gate_silu_vector(dve, step, layer):
            dve.wait_ge(mix_sigmoid, layer + 1)
            step(dve.tensor_tensor(g_out[:, :, :], g_out[:, :, :], xn[:, :, :], ALU.mult))

        def mix_vector(dve, step, layer, s_of):
            def new_x(b):
                tiles = slice(BT * b, BT * b + BT)
                s_b, read, value = s_of(b)
                ins = dve.tensor_tensor(s_out[:, tiles, :], s_b, g_out[:, tiles, :], ALU.mult)
                if read:
                    ins.then_inc(read, 1)
                    dve.wait_ge(read, value)
                else:
                    step(ins)
                ins = dve.tensor_tensor(x[:, tiles, :], x[:, tiles, :], s_out[:, tiles, :], ALU.add)
                if layer < 3:
                    step(ins)
                else:
                    ins.then_inc(x_final, 1)

            if layer < 3:
                norm_vector(dve, step, layer + 1, new_x)
            else:
                for b in range(BATCH):
                    new_x(b)

        at = Region(0, LATE)
        stack_q = at("stack_q", [P, H1, SEQ], BF16)
        stack_k = at("stack_k", [P, H1, SEQ], BF16)
        wqkv = at("wqkv", [P, 3, P])
        wout = at("wout", [P, P])
        qk_bias = at("qk_bias", [P, 2])
        v_bias = at("v_bias", [P, P])
        out_bias = at("out_bias", [P, P])
        v_all = at("v_all", [P, TILES, D])
        v_now = at("v_now", [P, 4, BT, 4, D1 + 1])
        neg_max = at("neg_max", [P, 2, BT, 4])
        max_rest = at("max_rest", [P, BT, 4])
        max_parts = at("max_parts", [P, BT, 3, 4], BF16)
        max_rows = at("max_rows", [3 * 4, SEQ], BF16)
        o_T = at("o_T", [P, SEQ])
        o_rec = at("o_rec", [P, BT, 4])
        oT = at("oT", [P, 2, SEQ])
        loop_a = Region(at.at, LATE)
        prob_at = at.at
        prob = at("prob", [P, 4, 1280])
        xb1 = loop_a("xb1", [P, SEQ])
        qk = loop_a("qk", [P, 2, SEQ])
        parts = loop_a("parts", [P, 2, 2, 3, SEQ], BF16)
        o_tok = squares
        identb = sb("identb", [P, P], BF16)
        onesb = sb("onesb", [P, P], BF16)
        negb = sb("negb", [P, 4, P], BF16)
        negTb = sb("negTb", [P, 2, P], BF16)
        q_rows, k_rows = scratch["q_rows"], scratch["k_rows"]
        PER_CHANNEL = 7
        ROWS = PER_CHANNEL * D1
        SHIFT_ROWS = slice(6, 6 + 2 * PER_CHANNEL + 1, PER_CHANNEL)

        at_weights = sem("at_weights")
        at_x_copied = sem("at_x_copied")
        at_projected = sem("at_projected")
        at_biased = sem("at_biased")
        at_parts = sem("at_parts")
        onesb_set = sem("onesb_set")
        at_rows_stored = [sem(f"at_rows_stored{n}") for n in range(2)]
        at_stacks_set = sem("at_stacks_set")
        at_loaded = [sem(f"at_loaded{n}") for n in range(4)]
        at_scores_a = sem("at_scores_a")
        at_max = sem("at_max")
        at_own = sem("at_own")
        at_max_split = sem("at_max_split")
        at_max_turned = sem("at_max_turned")
        at_max_rows = sem("at_max_rows")
        at_max_moved = sem("at_max_moved")
        at_scores = sem("at_scores")
        at_exp = sem("at_exp")
        at_values = sem("at_values")
        at_o_back = sem("at_o_back")
        at_sums_zero = sem("at_sums_zero")
        at_o_read = sem("at_o_read")
        at_v_now = sem("at_v_now")
        at_oT_copied = sem("at_oT_copied")
        at_o_turned = sem("at_o_turned")
        at_oT = sem("at_oT")
        at_s = sem("at_s")
        at_s_copied = sem("at_s_copied")

        GROUPS = 16
        EXPERTS3_TILES = [range(0, 3), range(3, 7), range(7, 9), range(9, TILES)]
        STORES = 16 * 6
        FILLS = [(0, 0, 4), (1, 0, 2), (1, 2, 2)] + [(qt, h, 1) for qt in (2, 3) for h in range(4)]
        FILL_BANKS = [0, 1, 2] * 3 + [0, 1]
        NF = len(FILLS)
        UNITS = [("x", 0), ("y", 0), ("x", 1), ("y", 1), ("c", 0), ("x", 2), ("y", 2), ("x", 3), ("y", 3), ("c", 2)]
        UNIT_BANKS = [4, 5, 6] * 3 + [5]
        NU = len(UNITS)

        def last_use(bank_list, n):
            for back in range(1, len(bank_list) + 1):
                if bank_list[n - back] == bank_list[n]:
                    return n - back + 1

        class Step:

            def __init__(self, t, turn, run):
                self.t, self.turn, self.run = t, turn, run
                self.has = {"A": t < GROUPS, "M": 1 <= t <= GROUPS, "B": 2 <= t <= GROUPS + 1, "O": 3 <= t}

            def count(self, of_run, rate):
                known = of_run + rate * GROUPS * self.run
                return known if self.turn is None else known + self.turn * (4 * rate)

        def all_steps(eng, run):
            for t in range(3):
                yield Step(t, None, run)
            with eng.Fori(0, 3) as i:
                for t in range(3, 7):
                    yield Step(t, i, run)
            for t in range(15, GROUPS + 3):
                yield Step(t, None, run)

        def project_sync(sp, run):
            layer = 2 * run + 1
            sp.wait_ge(norm_centered, BATCH * layer + 4)
            sp.dma_start(wqkv, a[f"wqkv{layer}"]).then_inc(at_weights, 16)
            sp.dma_start(wout, a[f"wout{layer}"]).then_inc(at_weights, 16)
            sp.dma_start(qk_bias, a[f"qk_bias{layer}"]).then_inc(at_weights, 16)
            sp.dma_start(v_bias, a[f"v_bias{layer}"].partition_broadcast(P)).then_inc(at_weights, 16)
            sp.dma_start(out_bias, a[f"out_bias{layer}"].partition_broadcast(P)).then_inc(at_weights, 16)
            for b in range(BATCH):
                n = b % 2
                sp.wait_ge(at_parts, BATCH * run + b + 1)
                for w, rows in enumerate((q_rows, k_rows)):
                    for k_part, first in enumerate((0, 3, 5)):
                        times = 3 - k_part
                        to = rows[b, :, first:first + times, :]
                        source = parts[:, n, 0, 0:times, :] if w == 0 else \
                            bcast(parts[:, n, 1, k_part, :].unsqueeze(1), (P, times, SEQ))
                        sp.dma_start(to, source).then_inc(at_rows_stored[n], 16)
                if run == 1 and b == 2:
                    first_stacks_sync(sp, run)

        def stack_loader(sp):
            def load(slot, batch):
                heads = slice(4 * slot, 4 * slot + 4)
                at_b = bass.ds(batch, 1) if not isinstance(batch, int) else slice(batch, batch + 1)
                for stack, rows in ((stack_q, q_rows), (stack_k, k_rows)):
                    sp.dma_start(stack[0:ROWS, heads, :],
                                 rows[at_b, 4 * slot * D1:(4 * slot + 4) * D1, :, :].rearrange("o (h i) r s -> (o i r) h s", i=D1))\
                        .then_inc(at_loaded[slot], 16)
            return load

        def first_stacks_sync(sp, run):
            load = stack_loader(sp)
            sp.wait_ge(at_rows_stored[0], STORES * (2 * run + 2))
            sp.wait_ge(at_stacks_set, 3 * run + 3)
            for slot in range(4):
                load(slot, 0)

        def attend_sync(sp, run, steps):
            load = stack_loader(sp)
            for n in range(2):
                sp.wait_ge(at_rows_stored[n], STORES * (2 * (run + 1) + 1))
            for st in steps:
                t = st.t
                if st.turn is not None and t + 1 >= 4:
                    batch = sp.snap(st.turn + (t + 1) // 4)
                if st.has["M"]:
                    heads = slice(4 * ((t - 1) % 4), 4 * ((t - 1) % 4) + 4)
                    sp.wait_ge(at_max_rows, st.count(t, 1))
                    sp.dma_start(stack_q[SHIFT_ROWS, heads, :].rearrange("r h s -> r (h s)"), max_rows)\
                        .then_inc(at_max_moved, 16)
                if 4 <= t + 1 < GROUPS:
                    sp.wait_ge(at_exp, st.count(NU * (t - 2), NU))
                    load((t + 1) % 4, batch if st.turn is not None else (t + 1) // 4)

        def values_of(pool, batch, slot):
            pool.tensor_copy(v_now[:, slot, :, :, 0:D1],
                             v_all[:, bass.ds(batch * BT, BT), 4 * slot * D1:(4 * slot + 4) * D1]
                             .rearrange("p t (h e) -> p t h e", e=D1)).then_inc(at_v_now, 1)

        def set_stacks(pool):
            pool.memset(stack_q, 0.0).then_inc(at_stacks_set, 1)
            pool.memset(stack_k, 1.0).then_inc(at_stacks_set, 1)
            pool.memset(v_now, 1.0).then_inc(at_stacks_set, 1)

        def project_gpsimd(pool, run):
            B0 = BATCH * run

            pool.wait_ge(at_stacks_set, 3 * run + 3)
            pool.wait_ge(at_biased, B0 + BATCH + 2)
            for slot in range(4):
                values_of(pool, 0, slot)

        def attend_gpsimd(pool, run):
            with pool.Fori(1, BATCH) as b:
                for slot in range(4):
                    pool.wait_ge(at_values, 4 * (b - 1) + slot + 1 + 16 * run)
                    values_of(pool, b, slot)

        def project_tensor(pe, run):
            pe.wait_ge(at_weights, 80 * (run + 1))
            with pe.Fori(2 * run, 2 * run + 2) as i:
                for m in range(2):
                    b = 2 * i + m
                    pe.wait_ge(at_x_copied, b + 1)
                    if m == 1 and run == 0:
                        pe.wait_ge(route_read, 1)
                    pe.wait_ge(at_biased, b + 1)
                    for n in range(2):
                        pe.matmul(banks[:, 3 * m + n, :], wqkv[:, n, :], xb1, start=True, stop=True)
                    for t in range(BT):
                        ins = pe.matmul(banks[:, 3 * m + 2, t * P:(t + 1) * P], xb1[:, t * P:(t + 1) * P], wqkv[:, 2, :],
                                        start=True, stop=True)
                    ins.then_inc(at_projected, 1)

        def attend_tensor(pe, run, steps):

            def stage_a(st, which):
                slot = st.t % 4
                for n in which:
                    qt, first, heads = FILLS[n]
                    bank, length = FILL_BANKS[n], (qt + 1) * P
                    if n == 0:
                        pe.wait_ge(at_loaded[slot], 32 * (st.t // 4 + 1 + 4 * run) + (0 if st.turn is None else st.turn * 32))
                    used = NF * st.t + last_use(FILL_BANKS, n)
                    if used > 0 or run:
                        pe.wait_ge(at_max, st.count(used, NF))
                    for g in range(heads):
                        h = 4 * slot + first + g
                        pe.matmul(banks[:, bank, g * length:(g + 1) * length], stack_q[:, h, qt * P:(qt + 1) * P],
                                  stack_k[:, h, 0:length], start=(g == 0), stop=False)
                    diagonal = banks[:, bank, 0:heads * length].rearrange("p (g l) -> p g l", g=heads)[:, :, length - P:length]
                    pe.matmul(diagonal, identb[:, :], negb[:, 0:heads, :], start=False, stop=True).then_inc(at_scores_a, 1)

            def stage_m(st):
                if st.t > 3 or run:
                    pe.wait_ge(at_o_read, st.count(st.t - 3, 1) if st.t > 3 else GROUPS)
                pe.wait_ge(at_max_split, st.count(st.t, 1))
                for qt in range(BT):
                    ins = pe.matmul(banks[0:3 * 4, 3, qt * P:(qt + 1) * P], max_parts[:, qt, :, :].rearrange("p n h -> p (n h)"),
                                    identb[:, :], start=True, stop=True)
                ins.then_inc(at_max_turned, 1)

            def scores_b(st, n):
                kind, e = UNITS[n]
                bank = UNIT_BANKS[n]
                h = 4 * ((st.t - 2) % 4) + e
                if n == 0:
                    pe.wait_ge(at_max_moved, st.count(16 * (st.t - 1), 16))
                used = NU * (st.t - 2) + last_use(UNIT_BANKS, n)
                if used > 0 or run:
                    pe.wait_ge(at_exp, st.count(used, NU))

                def keys(kt, h, col, start):
                    pe.matmul(banks[:, bank, col:col + SEQ - kt * P], stack_k[:, h, kt * P:(kt + 1) * P],
                              stack_q[:, h, kt * P:SEQ], start=start, stop=False)

                if kind == "x":
                    keys(0, h, 0, True)
                    masked, rows = banks[:, bank, 0:P], negTb[:, 0, :]
                else:
                    if kind == "y":
                        keys(1, h, 0, True)
                        keys(3, h, 384, False)
                    else:
                        keys(2, h, 0, True)
                        keys(2, h + 1, 256, False)
                    apart = 3 if kind == "y" else 2
                    masked = banks[:, bank, :].rearrange("p (a c) -> p a c", c=P)[:, 0:4:apart, :]
                    rows = negTb[:, :, :]
                pe.matmul(masked, identb[:, :], rows, start=False, stop=True).then_inc(at_scores, 1)

            def values(st):
                slot = (st.t - 2) % 4
                pe.wait_ge(at_exp, st.count(NU * (st.t - 1), NU))
                pe.wait_ge(at_v_now, st.count(st.t - 1, 1))
                if st.t == 2:
                    pe.wait_ge(at_sums_zero, run + 1)
                if st.t > 2 or run:
                    pe.wait_ge(at_oT_copied, st.count(st.t - 2, 1))
                for kt, col in ((0, 0), (1, 512), (2, 1024), (3, 896)):
                    for e in range(4):
                        ins = pe.matmul(banks[32 * e:32 * e + D1 + 1, 7, kt * P:SEQ], v_now[:, slot, kt, e, :],
                                        prob[:, e, col:col + SEQ - kt * P], start=(kt == 0), stop=(kt == 3))
                ins.then_inc(at_values, 1)

            def stage_o(st):
                if st.has["M"]:
                    pe.wait_ge(at_max_rows, st.count(st.t, 1))
                else:
                    pe.wait_ge(at_o_read, st.count(st.t - 3, 1))
                pe.wait_ge(at_oT_copied, st.count(st.t - 2, 1))
                for qt in range(BT):
                    ins = pe.transpose(banks[:, 3, qt * P:(qt + 1) * P], o_T[:, qt * P:(qt + 1) * P], C["ident"])
                ins.then_inc(at_o_back, 1)

            for st in steps:
                def a(*which):
                    if st.has["A"]:
                        stage_a(st, which)

                def b(*which):
                    if st.has["B"]:
                        for n in which:
                            scores_b(st, n)

                b(0, 1)
                a(0, 1)
                b(2, 3)
                a(2)
                b(4)
                if st.has["M"]:
                    stage_m(st)
                a(3, 4)
                b(5, 6)
                a(5)
                if st.has["O"]:
                    stage_o(st)
                b(7, 8)
                a(6, 7)
                b(9)
                a(8, 9, 10)
                if st.has["B"]:
                    values(st)
                if run == 1 and st.t >= GROUPS:
                    experts3_tensor(pe, EXPERTS3_TILES[st.t - GROUPS])
        def project_out_tensor(pe, run):
            B0 = BATCH * run

            def project_out(b):
                if b == 0:
                    pe.wait_ge(at_o_read, GROUPS * (run + 1))
                if b >= 2:
                    pe.wait_ge(at_oT, B0 + b - 1)
                for t in range(BT):
                    ins = pe.transpose(banks[:, (6, 4)[b % 2], t * P:(t + 1) * P], o_tok[:, BT * b + t, :], C["ident"])
                ins.then_inc(at_o_turned, 1)
                pe.wait_ge(at_oT, B0 + b + 1)
                if b >= 2:
                    pe.wait_ge(at_s_copied, B0 + b - 1)
                for t in range(BT):
                    ins = pe.matmul(banks[:, (3, 5)[b % 2], t * P:(t + 1) * P], oT[:, b % 2, t * P:(t + 1) * P], wout,
                                    start=True, stop=True)
                ins.then_inc(at_s, 1)

            project_out(0)
            project_out(1)
            if run == 1:
                experts3_tensor(pe, EXPERTS3_TILES[-1])
            project_out(2)
            project_out(3)

        def project_vector(dve, step, run):
            B0 = BATCH * run
            dve.wait_ge(at_weights, 80 * (run + 1))
            if run == 0:
                dve.sem_inc(at_biased, 2)
                for n in range(2):
                    dve.sem_inc(at_rows_stored[n], STORES)
            with step.loop_from(2 * run, 2, 8) as i:
                for n in range(2):
                    b = 2 * i + n
                    dve.wait_ge(at_projected, b + 1)
                    dve.tensor_scalar(qk[:, 0, :], banks[:, 3 * n, :], qk_bias[:, 0:1], float(D1) ** -0.5, ALU.add, ALU.mult)
                    dve.tensor_scalar(qk[:, 1, :], banks[:, 3 * n + 1, :], qk_bias[:, 1:2], None, ALU.add)
                    dve.tensor_tensor(v_all[:, bass.ds((b - B0) * BT, BT), :],
                                      banks[:, 3 * n + 2, :].rearrange("p (t d) -> p t d", d=D),
                                      bcast(v_bias.unsqueeze(1), (P, BT, D)), ALU.add).then_inc(at_biased, 1)
                    dve.wait_ge(at_biased, b + 3)
                    dve.wait_ge(at_rows_stored[n], STORES * i + STORES)
                    part = parts[:, n, :, :, :]
                    step(dve.tensor_copy(part[:, :, 0, :], qk))
                    step(dve.tensor_tensor(qk, qk, part[:, :, 0, :], ALU.subtract))
                    step(dve.tensor_copy(part[:, :, 1, :], qk))
                    step(dve.tensor_tensor(qk, qk, part[:, :, 1, :], ALU.subtract))
                    dve.tensor_copy(part[:, :, 2, :], qk).then_inc(at_parts, 1)
                    dve.wait_ge(at_parts, b + 1)

        def attend_vector(dve, step, run, steps):

            def stage_a(st, which):
                for n in which:
                    qt, first, heads = FILLS[n]
                    bank, length = FILL_BANKS[n], (qt + 1) * P
                    dve.wait_ge(at_scores_a, st.count(NF * st.t + n + 1, NF))
                    if n == 0 and (st.t > 1 or run):
                        dve.wait_ge(at_max_split, st.count(st.t - 1, 1) if st.t > 1 else GROUPS)
                    dve.tensor_reduce(neg_max[:, st.t % 2, qt, first:first + heads],
                                      banks[:, bank, 0:heads * length].rearrange("p (g l) -> p g l", g=heads),
                                      X, ALU.max, negate=True).then_inc(at_max, 1)

            def stage_m(st, own):
                dve.wait_ge(at_max, st.count(NF * st.t, NF))
                if st.t > 1 or run:
                    dve.wait_ge(at_max_turned, st.count(st.t - 1, 1))
                rest = neg_max[:, (st.t - 1) % 2, :, :]
                own(dve.tensor_copy(max_parts[:, :, 0, :], rest))
                own(dve.tensor_tensor(max_rest, rest, max_parts[:, :, 0, :], ALU.subtract))
                own(dve.tensor_copy(max_parts[:, :, 1, :], max_rest))
                own(dve.tensor_tensor(max_rest, max_rest, max_parts[:, :, 1, :], ALU.subtract))
                dve.tensor_copy(max_parts[:, :, 2, :], max_rest).then_inc(at_max_split, 1)

            def stage_o(st, own):
                t = st.t - 3
                dve.wait_ge(at_o_back, st.count(t + 1, 1))
                if t > 0 or run:
                    dve.wait_ge(at_o_read, st.count(t, 1))
                o = banks[:, 3, :].rearrange("p (t h r) -> p t h r", t=BT, h=4)
                own(dve.reciprocal(o_rec, o[:, :, :, D1]))
                tiles = slice(BT * (t // 4), BT * (t // 4) + BT) if st.turn is None else bass.ds(BT * (t // 4 + st.turn), BT)
                dve.tensor_tensor(o_tok[:, tiles, 4 * (t % 4) * D1:(4 * (t % 4) + 4) * D1].rearrange("p t (h e) -> p t h e", e=D1),
                                  o[:, :, :, 0:D1], bcast(o_rec.unsqueeze(3), (P, BT, 4, D1)), ALU.mult).then_inc(at_o_read, 1)

            dve.memset(banks[:, 7, :], 0.0).then_inc(at_sums_zero, 1)
            OWN = 5
            def before(t):
                return 4 * min(max(t - 1, 0), GROUPS) + min(max(t - 3, 0), GROUPS)

            for st in steps:
                made = [before(st.t)]

                def own(ins):
                    ins.then_inc(at_own, 1)
                    made[0] += 1
                    dve.wait_ge(at_own, st.count(made[0], OWN))

                if st.has["M"]:
                    stage_m(st, own)
                if st.has["A"]:
                    stage_a(st, range(0, 6))
                if st.has["O"]:
                    stage_o(st, own)
                if st.has["A"]:
                    stage_a(st, range(6, NF))
                if run == 0 and st.t == GROUPS:
                    gate_vector(dve, step, 1)
                if run == 0 and st.t == GROUPS + 2:
                    gate_silu_vector(dve, step, 1)
                if run == 1 and st.t == GROUPS:
                    routing_vector(dve, step, 3, read=False)
                if run == 1 and st.t >= GROUPS:
                    experts3_vector(dve, EXPERTS3_TILES[st.t - GROUPS])
                if run == 1 and st.t == GROUPS + 2:
                    attention_bias_vector(dve, 0)
                    attention_bias_vector(dve, 1)
                    experts3_vector(dve, EXPERTS3_TILES[-1])

        def attention_out(b):
            return banks[:, (3, 5)[b % 2], :].rearrange("p (t d) -> p t d", d=D)

        def attention_bias_vector(dve, b):
            dve.wait_ge(at_s, BATCH + b + 1)
            dve.tensor_tensor(s_out[:, BT * b:BT * b + BT, :], attention_out(b), bcast(out_bias.unsqueeze(1), (P, BT, D)), ALU.add)\
                .then_inc(at_s_copied, 1)

        def attention_s(dve, run, b):
            if run == 0:
                dve.wait_ge(at_s, b + 1)
                return attention_out(b), at_s_copied, b + 1
            if b >= 2:
                attention_bias_vector(dve, b)
            dve.wait_ge(at_s_copied, BATCH + b + 1)
            dve.wait_ge(f3_silu, b + 1)
            return s_out[:, BT * b:BT * b + BT, :], None, None

        def project_scalar(act, run):
            B0 = BATCH * run
            act.wait_ge(xnT_ready, 8 * run + 8)
            if run == 0:
                act.activation(xb1, xnT[:, 0:SEQ], ACT.Copy).then_inc(at_x_copied, 1)
            with act.Fori(B0 + 1, B0 + BATCH) as b:
                act.wait_ge(at_projected, b)
                act.activation(xb1, xnT[:, bass.ds((b - B0) * SEQ, SEQ)], ACT.Copy).then_inc(at_x_copied, 1)

        def attend_scalar(act, run, steps):
            def rows(st):
                if st.t > 1 or run:
                    act.wait_ge(at_max_moved, st.count(16 * (st.t - 1), 16))
                act.wait_ge(at_max_turned, st.count(st.t, 1))
                act.activation(max_rows, banks[0:3 * 4, 3, :], ACT.Copy).then_inc(at_max_rows, 1)

            def exponential(st, n):
                kind, e = UNITS[n]
                act.wait_ge(at_scores, st.count(NU * (st.t - 2) + n + 1, NU))
                if n == 0 and (st.t > 2 or run):
                    act.wait_ge(at_values, st.count(st.t - 2, 1))
                if kind == "c":
                    to, scores = prob[:, e:e + 2, 1024:1280], banks[:, UNIT_BANKS[n], :].rearrange("p (e c) -> p e c", e=2)
                else:
                    at_col = 0 if kind == "x" else 512
                    to, scores = prob[:, e, at_col:at_col + 512], banks[:, UNIT_BANKS[n], :]
                act.activation(to, scores, ACT.Exp).then_inc(at_exp, 1)

            for st in steps:
                if st.has["B"]:
                    for n in range(5):
                        exponential(st, n)
                if st.has["M"]:
                    rows(st)
                if st.has["B"]:
                    for n in range(5, NU):
                        exponential(st, n)
                    act.wait_ge(at_values, st.count(st.t - 1, 1))
                    if st.has["O"]:
                        act.wait_ge(at_o_back, st.count(st.t - 2, 1))
                    act.activation(o_T, banks[:, 7, :], ACT.Copy).then_inc(at_oT_copied, 1)
                if run == 0 and st.t == GROUPS + 1:
                    gate_scalar(act, 1)
                if run == 1 and st.t >= GROUPS:
                    experts3_scalar(act, EXPERTS3_TILES[st.t - GROUPS])

        def project_out_scalar(act, run):
            B0 = BATCH * run
            for b in range(BATCH):
                if run == 1 and b == 2:
                    first, end = EXPERTS3_TILES[-1][0], EXPERTS3_TILES[-1][-1] + 1
                    experts3_gate_scalar(act, 0)
                    experts3_gate_scalar(act, 1)
                    experts3_scalar(act, range(first, end - 2))
                    experts3_gate_scalar(act, 2)
                    experts3_scalar(act, range(end - 2, end))
                act.wait_ge(at_o_turned, B0 + b + 1)
                if b >= 2:
                    act.wait_ge(at_s, B0 + b - 1)
                act.activation(oT[:, b % 2, :], banks[:, (6, 4)[b % 2], :], ACT.Copy).then_inc(at_oT, 1)
            if run == 1:
                experts3_gate_scalar(act, 3)

        f1w = Region(LATE)
        w1_all = f1w("w1_all", [P, 8, F])
        w2_all = f1w("w2_all", [P, 8, F // P, D])
        b1T_all = f1w("b1T_all", [P, 8, F // P])
        b2_all = f1w("b2_all", [P, 8, D])
        w1_now = f1w("w1_now", [P, 4, F])
        hidT = f1w("hidT", [P, 4, F])
        f1 = Region(prob_at, LATE)
        rows4 = squares.rearrange("p (n j) d -> p n j d", n=4)
        rowsT = f1("rowsT", [P, 2, 4, P])
        hid = f1("hid", [P, 4, F // P, P])
        out4 = f1("out4", [P, 2, 4, D])
        f1_weights = sem("f1_weights")
        f1_turned = sem("f1_turned")
        f1_rowsT = sem("f1_rowsT")
        f1_up = sem("f1_up")
        f1_hid = sem("f1_hid")
        f1_w1 = sem("f1_w1")
        f1_hidT = sem("f1_hidT")
        f1_down = sem("f1_down")
        f1_out = sem("f1_out")

        def experts1_weights(sp):
            sp.dma_start(w1_all, a["L1_ffn_W1"].rearrange("(e p) f -> p e f", p=P)).then_inc(f1_weights, 16)
            sp.dma_start(w2_all, a["L1_ffn_W2"].rearrange("(e c p) d -> p e c d", e=8, p=P)).then_inc(f1_weights, 16)
            sp.dma_start(b1T_all, a["L1_b1T"]).then_inc(f1_weights, 16)
            sp.dma_start(b2_all.rearrange("p e d -> p (e d)"), a["L1_ffn_b2"].partition_broadcast(P)).then_inc(f1_weights, 16)

        def experts1_sync(sp):
            sp.wait_ge(rows_sent[1], 16 * TILES * 2)
            sp.wait_ge(at_parts, BATCH)
            with sp.Fori(0, PASSES[1]) as i:
                for n in range(GROUPS1):
                    row = sp.snap((GROUPS1 * i + n) * 4 * P)
                    sp.wait_ge(f1_turned, GROUPS1 * i + (4, 1, 2, 3, 5)[n])
                    sp.dma_start(rows4[:, n % 4, :, :], rows_in[1][bass.ds(row, 4 * P), :].rearrange("(j p) d -> p j d", p=P))\
                        .then_inc(loaded[n % 4], 16)

        def experts_of(eng, layer, first, count):
            _, values = nc.values_load_multi_w_load_instructions(
                tile_expert[0:1, layer - 1, bass.ds(first, count)], engines=[eng.engine], min_val=0, max_val=EXPERTS[layer] - 1)
            return values

        def experts1_tensor(pe):
            pe.wait_ge(at_biased, BATCH + 2)
            pe.sem_inc(f1_turned, 4)
            pe.wait_ge(f1_weights, 64)
            pe.wait_ge(route_slots, 2)
            with pe.Fori(0, PASSES[1]) as i:
                def turn(n):
                    if n % 4 == 0:
                        pe.wait_ge(loaded[0], LOADED_BEFORE[1] + 32 * i + (16 if n == 0 else 32))
                    else:
                        pe.wait_ge(loaded[n], LOADED_BEFORE[1] + 16 * i + 16)
                    for j in range(4):
                        ins = pe.transpose(banks[:, (0, 7)[n % 2], j * P:(j + 1) * P], rows4[:, n % 4, j, :], C["ident"])
                    ins.then_inc(f1_turned, 1)

                def up(k):
                    if k % 4 == 0:
                        pe.wait_ge(f1_rowsT, GROUPS1 * i + k // 4 + 1)
                    pe.wait_ge(f1_w1, 4 * GROUPS1 * i + k + 1)
                    for c in range(F // P):
                        ins = pe.matmul(banks[:, 1 + k % 4, c * P:(c + 1) * P], w1_now[:, k % 4, c * P:(c + 1) * P],
                                        rowsT[:, k // 4 % 2, k % 4, :], start=True, stop=True)
                    ins.then_inc(f1_up, 1)

                def down(k):
                    pe.wait_ge(f1_hidT, 4 * GROUPS1 * i + k + 1)
                    for c in range(F // P):
                        ins = pe.matmul(banks[:, 5 + k // 4 % 2, (k % 4) * D:(k % 4 + 1) * D], hidT[:, k % 4, c * P:(c + 1) * P],
                                        w2_all[:, bass.ds(experts[k], 1), c, :].rearrange("p a d -> p (a d)"),
                                        start=(c == 0), stop=(c == F // P - 1))
                    ins.then_inc(f1_down, 1)

                turn(0)
                experts = experts_of(pe, 1, 4 * GROUPS1 * i, 4 * GROUPS1)
                for k in range(4 * GROUPS1):
                    up(k)
                    if k % 4 == 1 and k // 4 + 1 < GROUPS1:
                        turn(k // 4 + 1)
                    if k >= 2:
                        down(k - 2)
                down(4 * GROUPS1 - 2)
                down(4 * GROUPS1 - 1)
            pe.wait_ge(f1_out, 40)

        def experts1_vector(dve):
            with dve.Fori(0, PASSES[1]) as i:
                experts = experts_of(dve, 1, 4 * GROUPS1 * i, 4 * GROUPS1)

                def outputs(n):
                    dve.wait_ge(outputs_free, stored_before[1] + GROUPS1 * i + (n if n > 0 else 1))
                    dve.wait_ge(f1_down, 4 * (GROUPS1 * i + n) + 4)
                    for j in range(4):
                        dve.tensor_tensor(out4[:, n % 2, j, :], banks[:, 5 + n % 2, j * D:(j + 1) * D],
                                          b2_all[:, bass.ds(experts[4 * n + j], 1), :].rearrange("p a d -> p (a d)"), ALU.add)\
                            .then_inc(f1_out, 1)

                for k in range(4 * GROUPS1):
                    dve.wait_ge(f1_up, 4 * GROUPS1 * i + k + 1)
                    dve.tensor_tensor(hid[:, k % 4, :, :], banks[:, 1 + k % 4, :].rearrange("p (c s) -> p c s", s=P),
                                      bcast(b1T_all[:, bass.ds(experts[k], 1), :].rearrange("p a c -> p (a c)").unsqueeze(2),
                                            (P, F // P, P)), ALU.add).then_inc(f1_hid, 1)
                    if k % 4 == 2 and k > 2:
                        outputs(k // 4 - 1)
                outputs(GROUPS1 - 1)

        def experts1_scalar(act):
            act.wait_ge(f1_weights, 64)
            for n in range(2):
                act.wait_ge(at_rows_stored[n], STORES * 3)
            act.wait_ge(route_slots, 2)
            with act.Fori(0, PASSES[1]) as i:
                experts = experts_of(act, 1, 4 * GROUPS1 * i, 4 * GROUPS1)

                def rows_turned(n):
                    act.wait_ge(f1_turned, GROUPS1 * i + n + 5)
                    act.activation(rowsT[:, n % 2, :, :].rearrange("p j s -> p (j s)"), banks[:, (0, 7)[n % 2], :], ACT.Copy)\
                        .then_inc(f1_rowsT, 1)

                def weights_to(k):
                    act.activation(w1_now[:, k % 4, :], w1_all[:, bass.ds(experts[k], 1), :].rearrange("p a f -> p (a f)"),
                                   ACT.Copy).then_inc(f1_w1, 1)

                weights_to(0)
                rows_turned(0)
                weights_to(1)
                weights_to(2)
                for k in range(4 * GROUPS1):
                    if k % 4 == 1 and k // 4 + 1 < GROUPS1:
                        rows_turned(k // 4 + 1)
                    if k + 3 < 4 * GROUPS1:
                        weights_to(k + 3)
                    act.wait_ge(f1_hid, 4 * GROUPS1 * i + k + 1)
                    act.activation(hidT[:, k % 4, :], hid[:, k % 4, :, :].rearrange("p c s -> p (c s)"), ACT.Relu).then_inc(f1_hidT, 1)
            act.wait_ge(rows_stored[1], 160)

        def experts1_gpsimd(pool):
            with pool.Fori(0, PASSES[1]) as i:
                for n in range(GROUPS1):
                    group = GROUPS1 * i + n
                    pool.wait_ge(f1_out, 4 * group + 4)
                    pool.dma_start(rows_out[1][bass.ds(group * 4 * P, 4 * P), :].rearrange("(j p) d -> p j d", p=P),
                                   out4[:, n % 2, :, :]).then_inc(rows_stored[1], 16)
                    pool.wait_ge(rows_stored[1], 16 * group + 16)
                    pool.sem_inc(outputs_free, 1)

        gr = Region(0, LATE)
        gru_in = gr("gru_in", [P, BATCH, SEQ])
        centred = gr("centred", [P, BATCH, SEQ])
        spread = gr("spread", [P, BATCH, SEQ])
        z_gate = gr("z_gate", [P, BATCH, SEQ])
        keep_gate = gr("keep_gate", [P, BATCH, SEQ])
        hid_sig = gr("hid_sig", [P, BATCH, SEQ])
        cand = gr("cand", [P, BATCH, SEQ])
        gru_w = gr("gru_w", [P, 2, P])
        gru_p = gr("gru_p", [P, 5])
        gru_vars = gr("gru_vars", [P, BATCH, BT])
        gru_rstds = gr("gru_rstds", [P, BATCH, BT])
        gru_all = Region(LATE)("gru_all", [P, 3, 2 * P + 4])
        inv_d = sb("inv_d", [P, P])

        gru_loaded = sem("gru_loaded")
        gru_set = sem("gru_set")
        gru_mean = sem("gru_mean")
        gru_centred = sem("gru_centred")
        gru_squared = sem("gru_squared")
        gru_var = sem("gru_var")
        gru_spread = sem("gru_spread")
        gru_var_eps = sem("gru_var_eps")
        gru_rstd = sem("gru_rstd")
        gru_normed = sem("gru_normed")
        gru_affine = sem("gru_affine")
        gru_gates = sem("gru_gates")
        gru_sig = sem("gru_sig")
        gru_cand = sem("gru_cand")
        gru_out = sem("gru_out")
        gru_turned = sem("gru_turned")
        gru_copied = sem("gru_copied")

        def gru_tensor(pe):
            pe.wait_ge(f2_out, 4 + 12)
            with pe.Fori(0, 3) as l:
                for b in range(BATCH):
                    pe.wait_ge(gru_out, BATCH * l + b + 1)
                    pe.matmul(banks[:, b, :], inv_d[:, :], gru_in[:, b, :], start=True, stop=True).then_inc(gru_mean, 1)
                for b in range(BATCH):
                    pe.wait_ge(gru_squared, BATCH * l + b + 1)
                    for t in range(BT):
                        ins = pe.matmul(banks[:, 4 + b, t:t + 1], spread[:, b, t * P:(t + 1) * P], inv_d[:, 0:1],
                                        start=True, stop=True)
                    ins.then_inc(gru_var, 1)
                for b in range(BATCH):
                    pe.wait_ge(gru_rstd, BATCH * l + b + 1)
                    for t in range(BT):
                        ins = pe.matmul(banks[:, 4 + b, t * P:(t + 1) * P], bcast(gru_rstds[:, b, t:t + 1], (P, P)), C["ident"],
                                        start=True, stop=True)
                    ins.then_inc(gru_spread, 1)
                pe.wait_ge(gru_set, l + 1)
                for b in range(BATCH):
                    pe.wait_ge(gru_affine, BATCH * l + b + 1)
                    pe.matmul(banks[:, b, :], gru_w[:, 0, :], centred[:, b, :], start=True, stop=True)
                    pe.matmul(banks[:, 4 + b, :], gru_w[:, 1, :], centred[:, b, :], start=True, stop=True).then_inc(gru_gates, 1)
            pe.wait_ge(gru_out, 4 * BATCH)
            for t in range(TILES):
                ins = pe.transpose(banks[:, t // 4, (t % 4) * P:(t % 4 + 1) * P], gru_in[:, t // BT, (t % BT) * P:(t % BT + 1) * P],
                                   C["ident"])
                if t % 4 == 3:
                    ins.then_inc(gru_turned, 1)

        def gru_input_vector(dve):
            dve.wait_ge(xnT_ready, 12)
            for b in range(BATCH):
                dve.tensor_copy(gru_in[:, b, :], xnT[:, b * SEQ:(b + 1) * SEQ]).then_inc(gru_out, 1)

        def gru_vector(dve, step):
            dve.wait_ge(gru_out, BATCH)
            with step.loop(2, 3 * BATCH) as l:
                gru_pass_vector(dve, step, l)
            gru_pass_vector(dve, step, 2)
            gate_silu_vector(dve, step, 2)

        def gru_pass_vector(dve, step, l):
            last = isinstance(l, int)
            for b in range(BATCH):
                dve.wait_ge(gru_mean, BATCH * l + b + 1)
                dve.tensor_tensor(centred[:, b, :], gru_in[:, b, :], banks[:, b, :], ALU.subtract).then_inc(gru_centred, 1)
            for b in range(BATCH):
                dve.wait_ge(gru_var, BATCH * l + b + 1)
                dve.tensor_scalar(gru_vars[:, b, :], banks[:, 4 + b, 0:BT], EPS, None, ALU.add).then_inc(gru_var_eps, 1)
            if last:
                gate_first_vector(dve, step, 2)
            for b in range(BATCH):
                dve.wait_ge(gru_spread, BATCH * l + b + 1)
                dve.tensor_tensor(centred[:, b, :], centred[:, b, :], banks[:, 4 + b, :], ALU.mult).then_inc(gru_normed, 1)
            if last:
                gate_second_vector(dve, step, 2)
            for b in range(BATCH):
                dve.wait_ge(gru_sig, BATCH * l + b + 1)
                step(dve.tensor_scalar(cand[:, b, :], banks[:, 4 + b, :], gru_p[:, 3:4], 0.0, ALU.add, ALU.max))
                dve.scalar_tensor_tensor(cand[:, b, :], hid_sig[:, b, :], 0.5, cand[:, b, :], ALU.min, ALU.add)\
                    .then_inc(gru_cand, 1)
            if last:
                gate_sum_vector(dve, 2)
            for b in range(BATCH):
                dve.wait_ge(gru_cand, BATCH * l + b + 1)
                step(dve.tensor_tensor(cand[:, b, :], cand[:, b, :], z_gate[:, b, :], ALU.mult))
                step(dve.tensor_tensor_scan(hid_sig[:, b, :], keep_gate[:, b, :], cand[:, b, :], 0.5, ALU.mult, ALU.add))
                dve.tensor_tensor(gru_in[:, b, :], gru_in[:, b, :], hid_sig[:, b, :], ALU.add).then_inc(gru_out, 1)

        def gru_s(dve, b):
            dve.wait_ge(gru_turned, b + 1)
            return banks[:, b, :].rearrange("p (t d) -> p t d", d=D), gru_copied, b + 1

        def gru_scalar(act):
            with act.Fori(0, 3) as l:
                for b in range(BATCH):
                    act.wait_ge(gru_centred, BATCH * l + b + 1)
                    act.activation(spread[:, b, :], centred[:, b, :], ACT.Square).then_inc(gru_squared, 1)
                act.wait_ge(gru_set, l + 1)
                for b in range(BATCH):
                    act.wait_ge(gru_normed, BATCH * l + b + 1)
                    act.activation(centred[:, b, :], centred[:, b, :], ACT.Identity, bias=gru_p[:, 1:2], scale=gru_p[:, 0:1])\
                        .then_inc(gru_affine, 1)
                act.wait_ge(rows_stored[2], 16 * 12)
                for b in range(BATCH):
                    act.wait_ge(gru_gates, BATCH * l + b + 1)
                    act.activation(z_gate[:, b, :], banks[:, b, :], ACT.Sigmoid, bias=gru_p[:, 2:3])
                    act.activation(keep_gate[:, b, :], banks[:, b, :], ACT.Sigmoid, bias=gru_p[:, 4:5], scale=-1.0)
                    act.activation(hid_sig[:, b, :], banks[:, 4 + b, :], ACT.Sigmoid, bias=gru_p[:, 3:4]).then_inc(gru_sig, 1)
            gate_scalar(act, 2)

        def gru_weights_gpsimd(pool, step, l):
            if l == 0:
                pool.wait_ge(gru_loaded, 16)
            step(pool.tensor_copy(gru_w.rearrange("p a e -> p (a e)"), gru_all[:, l, 0:2 * P]))
            step(pool.tensor_copy(gru_p[:, 0:4], gru_all[:, l, 2 * P:2 * P + 4]))
            pool.tensor_tensor(gru_p[:, 4:5], zeros[:, 0:1], gru_p[:, 2:3], ALU.subtract).then_inc(gru_set, 1)

        def gru_gpsimd(pool, step):
            fetches = fetch_rows(pool, 2, 12)
            for l in range(3):
                if l > 0:
                    pool.wait_ge(gru_cand, BATCH * l)
                    gru_weights_gpsimd(pool, step, l)
                for b in range(BATCH):
                    pool.wait_ge(gru_var_eps, BATCH * l + b + 1)
                    pool.tensor_tensor(gru_rstds[:, b, :], gru_vars[:, b, :], minus_half[:, 0:BT], ALU.pow)\
                        .then_inc(gru_rstd, 1)
                for _ in range((16, 16, 0)[l]):
                    next(fetches)

        E2, F2 = 16, 64
        f2w = Region(LATE + 3 * (2 * P + 4))
        wgu_all = f2w("wgu_all", [P, E2, 2 * F2])
        wd_all = f2w("wd_all", [P, E2, D])
        shared_w = f2w("shared_w", [P, 4, P])
        shared_d = f2w("shared_d", [P, 2, D])
        shared_sig = f2w("shared_sig", [P, TILES])
        f2 = Region(0, LATE)
        sh_sig = f2("sh_sig", [P, 2, SEQ])
        sh_h = f2("sh_h", [P, 2, SEQ])
        rows4b = f2("rows4b", [P, 4, 4, D])
        rowsTb = f2("rowsTb", [P, 4, 4, P])
        gu_sig = f2("gu_sig", [P, 4, 4, F2])
        hid2 = f2("hid2", [P, 4, 4, 2 * F2])
        hidT2 = f2("hidT2", [P, 4, 4, P])
        out4b = f2("out4b", [P, 4, 4, D])
        f2_weights = sem("f2_weights")
        sh_gate_sig = sem("sh_gate_sig")
        sh_up = sem("sh_up")
        sh_sigmoid = sem("sh_sigmoid")
        sh_hidden = sem("sh_hidden")
        sh_down = sem("sh_down")
        sh_added = sem("sh_added")
        f2_turned = sem("f2_turned")
        f2_rowsT = sem("f2_rowsT")
        f2_up = sem("f2_up")
        f2_sig = sem("f2_sig")
        f2_hid = sem("f2_hid")
        f2_hid_turned = sem("f2_hid_turned")
        f2_hidT = sem("f2_hidT")
        f2_down = sem("f2_down")
        f2_out = sem("f2_out")

        def shared_tensor(pe):
            pe.wait_ge(f2_weights, 16 * 5)
            with pe.Fori(0, BATCH) as b:
                for c in range(2):
                    for n in (c, 2 + c):
                        ins = pe.matmul(banks[:, n, :], shared_w[:, n, :], xnT[:, bass.ds(b * SEQ, SEQ)], start=True, stop=True)
                    ins.then_inc(sh_up, 1)
                pe.wait_ge(sh_hidden, 2 * b + 2)
                for t in range(BT):
                    for c in range(2):
                        ins = pe.matmul(banks[:, 4, t * D:(t + 1) * D], sh_h[:, c, t * P:(t + 1) * P], shared_d[:, c, :],
                                        start=(c == 0), stop=(c == 1))
                ins.then_inc(sh_down, 1)
            pe.wait_ge(sh_added, BATCH)

        def shared_scalar(act):
            act.activation(shared_sig, shared_logit[:, :], ACT.Sigmoid).then_inc(sh_gate_sig, 1)
            with act.Fori(0, BATCH) as b:
                for c in range(2):
                    act.wait_ge(sh_up, 2 * b + c + 1)
                    act.activation(sh_sig[:, c, :], banks[:, c, :], ACT.Sigmoid).then_inc(sh_sigmoid, 1)

        def shared_vector(dve, step):
            dve.wait_ge(sh_gate_sig, 1)
            with step.loop(BATCH, 2) as b:
                for c in range(2):
                    dve.wait_ge(sh_sigmoid, 2 * b + c + 1)
                    step(dve.tensor_tensor(sh_h[:, c, :], banks[:, c, :], sh_sig[:, c, :], ALU.mult))
                    dve.tensor_tensor(sh_h[:, c, :], banks[:, 2 + c, :], sh_h[:, c, :], ALU.mult).then_inc(sh_hidden, 1)
                dve.wait_ge(sh_down, b + 1)
                dve.tensor_tensor(g_out[:, bass.ds(b * BT, BT), :], banks[:, 4, :].rearrange("p (t d) -> p t d", d=D),
                                  bcast(shared_sig[:, bass.ds(b * BT, BT)].unsqueeze(2), (P, BT, D)), ALU.mult)\
                    .then_inc(sh_added, 1)

        def experts2_sync(sp):
            sp.wait_ge(rows_sent[2], 16 * TILES * 2)
            with sp.Fori(0, PASSES[2]) as i:
                for n in range(4):
                    row = sp.snap((4 * i + n) * 4 * P)
                    sp.wait_ge(f2_turned, 4 * i + n + 1)
                    sp.dma_start(rows4b[:, n, :, :], rows_in[2][bass.ds(row, 4 * P), :].rearrange("(j p) d -> p j d", p=P))\
                        .then_inc(loaded[n], 16)

        def experts2_tensor(pe):
            pe.sem_inc(f2_turned, 4)
            pe.sem_inc(f2_out, 4)
            pe.wait_ge(route_slots, 3)
            with pe.Fori(0, 3) as i:
                experts = experts_of(pe, 2, 16 * i, 16)
                for n in range(4):
                    pe.wait_ge(loaded[n], LOADED_BEFORE[2][n] + 16 * i + 16)
                    for j in range(4):
                        ins = pe.transpose(banks[:, 2 * n, j * P:(j + 1) * P], rows4b[:, n, j, :], C["ident"])
                    ins.then_inc(f2_turned, 1)
                for n in range(4):
                    pe.wait_ge(f2_rowsT, 4 * i + n + 1)
                    pe.wait_ge(f2_out, 4 * i + n + 1)
                    for j in range(4):
                        ins = pe.matmul(banks[:, 2 * n + 1, j * P:(j + 1) * P], rowsTb[:, n, j, :],
                                        wgu_all[:, bass.ds(experts[4 * n + j], 1), :].rearrange("p a f -> p (a f)"),
                                        start=True, stop=True)
                    ins.then_inc(f2_up, 1)
                for n in range(4):
                    pe.wait_ge(f2_hid, 4 * i + n + 1)
                    for j in range(4):
                        ins = pe.transpose(banks[:, 2 * n, j * P:(j + 1) * P], hid2[:, n, j, :], C["ident"])
                    ins.then_inc(f2_hid_turned, 1)
                for n in range(4):
                    pe.wait_ge(f2_hidT, 4 * i + n + 1)
                    for j in range(4):
                        ins = pe.matmul(banks[:, 2 * n + 1, j * P:(j + 1) * P], hidT2[:, n, j, :],
                                        wd_all[:, bass.ds(experts[4 * n + j], 1), :].rearrange("p a f -> p (a f)"),
                                        start=True, stop=True)
                    ins.then_inc(f2_down, 1)

        def experts2_scalar(act):
            with act.Fori(0, 3) as i:
                for n in range(4):
                    act.wait_ge(f2_turned, 4 * i + n + 5)
                    act.activation(rowsTb[:, n, :, :].rearrange("p j s -> p (j s)"), banks[:, 2 * n, :], ACT.Copy)\
                        .then_inc(f2_rowsT, 1)
                for n in range(4):
                    act.wait_ge(f2_up, 4 * i + n + 1)
                    gu = banks[:, 2 * n + 1, :].rearrange("p (j f) -> p j f", j=4)
                    act.activation(gu_sig[:, n, :, :], gu[:, :, 0:F2], ACT.Sigmoid).then_inc(f2_sig, 1)
                for n in range(4):
                    act.wait_ge(f2_hid_turned, 4 * i + n + 1)
                    act.activation(hidT2[:, n, :, :].rearrange("p j s -> p (j s)"), banks[:, 2 * n, :], ACT.Copy)\
                        .then_inc(f2_hidT, 1)

        def experts2_vector(dve, step):
            step(dve.memset(hid2, 0.0))
            with step.loop(3, 4) as i:
                for n in range(4):
                    gu = banks[:, 2 * n + 1, :].rearrange("p (j f) -> p j f", j=4)
                    dve.wait_ge(f2_sig, 4 * i + n + 1)
                    step(dve.tensor_tensor(hid2[:, n, :, 0:F2], gu[:, :, 0:F2], gu_sig[:, n, :, :], ALU.mult))
                    dve.tensor_tensor(hid2[:, n, :, 0:F2], gu[:, :, F2:2 * F2], hid2[:, n, :, 0:F2], ALU.mult).then_inc(f2_hid, 1)
                dve.wait_ge(outputs_free, stored_before[2] + i + 1)
                for n in range(4):
                    dve.wait_ge(f2_down, 4 * i + n + 1)
                    dve.tensor_copy(out4b[:, n, :, :], banks[:, 2 * n + 1, :].rearrange("p (j d) -> p j d", d=D)).then_inc(f2_out, 1)

        def experts2_gpsimd(pool):
            with pool.Fori(0, 3) as i:
                for n in range(4):
                    pool.wait_ge(f2_out, 4 * i + n + 5)
                    pool.dma_start(rows_out[2][bass.ds((4 * i + n) * 4 * P, 4 * P), :].rearrange("(j p) d -> p j d", p=P),
                                   out4b[:, n, :, :]).then_inc(rows_stored[2], 16)
                pool.wait_ge(rows_stored[2], 64 * i + 64)
                pool.sem_inc(outputs_free, 1)

        f3w = Region(LATE)
        up3T = f3w("up3T", [P, 8, F // P, D])
        down3 = f3w("down3", [P, 8, F // P, D])
        w3 = f3w("w3", [P, 8, D])
        chosen3 = f3w("chosen3", [P, 2, 8, D])
        f3_weights = sem("f3_weights")
        f3_product = sem("f3_product")
        f3_w3 = sem("f3_w3")
        f3_all = sem("f3_all")
        f3_masked = sem("f3_masked")

        f3_masked_act = sem("f3_masked_act")
        f3_reduced = sem("f3_reduced")
        f3_silu = sem("f3_silu")

        def experts3_weights_tensor(pe):
            pe.wait_ge(f3_weights, 32)
            for n in range(2):
                if n == 1:
                    pe.wait_ge(f3_w3, 1)
                for e in range(4 * n, 4 * n + 4):
                    for c in range(F // P):
                        ins = pe.matmul(banks[:, 6, (e % 4) * D:(e % 4 + 1) * D], up3T[:, e, c, :], down3[:, e, c, :],
                                        start=(c == 0), stop=(c == F // P - 1))
                ins.then_inc(f3_product, 1)
            pe.wait_ge(f3_w3, 2)

        def experts3_weights_scalar(act):
            for n in range(2):
                act.wait_ge(f3_product, n + 1)
                act.activation(w3[:, 4 * n:4 * n + 4, :].rearrange("p e d -> p (e d)"), banks[:, 6, :], ACT.Copy).then_inc(f3_w3, 1)

        def experts3_tensor(pe, tiles):
            if tiles[0] == 0:
                pe.wait_ge(at_max, NF * GROUPS * 2)
            for u in range(2 * tiles[0], 2 * tiles[-1] + 2):
                t, n = u // 2, u % 2
                if u >= 3:
                    pe.wait_ge((f3_masked, f3_masked_act)[(u - 3) % 2], (u - 3) // 2 + 1)
                pe.matmul(banks[:, u % 3, :], xnT[:, t * P:(t + 1) * P], w3[:, 4 * n:4 * n + 4, :], start=True, stop=True)\
                    .then_inc(f3_all, 1)

        def experts3_gate_scalar(act, b):
            act.wait_ge(f3_reduced, BT * b + BT)
            act.activation(xn[:, BT * b:BT * b + BT, :], g_out[:, BT * b:BT * b + BT, :], ACT.Sigmoid).then_inc(mix_sigmoid, 1)

        def experts3_gate_gpsimd(pool):
            for b in range(BATCH):
                tiles = slice(BT * b, BT * b + BT)
                pool.wait_ge(mix_sigmoid, 3 + b + 1)
                pool.tensor_tensor(g_out[:, tiles, :], g_out[:, tiles, :], xn[:, tiles, :], ALU.mult).then_inc(f3_silu, 1)

        def experts3_vector(dve, tiles):
            chosen = picks[:, 0:TILES * 8].rearrange("p (t e) -> p t e", e=8)
            if tiles[0] == 0:
                dve.wait_ge(route_picked, 4)

            def masked(t):
                if t >= 2:
                    dve.wait_ge(f3_reduced, t - 1)
                dve.wait_ge(f3_all, 2 * t + 1)
                dve.tensor_tensor(chosen3[:, t % 2, 0:4, :], banks[:, 2 * t % 3, :].rearrange("p (e d) -> p e d", d=D),
                                  bcast(chosen[:, t, 0:4].unsqueeze(2), (P, 4, D)), ALU.mult).then_inc(f3_masked, 1)

            masked(tiles[0])
            for t in tiles:
                if t + 1 in tiles:
                    masked(t + 1)
                dve.wait_ge(f3_masked, t + 1)
                dve.wait_ge(f3_masked_act, t + 1)
                dve.tensor_reduce(g_out[:, t, :], chosen3[:, t % 2, :, :].rearrange("p e d -> p d e"), X, ALU.add)\
                    .then_inc(f3_reduced, 1)

        def experts3_scalar(act, tiles):
            if tiles[0] == 0:
                act.wait_ge(route_picked, 4)
            for t in tiles:
                act.wait_ge(f3_all, 2 * t + 2)
                if t >= 2:
                    act.wait_ge(f3_reduced, t - 1)
                for e in range(4, 8):
                    ins = act.activation(chosen3[:, t % 2, e, :], banks[:, (2 * t + 1) % 3, (e - 4) * D:(e - 3) * D], ACT.Copy,
                                         scale=picks[:, 8 * t + e:8 * t + e + 1])
                ins.then_inc(f3_masked_act, 1)

        block = ctx.enter_context(nc.Block())

        @block.sync
        def _(sp):
            sp.dma_start(x[:, :, :], a["L0_attn_X"].rearrange("(t p) d -> p t d", p=P)).then_inc(x_loaded, 16)
            sp.dma_start(const[:, :], a["const"]).then_inc(const_loaded, 16)
            sp.dma_start(w0[:, :, :], a["w0"]).then_inc(l0_weights, 16)
            sp.dma_start(w0vg[:, :, :], a["w0vg"]).then_inc(l0_weights, 16)
            sp.dma_start(w0o[:, :], a["L0_attn_W_O"]).then_inc(l0_weights, 16)
            sp.dma_start(gn_w[:, :], a["L0_attn_gn_weight"].partition_broadcast(P)).then_inc(l0_weights, 16)
            sp.dma_start(gn_b[:, :], a["L0_attn_gn_bias"].partition_broadcast(P)).then_inc(l0_weights, 16)
            for layer in range(4):
                sp.dma_start(router[layer][:, :], a[f"router{layer}"]).then_inc(routers_loaded, 16)
            sp.dma_start(gate_b1[:, :], a["L1_ffn_gate_b"].partition_broadcast(P)).then_inc(routers_loaded, 16)
            sp.wait_ge(zeros_set, 1)
            for layer in range(3):
                rows = 8 * CAP if layer == 0 else rows_in[layer].shape[0]
                sp.dma_start(rows_in[layer][0:rows, :].rearrange("(n p r) d -> p n (r d)", p=P, r=4),
                             bcast(zeros[:, :].unsqueeze(1), (P, rows // 512, 512)))\
                    .then_inc(rows_zeroed if layer == 0 else scratch_filled, 16)
            sp.wait_ge(onesb_set, 1)
            for b in range(BATCH):
                sp.dma_start(q_rows[b, :, PER_CHANNEL - 1, :], zeros[:, 0:SEQ // 2].bitcast(BF16)).then_inc(scratch_filled, 16)
                sp.dma_start(k_rows[b, :, PER_CHANNEL - 1, :].rearrange("p (n c) -> p n c", c=P),
                             bcast(onesb[:, :].unsqueeze(1), (P, SEQ // P, P))).then_inc(scratch_filled, 16)
            experts1_weights(sp)
            experts0_sync(sp)
            sp.wait_ge(scratch_filled, SCRATCH_FILLED)
            project_sync(sp, 0)
            experts1_sync(sp)
            first_stacks_sync(sp, 0)
            sp.wait_ge(rows_stored[1], 160)
            sp.dma_start(gru_all, a["gru"]).then_inc(gru_loaded, 16)
            sp.dma_start(wgu_all, a["L2_gu"]).then_inc(f2_weights, 16)
            for n in range(2):
                sp.dma_start(wd_all[n * 64:(n + 1) * 64], a["L2_ffn_Wd"].rearrange("e f d -> f e d")).then_inc(f2_weights, 16)
            sp.dma_start(shared_w, a["L2_shared"]).then_inc(f2_weights, 16)
            sp.dma_start(shared_d, a["L2_ffn_Sd"].rearrange("(c p) d -> p c d", p=P)).then_inc(f2_weights, 16)
            attend_sync(sp, 0, all_steps(sp, 0))
            experts2_sync(sp)
            sp.wait_ge(rows_stored[2], 192)
            sp.wait_ge(gru_set, 3)
            sp.dma_start(up3T, a["L3_upT"].rearrange("e (c p) d -> p e c d", p=P)).then_inc(f3_weights, 16)
            sp.dma_start(down3, a["L3_ffn_w_down"].rearrange("e (c p) d -> p e c d", p=P)).then_inc(f3_weights, 16)
            project_sync(sp, 1)
            attend_sync(sp, 1, all_steps(sp, 1))
            for b in range(BATCH):
                sp.wait_ge(x_final, b + 1)
                sp.dma_start(out[b * SEQ:(b + 1) * SEQ, :].rearrange("(t p) d -> p t d", p=P), x[:, BT * b:BT * b + BT, :])\
                    .then_inc(out_stored, 16)
            sp.wait_ge(out_stored, 16 * BATCH)

        @block.gpsimd
        def _(pool):
            step = Steps(pool, pool_step)
            pool.memset(minus_half[:, :], -0.5).then_inc(pool_consts_set, 1)
            pool.memset(ones[:, :], 1.0).then_inc(pool_consts_set, 1)
            pool.memset(zeros[:, :], 0.0).then_inc(zeros_set, 1)
            pool.memset(onesb[:, :], 1.0).then_inc(onesb_set, 1)
            pool.memset(inv_d[:, :], 1.0 / D).then_inc(pool_consts_set, 1)
            pool.memset(v_half, 0.0).then_inc(pool_consts_set, 1)
            pool.wait_ge(pool_consts_set, 4)
            norm_gpsimd(pool, 0)
            pool.wait_ge(const_loaded, 16)
            send_rows(pool, 0)
            experts0_gpsimd(pool)
            retention_gpsimd(pool)
            norm_gpsimd(pool, 1)
            set_stacks(pool)
            send_rows(pool, 1)
            project_gpsimd(pool, 0)
            experts1_gpsimd(pool)
            for _ in fetch_rows(pool, 1, 10):
                pass
            attend_gpsimd(pool, 0)
            norm_gpsimd(pool, 2)
            send_rows(pool, 2)
            gru_weights_gpsimd(pool, step, 0)
            experts2_gpsimd(pool)
            gru_gpsimd(pool, step)
            norm_gpsimd(pool, 3)
            set_stacks(pool)
            project_gpsimd(pool, 1)
            attend_gpsimd(pool, 1)
            experts3_gate_gpsimd(pool)

        @block.scalar
        def _(act):
            norm_scalar(act, 0)
            routing_scalar(act, 0)
            retention_first_scalar(act)
            experts0_scalar(act)
            retention_rest_scalar(act)
            norm_scalar(act, 1)
            routing_scalar(act, 1)
            project_scalar(act, 0)
            experts1_scalar(act)
            attend_scalar(act, 0, all_steps(act, 0))
            project_out_scalar(act, 0)
            norm_scalar(act, 2)
            routing_scalar(act, 2)
            shared_scalar(act)
            experts2_scalar(act)
            gru_scalar(act)
            norm_scalar(act, 3)
            project_scalar(act, 1)
            experts3_weights_scalar(act)
            attend_scalar(act, 1, all_steps(act, 1))
            project_out_scalar(act, 1)

        @block.vector
        def _(dve):
            step = Steps(dve, dve_step)
            dve.wait_ge(x_loaded, 16)
            norm_vector(dve, step, 0)
            dve.wait_ge(const_loaded, 16)
            dve.wait_ge(pool_consts_set, 4)
            routing_vector(dve, step, 0)
            retention_first_vector(dve, step)
            step(dve.tensor_copy(identb[:, :], C["ident"]))
            step(dve.tensor_copy(negb[:, :, :], bcast(C["neg"].unsqueeze(1), (P, 4, P))))
            step(dve.tensor_copy(negTb[:, :, :], bcast(C["negT"].unsqueeze(1), (P, 2, P))))
            experts0_vector(dve)
            retention_rest_vector(dve, step)
            mix_vector(dve, step, 0, lambda b: retention_s(dve, b))
            routing_vector(dve, step, 1)
            project_vector(dve, step, 0)
            experts1_vector(dve)
            attend_vector(dve, step, 0, all_steps(dve, 0))
            mix_vector(dve, step, 1, lambda b: attention_s(dve, 0, b))
            routing_vector(dve, step, 2)
            shared_vector(dve, step)
            gru_input_vector(dve)
            experts2_vector(dve, step)
            gru_vector(dve, step)
            mix_vector(dve, step, 2, lambda b: gru_s(dve, b))
            project_vector(dve, step, 1)
            routing_vector(dve, step, 3, rest=False)
            attend_vector(dve, step, 1, all_steps(dve, 1))
            mix_vector(dve, step, 3, lambda b: attention_s(dve, 1, b))

        @block.tensor
        def _(pe):
            pe.wait_ge(const_loaded, 16)
            pe.wait_ge(pool_consts_set, 4)
            norm_tensor(pe, 0)
            routing_tensor(pe, 0)
            retention_first_tensor(pe)
            experts0_tensor(pe)
            retention_rest_tensor(pe)
            norm_tensor(pe, 1)
            routing_tensor(pe, 1)
            project_tensor(pe, 0)
            experts1_tensor(pe)
            attend_tensor(pe, 0, all_steps(pe, 0))
            project_out_tensor(pe, 0)
            norm_tensor(pe, 2)
            routing_tensor(pe, 2)
            shared_tensor(pe)
            experts2_tensor(pe)
            gru_tensor(pe)
            norm_tensor(pe, 3)
            project_tensor(pe, 1)
            experts3_weights_tensor(pe)
            pe.wait_ge(at_biased, 2 * BATCH + 2)
            for b in range(BATCH):
                routing_logits(pe, 3, b)
            pe.wait_ge(route_read, 2)
            attend_tensor(pe, 1, all_steps(pe, 1))
            project_out_tensor(pe, 1)


def laid_out(i):
    def blocks(w):
        full = np.zeros((D, D), w.dtype)
        for h in range(H0):
            full[h * D0:(h + 1) * D0, h * D0:(h + 1) * D0] = w[h]
        return full

    swap = np.arange(D) ^ 1
    q0, k0, v0 = (blocks(i[f"L0_attn_W_{n}"]) for n in "QKV")
    return {
        "const": constants(),
        "L0_attn_X": i["L0_attn_X"].reshape(T, D),
        "w0": np.stack([q0, q0[:, swap], k0, k0[:, swap]], axis=1),
        "w0vg": np.stack([v0, i["L0_attn_W_G"]], axis=1),
        "L0_attn_W_O": i["L0_attn_W_O"],
        "L0_attn_gn_weight": i["L0_attn_gn_weight"],
        "L0_attn_gn_bias": i["L0_attn_gn_bias"],
        "wqkv1": i["L1_attn_in_proj_weight"].reshape(3, D, D).transpose(2, 0, 1),
        "wout1": i["L1_attn_out_proj_weight"].T,
        "qk_bias1": np.zeros((D, 2), np.float32),
        "v_bias1": np.zeros(D, np.float32),
        "out_bias1": np.zeros(D, np.float32),
        "wqkv3": i["L3_attn_attn_W"].reshape(D, H1, 3, D1).transpose(0, 2, 1, 3).reshape(D, 3, D),
        "wout3": i["L3_attn_out_W"],
        "qk_bias3": i["L3_attn_attn_b"].reshape(H1, 3, D1).transpose(1, 0, 2).reshape(3, D)[:2].T,
        "v_bias3": i["L3_attn_attn_b"].reshape(H1, 3, D1).transpose(1, 0, 2).reshape(3, D)[2],
        "out_bias3": i["L3_attn_out_b"],
        "L1_ffn_W1": i["L1_ffn_W1"].reshape(8 * D, F),
        "L1_b1T": i["L1_ffn_b1"].reshape(8, F // P, P).transpose(2, 0, 1),
        "L1_ffn_W2": i["L1_ffn_W2"].reshape(8 * F, D),
        "L1_ffn_b2": i["L1_ffn_b2"].reshape(8 * D),
        "gru": np.concatenate([i["L2_attn_W"].transpose(1, 0, 2), i["L2_attn_ln_gamma"].T[:, :, None],
                               i["L2_attn_ln_beta"].T[:, :, None], i["L2_attn_b"].reshape(3, 2, D).transpose(2, 0, 1)], axis=2),
        "L2_gu": np.concatenate([i["L2_ffn_Wg"], i["L2_ffn_Wu"]], axis=2).transpose(1, 0, 2),
        "L2_ffn_Wd": i["L2_ffn_Wd"],
        "L2_shared": np.concatenate([i["L2_ffn_Sg"], i["L2_ffn_Su"]], axis=1).reshape(D, 4, P),
        "L2_ffn_Sd": i["L2_ffn_Sd"],
        "L3_upT": i["L3_ffn_w_up"].transpose(0, 2, 1),
        "L3_ffn_w_down": i["L3_ffn_w_down"],
        "router0": i["L0_ffn_Wr"],
        "router1": i["L1_ffn_gate_w"],
        "router2": np.concatenate([i["L2_ffn_router_w"].T, i["L2_ffn_shared_gate_w"]], axis=1),
        "router3": i["L3_ffn_gate_w"].T,
        "L1_ffn_gate_b": i["L1_ffn_gate_b"],
        "L0_ffn_W1": i["L0_ffn_W1"].reshape(8 * D, F),
        "L0_ffn_W2": i["L0_ffn_W2"].reshape(8 * F, D),
    }


def kernel(**inputs):
    import concourse.bacc as _bacc
    from concourse.bass_utils import run_bass_kernel_spmd as _run

    nc = _bacc.Bacc("TRN2", target_bir_lowering=False, num_devices=1)
    arrays, args = {}, {}
    for name, value in laid_out({k: np.asarray(v) for k, v in inputs.items()}).items():
        arrays[f"in_{name}"] = np.ascontiguousarray(value)
        args[name] = nc.dram_tensor(f"in_{name}", value.shape, mybir.dt.from_np(value.dtype), kind="ExternalInput").ap()
    out = nc.dram_tensor("out", (T, D), F32, kind="ExternalOutput").ap()
    scratch = {kind: [nc.dram_tensor(f"{kind}{n}", (rows, D), F32).ap()
                      for n, rows in enumerate((8 * CAP + dropped, 40 * P, 48 * P))]
               for kind, dropped in (("rows_in", T), ("rows_out", 0))}
    scratch["q_rows"] = nc.dram_tensor("q_rows", (BATCH, D, 7, SEQ), BF16).ap()
    scratch["k_rows"] = nc.dram_tensor("k_rows", (BATCH, D, 7, SEQ), BF16).ap()
    build(nc, args, out, scratch)
    r = _run(nc, [arrays], core_ids=[0])
    return r.results[0]["out"].reshape(BATCH, SEQ, D)
```
